# Optimizing a Trainium2 kernel written in Bass

```python
import numpy as np
import jax
import jax.numpy as jnp

def _softmax(x, axis=-1):
    return jax.nn.softmax(x, axis=axis)

def _gelu(x):
    return jax.nn.gelu(x, approximate=True)

def _silu(x):
    return jax.nn.silu(x)

def _sigmoid(x):
    return jax.nn.sigmoid(x)

def _layernorm(x, axis=-1, eps=1e-05):
    m = jnp.mean(x, axis=axis, keepdims=True)
    v = jnp.var(x, axis=axis, keepdims=True)
    return (x - m) / jnp.sqrt(v + eps)

def _scatter_add(tgt, idx, src, axis=0):
    return tgt.at[idx].add(src)

def _segment_sum(src, seg, n):
    return jax.ops.segment_sum(src, seg, n)
kernel_name = 'mk_perceiver_d2_seqx_r4_7bca7f'

def setup_inputs(seed: int=0):
    np.random.seed(seed)
    _w = jnp.asarray

    def _rec_inputs():
        import jax
        import jax.numpy as jnp
        _rk = jax.random.key(seed)
        x = -0.0002928 + 1 * jax.random.normal(jax.random.fold_in(_rk, 1), (1, 128, 256), jnp.float32)
        _lenS = 128 - jax.random.randint(jax.random.fold_in(_rk, 7), (1,), 0, max(1, 128 // 4) + 1, jnp.int32)
        _lenS2 = 12544 - jax.random.randint(jax.random.fold_in(_rk, 8), (1,), 0, max(1, 12544 // 4) + 1, jnp.int32)
        _ctx_1024P = jax.random.normal(jax.random.fold_in(_rk, 11), (1, 16, 256), jnp.float32)
        _ctx_1024c = jax.random.dirichlet(jax.random.fold_in(_rk, 511), 0.3 * jnp.ones((16,), jnp.float32), (1, 12544))
        _ctx_1024t = jnp.einsum('bsk,bkd->bsd', _ctx_1024c, _ctx_1024P)
        _ctx_1024t = _ctx_1024t * jax.lax.rsqrt(jnp.mean(jnp.square(_ctx_1024t)) + 1e-12) * 0.953939
        ctx_1024 = -1.39393e-06 + 0.999914 * (_ctx_1024t + 0.3 * jax.random.normal(jax.random.fold_in(_rk, 611), (1, 12544, 256), jnp.float32))
        return (x, ctx_1024)
    x, ctx_1024 = _rec_inputs()

    def _L0_xattn_setup():
        import jax, jax.numpy as jnp
        import numpy as np
        N_HEADS = 16
        D_IN = 256
        D_K = 64
        D_V_HEAD = 256 // N_HEADS
        key = jax.random.key(seed)
        k1, k2, k3, k4, k5 = jax.random.split(key, 5)
        B, LQ, LK = (2, 512, 512)
        s = 1.0 / np.sqrt(D_IN)
        return {'input_q': jax.random.normal(k1, (B, LQ, D_IN), dtype=jnp.float32), 'input_k': jax.random.normal(k2, (B, LK, D_IN), dtype=jnp.float32), 'wq': jax.random.uniform(k3, (D_IN, D_K * N_HEADS), jnp.float32, -s, s), 'wk': jax.random.uniform(k4, (D_IN, D_K * N_HEADS), jnp.float32, -s, s), 'wv': jax.random.uniform(k5, (D_IN, D_V_HEAD * N_HEADS), jnp.float32, -s, s)}
    _L0_xattn_all = _L0_xattn_setup()
    _L0_xattn_in = {k: v for k, v in _L0_xattn_all.items() if k in ('wq', 'wk', 'wv')}
    del _L0_xattn_all

    def _L0_attn_setup():
        import jax, jax.numpy as jnp
        import numpy as np
        EMBED = 256
        WIN = 128
        NUM_HEADS = 16
        HQ = 16
        HKV = 4
        HEAD_DIM = EMBED // NUM_HEADS
        G = HQ // HKV
        key = jax.random.key(seed)
        k = jax.random.split(key, 5)
        B, S = (1, 512)
        x = jax.random.normal(k[0], (B, S, EMBED), dtype=jnp.float32)
        Wq = jax.random.normal(k[1], (HQ * HEAD_DIM, EMBED), dtype=jnp.float32) * 0.02
        Wk = jax.random.normal(k[2], (HKV * HEAD_DIM, EMBED), dtype=jnp.float32) * 0.02
        Wv = jax.random.normal(k[3], (HKV * HEAD_DIM, EMBED), dtype=jnp.float32) * 0.02
        Wo = jax.random.normal(k[4], (EMBED, HQ * HEAD_DIM), dtype=jnp.float32) * 0.02
        return {'x': x, 'Wq': Wq, 'Wk': Wk, 'Wv': Wv, 'Wo': Wo}
    _L0_attn_all = _L0_attn_setup()
    _L0_attn_in = {k: v for k, v in _L0_attn_all.items() if k in ('Wq', 'Wk', 'Wv', 'Wo')}
    del _L0_attn_all

    def _L0_ffn_setup():
        import jax, jax.numpy as jnp
        import numpy as np
        D_IN, D_HID = (256, 1024)

        def _ternary(key, shape):
            return jax.random.randint(key, shape, -1, 2).astype(jnp.float32)

        def _tlin(x, w, s):
            return jnp.einsum('bsi,oi->bso', x, w) * s
        key = jax.random.key(seed)
        ks = jax.random.split(key, 12)
        inv = lambda fan: 1.0 / np.sqrt(fan).astype(np.float32)
        return {'x': jax.random.normal(ks[0], (4, 512, D_IN), dtype=jnp.float32), 'w1_w': _ternary(ks[1], (D_HID, D_IN)), 'w1_s': jax.random.uniform(ks[2], (D_HID,), dtype=jnp.float32) * inv(D_IN), 'w2_w': _ternary(ks[3], (D_HID, D_IN)), 'w2_s': jax.random.uniform(ks[4], (D_HID,), dtype=jnp.float32) * inv(D_IN), 'h1_w': _ternary(ks[5], (D_HID, D_HID)), 'h1_s': jax.random.uniform(ks[6], (D_HID,), dtype=jnp.float32) * inv(D_HID), 'h2_w': _ternary(ks[7], (D_HID, D_HID)), 'h2_s': jax.random.uniform(ks[8], (D_HID,), dtype=jnp.float32) * inv(D_HID), 'w3_w': _ternary(ks[9], (D_IN, D_HID)), 'w3_s': jax.random.uniform(ks[10], (D_IN,), dtype=jnp.float32) * inv(D_HID)}
    _L0_ffn_all = _L0_ffn_setup()
    _L0_ffn_in = {k: v for k, v in _L0_ffn_all.items() if k in ('w1_w', 'w1_s', 'w2_w', 'w2_s', 'h1_w', 'h1_s', 'h2_w', 'h2_s', 'w3_w', 'w3_s')}
    del _L0_ffn_all

    def _L1_xattn_setup():
        import jax, jax.numpy as jnp
        import numpy as np
        B, L_ENC, L_DEC, D = (16, 128, 128, 256)
        key = jax.random.key(seed)
        k1, k2, k3, k4, k5, k6 = jax.random.split(key, 6)
        encoder_hc = jax.random.normal(k1, (B, L_ENC, D), dtype=jnp.float32)
        decoder_hq = jax.random.normal(k2, (B, L_DEC, D), dtype=jnp.float32)
        w_sim = jax.random.normal(k3, (3 * D,), dtype=jnp.float32) * 0.02
        b_sim = jax.random.normal(k4, (1,), dtype=jnp.float32) * 0.02
        W_qv = jax.random.normal(k5, (4 * D, D), dtype=jnp.float32) * 0.02
        b_qv = jax.random.normal(k6, (D,), dtype=jnp.float32) * 0.02
        return {'encoder_hc': encoder_hc, 'decoder_hq': decoder_hq, 'w_sim': w_sim, 'b_sim': b_sim, 'W_qv': W_qv, 'b_qv': b_qv}
    _L1_xattn_all = _L1_xattn_setup()
    _L1_xattn_in = {k: v for k, v in _L1_xattn_all.items() if k in ('w_sim', 'b_sim', 'W_qv', 'b_qv')}
    del _L1_xattn_all

    def _L1_attn_setup():
        import jax, jax.numpy as jnp
        import numpy as np
        NUM_HEADS, D_HEAD, D_MODEL, N_CTX = (16, 64, 256, 512)
        BATCH, SEQ = (4, 512)
        key = jax.random.key(seed)
        kx, kq, kk, kv, ko = jax.random.split(key, 5)
        x = jax.random.normal(kx, (BATCH, SEQ, D_MODEL), dtype=jnp.float32)
        Q = jax.random.normal(kq, (NUM_HEADS, D_HEAD, D_MODEL), dtype=jnp.float32) / np.sqrt(D_MODEL)
        K = jax.random.normal(kk, (NUM_HEADS, D_HEAD, D_MODEL), dtype=jnp.float32) / np.sqrt(D_MODEL)
        V = jax.random.normal(kv, (NUM_HEADS, D_HEAD, D_MODEL), dtype=jnp.float32) / np.sqrt(D_MODEL)
        O = jax.random.normal(ko, (D_MODEL, NUM_HEADS * D_HEAD), dtype=jnp.float32) / np.sqrt(NUM_HEADS * D_HEAD)
        return {'x': x, 'Q': Q, 'K': K, 'V': V, 'O': O}
    _L1_attn_all = _L1_attn_setup()
    _L1_attn_in = {k: v for k, v in _L1_attn_all.items() if k in ('Q', 'K', 'V', 'O')}
    del _L1_attn_all

    def _L1_ffn_setup():
        import jax, jax.numpy as jnp
        import numpy as np
        N_EMBD = 256
        N_EXPERTS = 16
        TOP_K = 2
        N_SHARED = 1
        HIDDEN = 4 * N_EMBD

        def _ffn(xf, w1, b1, w2, b2):
            h = jnp.maximum(xf @ w1 + b1, 0.0)
            return h @ w2 + b2
        key = jax.random.key(seed)
        ks = jax.random.split(key, 12)
        s = 0.02
        x = jax.random.normal(ks[0], (4, 512, N_EMBD), dtype=jnp.float32)
        router_w = jax.random.normal(ks[1], (N_EMBD, N_EXPERTS), dtype=jnp.float32) * s
        expert_bias = jnp.zeros((N_EXPERTS,), dtype=jnp.float32)
        shared_w1 = jax.random.normal(ks[2], (N_SHARED, N_EMBD, HIDDEN), dtype=jnp.float32) * s
        shared_b1 = jnp.zeros((N_SHARED, HIDDEN), dtype=jnp.float32)
        shared_w2 = jax.random.normal(ks[3], (N_SHARED, HIDDEN, N_EMBD), dtype=jnp.float32) * s
        shared_b2 = jnp.zeros((N_SHARED, N_EMBD), dtype=jnp.float32)
        routed_w1 = jax.random.normal(ks[4], (N_EXPERTS, N_EMBD, HIDDEN), dtype=jnp.float32) * s
        routed_b1 = jnp.zeros((N_EXPERTS, HIDDEN), dtype=jnp.float32)
        routed_w2 = jax.random.normal(ks[5], (N_EXPERTS, HIDDEN, N_EMBD), dtype=jnp.float32) * s
        routed_b2 = jnp.zeros((N_EXPERTS, N_EMBD), dtype=jnp.float32)
        return {'x': x, 'router_w': router_w, 'expert_bias': expert_bias, 'shared_w1': shared_w1, 'shared_b1': shared_b1, 'shared_w2': shared_w2, 'shared_b2': shared_b2, 'routed_w1': routed_w1, 'routed_b1': routed_b1, 'routed_w2': routed_w2, 'routed_b2': routed_b2}
    _L1_ffn_all = _L1_ffn_setup()
    _L1_ffn_in = {k: v for k, v in _L1_ffn_all.items() if k in ('router_w', 'expert_bias', 'shared_w1', 'shared_b1', 'shared_w2', 'shared_b2', 'routed_w1', 'routed_b1', 'routed_w2', 'routed_b2')}
    del _L1_ffn_all
    return {'x': x, 'ctx_1024': ctx_1024, 'L0_xattn_wq': _L0_xattn_in['wq'], 'L0_xattn_wk': _L0_xattn_in['wk'], 'L0_xattn_wv': _L0_xattn_in['wv'], 'L0_attn_Wq': _L0_attn_in['Wq'], 'L0_attn_Wk': _L0_attn_in['Wk'], 'L0_attn_Wv': _L0_attn_in['Wv'], 'L0_attn_Wo': _L0_attn_in['Wo'], 'L0_ffn_w1_w': _L0_ffn_in['w1_w'], 'L0_ffn_w1_s': _L0_ffn_in['w1_s'], 'L0_ffn_w2_w': _L0_ffn_in['w2_w'], 'L0_ffn_w2_s': _L0_ffn_in['w2_s'], 'L0_ffn_h1_w': _L0_ffn_in['h1_w'], 'L0_ffn_h1_s': _L0_ffn_in['h1_s'], 'L0_ffn_h2_w': _L0_ffn_in['h2_w'], 'L0_ffn_h2_s': _L0_ffn_in['h2_s'], 'L0_ffn_w3_w': _L0_ffn_in['w3_w'], 'L0_ffn_w3_s': _L0_ffn_in['w3_s'], 'L1_xattn_w_sim': _L1_xattn_in['w_sim'], 'L1_xattn_b_sim': _L1_xattn_in['b_sim'], 'L1_xattn_W_qv': _L1_xattn_in['W_qv'], 'L1_xattn_b_qv': _L1_xattn_in['b_qv'], 'L1_attn_Q': _L1_attn_in['Q'], 'L1_attn_K': _L1_attn_in['K'], 'L1_attn_V': _L1_attn_in['V'], 'L1_attn_O': _L1_attn_in['O'], 'L1_ffn_router_w': _L1_ffn_in['router_w'], 'L1_ffn_expert_bias': _L1_ffn_in['expert_bias'], 'L1_ffn_shared_w1': _L1_ffn_in['shared_w1'], 'L1_ffn_shared_b1': _L1_ffn_in['shared_b1'], 'L1_ffn_shared_w2': _L1_ffn_in['shared_w2'], 'L1_ffn_shared_b2': _L1_ffn_in['shared_b2'], 'L1_ffn_routed_w1': _L1_ffn_in['routed_w1'], 'L1_ffn_routed_b1': _L1_ffn_in['routed_b1'], 'L1_ffn_routed_w2': _L1_ffn_in['routed_w2'], 'L1_ffn_routed_b2': _L1_ffn_in['routed_b2']}

def reference(x, ctx_1024, L0_xattn_wq, L0_xattn_wk, L0_xattn_wv, L0_attn_Wq, L0_attn_Wk, L0_attn_Wv, L0_attn_Wo, L0_ffn_w1_w, L0_ffn_w1_s, L0_ffn_w2_w, L0_ffn_w2_s, L0_ffn_h1_w, L0_ffn_h1_s, L0_ffn_h2_w, L0_ffn_h2_s, L0_ffn_w3_w, L0_ffn_w3_s, L1_xattn_w_sim, L1_xattn_b_sim, L1_xattn_W_qv, L1_xattn_b_qv, L1_attn_Q, L1_attn_K, L1_attn_V, L1_attn_O, L1_ffn_router_w, L1_ffn_expert_bias, L1_ffn_shared_w1, L1_ffn_shared_b1, L1_ffn_shared_w2, L1_ffn_shared_b2, L1_ffn_routed_w1, L1_ffn_routed_b1, L1_ffn_routed_w2, L1_ffn_routed_b2):
    import jax
    import jax.numpy as jnp

    def _L0_xattn_ref(input_q, input_k, wq, wk, wv):
        import jax, jax.numpy as jnp
        import numpy as np
        N_HEADS = 16
        D_IN = 256
        D_K = 64
        D_V_HEAD = 256 // N_HEADS
        B, LQ, _ = input_q.shape
        _, LK, _ = input_k.shape
        q = (input_q @ wq).reshape(B, LQ, N_HEADS, D_K).transpose(0, 2, 1, 3)
        k = (input_k @ wk).reshape(B, LK, N_HEADS, D_K).transpose(0, 2, 1, 3)
        v = (input_k @ wv).reshape(B, LK, N_HEADS, D_V_HEAD).transpose(0, 2, 1, 3)
        attn = jnp.einsum('bhqd,bhkd->bhqk', q, k) / jnp.sqrt(jnp.float32(D_K))
        attn = jax.nn.softmax(attn, axis=-1)
        out = jnp.einsum('bhqk,bhkd->bhqd', attn, v)
        return out.transpose(0, 2, 1, 3).reshape(B, LQ, D_V_HEAD * N_HEADS)

    def _L0_attn_ref(x, Wq, Wk, Wv, Wo):
        import jax, jax.numpy as jnp
        import numpy as np
        EMBED = 256
        WIN = 128
        NUM_HEADS = 16
        HQ = 16
        HKV = 4
        HEAD_DIM = EMBED // NUM_HEADS
        G = HQ // HKV
        B, S, _ = x.shape
        W = 2 * WIN + 1
        scale = 1.0 / np.sqrt(HEAD_DIM).astype(np.float32)
        Q = (x @ Wq.T).reshape(B, S, HKV, G, HEAD_DIM)
        K = (x @ Wk.T).reshape(B, S, HKV, HEAD_DIM)
        V = (x @ Wv.T).reshape(B, S, HKV, HEAD_DIM)
        offs = jnp.arange(W) - WIN
        idx = jnp.arange(S)[:, None] + offs[None, :]
        valid = (idx >= 0) & (idx < S)
        idxc = jnp.clip(idx, 0, S - 1)
        K_win = K[:, idxc]
        V_win = V[:, idxc]
        scores = jnp.einsum('bskgd,bswkd->bskgw', Q, K_win) * scale
        scores = jnp.where(valid[None, :, None, None, :], scores, jnp.float32(-jnp.inf))
        attn = jax.nn.softmax(scores, axis=-1)
        out = jnp.einsum('bskgw,bswkd->bskgd', attn, V_win)
        out = out.reshape(B, S, HQ * HEAD_DIM)
        return out @ Wo.T

    def _L0_ffn_ref(x, w1_w, w1_s, w2_w, w2_s, h1_w, h1_s, h2_w, h2_s, w3_w, w3_s):
        import jax, jax.numpy as jnp
        import numpy as np
        D_IN, D_HID = (256, 1024)

        def _ternary(key, shape):
            return jax.random.randint(key, shape, -1, 2).astype(jnp.float32)

        def _tlin(x, w, s):
            return jnp.einsum('bsi,oi->bso', x, w) * s
        h = jax.nn.silu(_tlin(x, w1_w, w1_s)) * _tlin(x, w2_w, w2_s)
        h = jax.nn.gelu(_tlin(h, h1_w, h1_s), approximate=False)
        h = jax.nn.gelu(_tlin(h, h2_w, h2_s), approximate=False)
        return _tlin(h, w3_w, w3_s)

    def _L1_xattn_ref(encoder_hc, decoder_hq, w_sim, b_sim, W_qv, b_qv):
        import jax, jax.numpy as jnp
        import numpy as np
        B, L_ENC, L_DEC, D = (16, 128, 128, 256)
        d = encoder_hc.shape[-1]
        w1, w2, w3 = (w_sim[:d], w_sim[d:2 * d], w_sim[2 * d:])
        Sim = (encoder_hc @ w1)[:, :, None] + (decoder_hq @ w2)[:, None, :] + jnp.einsum('bid,bjd->bij', encoder_hc * w3, decoder_hq) + b_sim[0]
        A = jax.nn.softmax(Sim, axis=2)
        hq_hat = jnp.einsum('bij,bjd->bid', A, decoder_hq)
        Batt = jax.nn.softmax(jnp.max(Sim, axis=2), axis=1)
        hc_bar = jnp.einsum('bi,bid->bd', Batt, encoder_hc)[:, None, :]
        hc_hat = jnp.broadcast_to(hc_bar, encoder_hc.shape)
        feats = jnp.concatenate([encoder_hc, hq_hat, encoder_hc * hq_hat, encoder_hc * hc_hat], axis=-1)
        hcq = feats @ W_qv + b_qv
        return hcq

    def _L1_attn_ref(x, Q, K, V, O):
        import jax, jax.numpy as jnp
        import numpy as np
        NUM_HEADS, D_HEAD, D_MODEL, N_CTX = (16, 64, 256, 512)
        BATCH, SEQ = (4, 512)
        q = jnp.einsum('nhm,btm->bnth', Q, x)
        k = jnp.einsum('nhm,btm->bnth', K, x)
        v = jnp.einsum('nhm,btm->bnth', V, x)
        scores = jnp.einsum('bnqh,bnkh->bnqk', q, k)
        s = x.shape[1]
        causal = jnp.tril(jnp.ones((s, s), dtype=bool))
        masked = jnp.where(causal, scores, jnp.float32(-10000000000.0))
        attn = jax.nn.softmax(masked, axis=-1)
        z = jnp.einsum('bnqk,bnkh->bnqh', attn, v)
        z = jnp.transpose(z, (0, 2, 1, 3)).reshape(x.shape[0], s, -1)
        return jnp.einsum('ma,bqa->bqm', O, z)

    def _L1_ffn_ref(x, router_w, expert_bias, shared_w1, shared_b1, shared_w2, shared_b2, routed_w1, routed_b1, routed_w2, routed_b2):
        import jax, jax.numpy as jnp
        import numpy as np
        N_EMBD = 256
        N_EXPERTS = 16
        TOP_K = 2
        N_SHARED = 1
        HIDDEN = 4 * N_EMBD

        def _ffn(xf, w1, b1, w2, b2):
            h = jnp.maximum(xf @ w1 + b1, 0.0)
            return h @ w2 + b2
        B, T, C = x.shape
        x_flat = x.reshape(-1, C)
        N = x_flat.shape[0]
        shared_out = jnp.zeros_like(x_flat)
        for s in range(N_SHARED):
            shared_out = shared_out + _ffn(x_flat, shared_w1[s], shared_b1[s], shared_w2[s], shared_b2[s])
        logits = x_flat @ router_w + expert_bias
        top_vals, top_idx = jax.lax.top_k(logits, TOP_K)
        weights = jax.nn.softmax(top_vals.astype(jnp.float32), axis=-1).astype(x.dtype)
        comb = jnp.zeros((N, N_EXPERTS), dtype=x.dtype)
        comb = comb.at[jnp.arange(N)[:, None], top_idx].add(weights)
        routed_out = jnp.zeros_like(x_flat)
        for e in range(N_EXPERTS):
            y_e = _ffn(x_flat, routed_w1[e], routed_b1[e], routed_w2[e], routed_b2[e])
            routed_out = routed_out + comb[:, e:e + 1] * y_e
        return (shared_out + routed_out).reshape(B, T, C)
    x = x + _L0_xattn_ref(_layernorm(x, axis=-1), ctx_1024, L0_xattn_wq, L0_xattn_wk, L0_xattn_wv)
    x = x + _L0_attn_ref(_layernorm(x, axis=-1), L0_attn_Wq, L0_attn_Wk, L0_attn_Wv, L0_attn_Wo)
    x = x + _L0_ffn_ref(_layernorm(x, axis=-1), L0_ffn_w1_w, L0_ffn_w1_s, L0_ffn_w2_w, L0_ffn_w2_s, L0_ffn_h1_w, L0_ffn_h1_s, L0_ffn_h2_w, L0_ffn_h2_s, L0_ffn_w3_w, L0_ffn_w3_s)
    x = x + _L1_xattn_ref(_layernorm(x, axis=-1), ctx_1024, L1_xattn_w_sim, L1_xattn_b_sim, L1_xattn_W_qv, L1_xattn_b_qv)
    x = x + _L1_attn_ref(_layernorm(x, axis=-1), L1_attn_Q, L1_attn_K, L1_attn_V, L1_attn_O)
    x = x + _L1_ffn_ref(_layernorm(x, axis=-1), L1_ffn_router_w, L1_ffn_expert_bias, L1_ffn_shared_w1, L1_ffn_shared_b1, L1_ffn_shared_w2, L1_ffn_shared_b2, L1_ffn_routed_w1, L1_ffn_routed_b1, L1_ffn_routed_w2, L1_ffn_routed_b2)
    return x

_drawn_inputs = setup_inputs


def setup_inputs(seed=0):
    import zlib

    import numpy as np

    out = dict(_drawn_inputs(seed))
    spreads = {'L1_ffn_expert_bias': (0.0, 0.1),
     'L1_ffn_shared_b1': (0.0, 0.1),
     'L1_ffn_shared_b2': (0.0, 0.1),
     'L1_ffn_routed_b1': (0.0, 0.1),
     'L1_ffn_routed_b2': (0.0, 0.1)}
    factors = {}
    for name, (base, spread) in spreads.items():
        noise = np.random.default_rng([zlib.crc32(name.encode()), seed]).standard_normal(out[name].shape)
        drawn = base * np.exp(spread * noise) if base else spread * noise
        out[name] = jnp.asarray(drawn.astype(out[name].dtype))
    for name, factor in factors.items():
        out[name] = (out[name] * factor).astype(out[name].dtype)
    return out
```

```python
from contextlib import ExitStack

import concourse.bass as bass
from concourse import mybir
import numpy as np

F32 = mybir.dt.float32
F32R = mybir.dt.float32r
ALU = mybir.AluOpType
ACT = mybir.ActivationFunctionType
AX = mybir.AxisListType

P = 128
D = 256
DK = D // P
EPS = 1e-5
BANK = 512

N_KEYS = 12544
TILES = N_KEYS // P
CHUNK_TILES = 4
CHUNK = CHUNK_TILES * P
TAIL_TILES = TILES % CHUNK_TILES
N_FULL = TILES // CHUNK_TILES

X0_HEADS = 16
X0_DK = 64
X0_DV = D // X0_HEADS
PAIRS = X0_HEADS // 2
QUADS = X0_HEADS // 4
PADV = 32

A0_HEADS, A0_KV, A0_DH = 16, 4, 16
HID = 1024
HB = HID // P
A1_HEADS, A1_DH = 16, 64
N_EXPERTS = 16
E_UNROLL = 4


class Done:

    def __init__(self, sem):
        self.sem, self.n = sem, 0

    def mark(self, inst):
        inst.then_inc(self.sem, 1)
        self.n += 1
        return (self.sem, self.n)


class Link:

    def __init__(self, sem, consumer, step=1):
        self.sem, self.consumer, self.step, self.n = sem, consumer, step, 0

    def sent_by(self, inst):
        inst.then_inc(self.sem, self.step)

    def wait(self):
        self.n += self.step
        self.consumer.wait_ge(self.sem, self.n)

    def settle(self):
        if self.n:
            self.consumer.sem_inc(self.sem, -self.n)
            self.n = 0


def build(nc, a, out):
    ctx = ExitStack()
    PE, AC, DV, GP, SP = nc.tensor, nc.scalar, nc.vector, nc.gpsimd, nc.sync

    def sb(name, shape, dt=F32, stack=ctx):
        return stack.enter_context(nc.sbuf_tensor(name, [P] + list(shape), dt))

    def sem(name):
        return ctx.enter_context(nc.semaphore(name))

    pe, ac, dv, gp = (Done(sem("s_" + n)) for n in ("pe", "act", "dve", "pool"))
    seen = {}

    def wait(eng, *points):
        for s, v in points:
            key = (id(eng), id(s))
            if seen.get(key, 0) < v:
                eng.wait_ge(s, v)
                seen[key] = v

    n_loads = [0]

    def load(dst, src, eng=SP):
        n_loads[0] += 1
        s = sem(f"s_load{n_loads[0]}")
        eng.dma_start(dst, src).then_inc(s, 16)
        return (s, 16)

    def settle(consumers):
        for eng, links in consumers.items():
            if any(l.n for l in links):
                if eng is not SP:
                    eng.drain()
                for l in links:
                    l.settle()

    ps = ctx.enter_context(nc.psum_tensor("ps", [P, 8, BANK], F32))

    ident = sb("ident", [P])
    mask4 = sb("mask4", [4])
    mask2 = sb("mask2", [2])
    ones = sb("ones", [P])
    minus_half = sb("minus_half", [1])
    pos = sb("pos", [N_EXPERTS])
    pos99 = sb("pos99", [N_EXPERTS])
    GP.memset(ident[:, :], 0.0)
    GP.memset(mask4[:, :], 1.0)
    GP.memset(minus_half[:, :], -0.5)
    GP.memset(mask2[:, :], 1.0)
    c0 = gp.mark(GP.memset(ones[:, :], 1.0))
    wait(GP, c0)
    GP.affine_select(out=ident[:, :], in_=ident[:, :], compare_op=ALU.not_equal, fill=1.0,
                     base=0, pattern=[[-1, P]], channel_multiplier=1)
    GP.affine_select(out=mask4[:, :], in_=mask4[:, :], compare_op=ALU.is_ge, fill=0.0,
                     base=0, pattern=[[-32, 4]], channel_multiplier=1)
    c1 = gp.mark(GP.affine_select(out=mask2[:, :], in_=mask2[:, :], compare_op=ALU.is_ge, fill=0.0,
                                  base=0, pattern=[[-64, 2]], channel_multiplier=1))
    wait(GP, c1)
    GP.affine_select(out=mask4[:, :], in_=mask4[:, :], compare_op=ALU.is_ge, fill=0.0,
                     base=31, pattern=[[32, 4]], channel_multiplier=-1)
    GP.affine_select(out=mask2[:, :], in_=mask2[:, :], compare_op=ALU.is_ge, fill=0.0,
                     base=63, pattern=[[64, 2]], channel_multiplier=-1)
    GP.iota(pos[:, :], pattern=[[1, N_EXPERTS]], base=0, channel_multiplier=0,
            allow_small_or_imprecise_dtypes=True)
    consts = gp.mark(GP.iota(pos99[:, :], pattern=[[1, N_EXPERTS]], base=99, channel_multiplier=0,
                             allow_small_or_imprecise_dtypes=True))
    for e in (PE, DV, AC):
        wait(e, consts)

    xbuf = [sb("x_even", [D]), sb("x_odd", [D])]
    xn = sb("xn", [D])
    xnT = sb("xnT", [DK, P])
    stat = sb("stat", [8])
    mv = sb("mv", [2])
    rstd = sb("rstd", [1])
    last = {"x": None, "xn_free": []}
    state = {"x": 0}

    readers = {b: [] for b in range(8)}
    turn = [0]

    def next_bank():
        b = turn[0] % 8
        turn[0] += 1
        wait(PE, *readers[b])
        readers[b] = []
        return b

    def next_banks(n):
        if turn[0] % 8 + n > 8:
            turn[0] += 8 - turn[0] % 8
        return [next_bank() for _ in range(n)][0]

    def read_by(b, point, n=1):
        for i in range(n):
            readers[b + i].append(point)

    flip = [0]

    def copy_out(dst, src, banks, after, mul=None, eng=None):
        flip[0] += 1
        use_act = flip[0] % 2 if eng is None else eng == "act"
        if use_act:
            wait(AC, *after)
            i = AC.copy(dst, src) if mul is None else AC.mul(dst, src, mul)
            p = ac.mark(i)
        else:
            wait(DV, *after)
            i = (DV.tensor_copy(dst, src) if mul is None
                 else DV.tensor_scalar(dst, src, mul, None, ALU.mult))
            p = dv.mark(i)
        for b in banks:
            read_by(b, p)
        return p

    def matmuls(dst, pairs):
        for i, (l, r) in enumerate(pairs):
            m = PE.matmul(dst, l, r, start=(i == 0), stop=(i == len(pairs) - 1))
        return pe.mark(m)

    def transposed(dst, blocks, after):
        points = []
        per = BANK // P
        rows = blocks[0].shape[0]
        for i in range(0, len(blocks), per):
            part = blocks[i:i + per]
            b = next_bank()
            wait(PE, *after)
            for j, blk in enumerate(part):
                t = PE.transpose(ps[:, b, j * P:j * P + rows], blk, ident[0:rows, 0:rows])
            t = pe.mark(t)
            points.append(copy_out(dst(i, len(part)),
                                   ps[:, b, 0:len(part) * P].rearrange("p (n c) -> p n c", c=P)[:, :, 0:rows],
                                   [b], [t]))
        return points

    def layer_norm():
        x = xbuf[state["x"]]
        wait(DV, last["x"])
        s0 = dv.mark(DV.bn_stats(stat[:, 0:6], x[:, :]))
        wait(DV, s0)
        s1 = dv.mark(DV.bn_aggr(mv[:, :], stat[:, 0:6]))
        wait(DV, s1)
        s2 = dv.mark(DV.tensor_scalar(mv[:, 1:2], mv[:, 1:2], EPS, None, ALU.add))
        wait(GP, s2)
        s2 = gp.mark(GP.tensor_tensor(rstd[:, :], mv[:, 1:2], minus_half[:, :], ALU.pow))
        wait(DV, s2, *last["xn_free"])
        s3 = dv.mark(DV.tensor_scalar(xn[:, :], x[:, :], mv[:, 0:1], rstd[:, 0:1], ALU.subtract, ALU.mult))
        tp = transposed(lambda i, n: xnT[:, :, :], [xn[:, k * P:(k + 1) * P] for k in range(DK)], [s3])
        last["xn_free"] = tp
        return s3, tp

    def add_to_x(branch, after, banks=()):
        x, y = xbuf[state["x"]], xbuf[1 - state["x"]]
        wait(DV, *after)
        last["x"] = dv.mark(DV.tensor_tensor(y[:, :], x[:, :], branch, ALU.add))
        for b in banks:
            read_by(b, last["x"])
        state["x"] = 1 - state["x"]

    def bc(ap, n):
        return ap.unsqueeze(ap.ndim).to_broadcast(list(ap.shape) + [n])

    def finish():
        wait(SP, last["x"])
        s = sem("s_out")
        SP.dma_start(out.rearrange("b s d -> (b s) d"), xbuf[state["x"]][:, :]).then_inc(s, 16)
        SP.wait_ge(s, 16)
        ctx.close()

    ld_x = load(xbuf[0][:, :], a["x"].rearrange("b s d -> (b s) d"))
    last["x"] = ld_x

    ctx_rows = a["ctx_1024"].rearrange("b s d -> (b s) d")
    st = ExitStack()
    with st:
        wq = sb("x0_wq", [DK, X0_HEADS * X0_DK], stack=st)
        ld_wq = load(wq[:, :, :], a["L0_xattn_wq"].rearrange("(k p) n -> p k n", p=P))
        ctx_nat = [sb(f"ctx_nat{i}", [CHUNK_TILES, D], stack=st) for i in range(2)]
        sem_ctx = [Link(sem(f"s_ctx{i}"), PE, 16) for i in range(2)]
        ctx_free = Link(sem("s_ctx_free"), SP)

        def load_ctx(slot, rows, nt):
            sem_ctx[slot].sent_by(SP.dma_start(ctx_nat[slot][:, 0:nt, :],
                                              rows.rearrange("(p t) d -> p t d", t=nt)))

        wk = sb("x0_wk", [DK, X0_HEADS * X0_DK], stack=st)
        ld_wk = load(wk[:, :, :], a["L0_xattn_wk"].rearrange("(k p) n -> p k n", p=P))
        wv = sb("x0_wv", [DK, D], stack=st)
        ld_wv = load(wv[:, :, :], a["L0_xattn_wv"].rearrange("(k p) n -> p k n", p=P))
        tail_rows = TAIL_TILES * P
        full_chunks = ctx_rows[tail_rows:N_KEYS, :].rearrange("(c p t) d -> c p t d", p=P, t=CHUNK_TILES)
        load_ctx(0, ctx_rows[0:tail_rows, :], TAIL_TILES)
        load_ctx(1, ctx_rows[tail_rows:tail_rows + CHUNK, :], CHUNK_TILES)

        wv_hi, wv_lo = sb("wv_hi", [DK, D], F32R, st), sb("wv_lo", [DK, D], F32R, st)
        wait(AC, ld_wv)
        t = ac.mark(AC.copy(wv_hi[:, :, :], wv[:, :, :]))
        wait(DV, t, ld_wv)
        wv_split = dv.mark(DV.tensor_tensor(wv_lo[:, :, :], wv[:, :, :], wv_hi[:, :, :], ALU.subtract))

        _, xnT_ok = layer_norm()
        qbd = sb("x0_qbd", [PAIRS, 2, P], stack=st)
        qbd_ok = []
        for p in range(PAIRS):
            b = next_bank()
            wait(PE, ld_wq, *xnT_ok)
            t = matmuls(ps[:, b, 0:P], [(wq[:, k, p * P:(p + 1) * P], xnT[:, k, :]) for k in range(DK)])
            wait(DV, t)
            for h in range(2):
                t = dv.mark(DV.tensor_scalar(qbd[:, p, h, :], ps[:, b, 0:P], mask2[:, h:h + 1],
                                             float(X0_DK) ** -0.5, ALU.mult, ALU.mult))
            read_by(b, t)
            qbd_ok.append(t)
        last["xn_free"] = last["xn_free"] + [t]
        wkT = sb("x0_wkT", [PAIRS, D], stack=st)
        wkT_ok = transposed(
            lambda i, n: wkT[:, i // DK:(i + n) // DK, :].rearrange("p a (k c) -> p (a k) c", c=P),
            [wk[:, k, p * P:(p + 1) * P] for p in range(PAIRS) for k in range(DK)], [ld_wk])
        qw_hi = sb("qw_hi", [DK, X0_HEADS, P], F32R, st)
        qw_lo = sb("qw_lo", [DK, X0_HEADS, P], F32R, st)
        for p in range(PAIRS):
            b = next_bank()
            wait(PE, wkT_ok[p * DK // 4], qbd_ok[p])
            for k in range(DK):
                t = matmuls(ps[:, b, k * 2 * P:(k + 1) * 2 * P],
                            [(wkT[:, p, k * P:(k + 1) * P], qbd[:, p, :, :])])
            src = ps[:, b, :].rearrange("p (k h c) -> p k h c", k=DK, h=2)
            wait(AC, t)
            t = ac.mark(AC.copy(qw_hi[:, :, 2 * p:2 * p + 2, :], src))
            wait(DV, t)
            t = dv.mark(DV.tensor_tensor(qw_lo[:, :, 2 * p:2 * p + 2, :], src,
                                         qw_hi[:, :, 2 * p:2 * p + 2, :], ALU.subtract))
            read_by(b, t)
        qw_ok = t

        ctxT_hi = [sb(f"ctxT_hi{i}", [DK, CHUNK], F32R, st) for i in range(2)]
        ctxT_lo = [sb(f"ctxT_lo{i}", [DK, CHUNK], F32R, st) for i in range(2)]
        vals = [sb(f"vals{i}", [CHUNK_TILES, X0_HEADS, PADV], stack=st) for i in range(2)]
        probs = [sb(f"probs{i}", [2, CHUNK], stack=st) for i in range(2)]
        probsT = [sb(f"probsT{i}", [4, CHUNK], stack=st) for i in range(2)]
        outT = sb("outT", [QUADS, P], stack=st)
        negm = [sb(f"negm{i}", [X0_HEADS], stack=st) for i in range(2)]
        negc = sb("negc", [X0_HEADS], stack=st)
        dm = sb("dm", [X0_HEADS], stack=st)
        alpha = sb("alpha", [X0_HEADS], stack=st)
        VW = X0_DV + 1
        acc = sb("acc", [X0_HEADS, VW], stack=st)
        GP.memset(negm[1][:, :], 3e38)
        GP.memset(acc[:, :, :], 0.0)
        GP.memset(vals[0][:, :, :, X0_DV:PADV], 1.0)
        init = gp.mark(GP.memset(vals[1][:, :, :, X0_DV:PADV], 1.0))

        to_max = Link(sem("l_to_max"), DV)
        to_exp = Link(sem("l_to_exp"), AC)
        to_turn = Link(sem("l_to_turn"), PE)
        turned0 = Link(sem("l_turned0"), AC)
        turned1 = Link(sem("l_turned1"), DV)
        kept0 = Link(sem("l_kept0"), PE)
        kept1 = Link(sem("l_kept1"), PE)
        g_to_act = Link(sem("l_g_to_act"), AC)
        g_to_dve = Link(sem("l_g_to_dve"), DV)
        hi_kept = Link(sem("l_hi_kept"), DV)
        g_from_act = Link(sem("l_g_from_act"), PE)
        g_from_dve = Link(sem("l_g_from_dve"), PE)
        out_full = Link(sem("l_out_full"), AC)
        out_kept = Link(sem("l_out_kept"), PE)
        alpha_ok = Link(sem("l_alpha_ok"), DV)
        self_dv = Link(sem("l_self_dv"), DV)

        S = lambda i: ps[:, 2 * i:2 * i + 2, :]
        T0, T1, G, O = (ps[:, b, :] for b in (4, 5, 6, 7))
        consumers = {
            PE: [to_turn, kept0, kept1, g_from_act, g_from_dve, out_kept] + sem_ctx,
            AC: [to_exp, turned0, g_to_act, out_full],
            DV: [to_max, turned1, g_to_dve, hi_kept, alpha_ok, self_dv],
            SP: [ctx_free],
        }

        g_by = ["none"]

        def g_free():
            if g_by[0] == "act":
                g_from_act.wait()
            elif g_by[0] == "dve":
                g_from_dve.wait()

        def x_piece(slot, k, nt):
            g_free()
            if k == 0:
                sem_ctx[slot].wait()
            for t in range(nt):
                m = PE.transpose(G[:, t * P:(t + 1) * P], ctx_nat[slot][:, t, k * P:(k + 1) * P], ident[:, :])
            g_to_act.sent_by(m)
            g_to_act.wait()
            hi_kept.sent_by(AC.copy(ctxT_hi[slot][:, k, 0:nt * P], G[:, 0:nt * P]))
            hi_kept.wait()
            g_from_dve.sent_by(DV.tensor_tensor(ctxT_lo[slot][:, k, 0:nt * P], G[:, 0:nt * P],
                                               ctxT_hi[slot][:, k, 0:nt * P], ALU.subtract))
            g_by[0] = "dve"

        def v_piece(slot, half):
            g_free()
            for i in range(2):
                cols = slice((2 * half + i) * P, (2 * half + i + 1) * P)
                terms = [(l[slot][:, k, cols], r[:, k, :]) for k in range(DK)
                         for l, r in ((ctxT_hi, wv_hi), (ctxT_hi, wv_lo), (ctxT_lo, wv_hi))]
                for n, (l, r) in enumerate(terms):
                    m = PE.matmul(G[:, i * D:(i + 1) * D], l, r, start=(n == 0), stop=(n == len(terms) - 1))
                    if half == 0 and i == 0 and n == 0:
                        ctx_free.sent_by(m)
            g_to_act.sent_by(m)
            g_to_act.wait()
            g_from_act.sent_by(AC.copy(vals[slot][:, 2 * half:2 * half + 2, :, 0:X0_DV],
                                      G.rearrange("p (t h c) -> p t h c", t=2, h=X0_HEADS)))
            g_by[0] = "act"

        def scores(slot, p, nt):
            for j in range(2):
                h = 2 * p + j
                terms = [(q[:, k, h, :], c[slot][:, k, 0:nt * P]) for k in range(DK)
                         for q, c in ((qw_hi, ctxT_hi), (qw_hi, ctxT_lo), (qw_lo, ctxT_hi))]
                for n, (l, r) in enumerate(terms):
                    m = PE.matmul(S(p % 2)[:, j, 0:nt * P], l, r, start=(n == 0), stop=(n == len(terms) - 1))
            to_max.sent_by(m)
            to_max.wait()
            self_dv.sent_by(DV.tensor_reduce(negc[:, 2 * p:2 * p + 2], S(p % 2)[:, :, 0:nt * P], AX.X, ALU.max))
            self_dv.wait()
            new = DV.scalar_tensor_tensor(
                out=negm[slot][:, 2 * p:2 * p + 2], in0=negc[:, 2 * p:2 * p + 2], scalar=-1.0,
                in1=negm[1 - slot][:, 2 * p:2 * p + 2], op0=ALU.mult, op1=ALU.min)
            if p == PAIRS - 1:
                self_dv.sent_by(new)
                self_dv.wait()
                new = DV.tensor_tensor(dm[:, :], negm[slot][:, :], negm[1 - slot][:, :], ALU.subtract)
            to_exp.sent_by(new)

        def exps(slot, p, nt):
            to_exp.wait()
            for j in range(2):
                i = AC.activation(probs[p % 2][:, j, 0:nt * P], S(p % 2)[:, j, 0:nt * P], ACT.Exp,
                                  bias=negm[slot][:, 2 * p + j:2 * p + j + 1], scale=1.0)
            to_turn.sent_by(i)
            if p == PAIRS - 1:
                alpha_ok.sent_by(AC.activation(alpha[:, :], dm[:, :], ACT.Exp))

        def turn_probs(p, nt):
            to_turn.wait()
            for j, (bank, link) in enumerate(((T0, turned0), (T1, turned1))):
                for t in range(nt):
                    m = PE.transpose(bank[:, t * P:(t + 1) * P], probs[p % 2][:, j, t * P:(t + 1) * P],
                                     ident[:, :])
                link.sent_by(m)
            dst = probsT[p // 2 % 2]
            turned0.wait()
            kept0.sent_by(AC.copy(dst[:, 2 * (p % 2), 0:nt * P], T0[:, 0:nt * P]))
            turned1.wait()
            kept1.sent_by(DV.tensor_copy(dst[:, 2 * (p % 2) + 1, 0:nt * P], T1[:, 0:nt * P]))

        def weighted(slot, q, nt):
            for t in range(nt):
                for j in range(4):
                    m = PE.matmul(O[PADV * j:PADV * (j + 1), q * P:(q + 1) * P], vals[slot][:, t, 4 * q + j, :],
                                  probsT[q % 2][:, j, t * P:(t + 1) * P], start=(t == 0), stop=(t == nt - 1),
                                  skip_group_check=True)
            if q == QUADS - 1:
                out_full.sent_by(m)
                out_full.wait()
                out_kept.sent_by(AC.copy(outT[:, :, :], O.rearrange("p (q c) -> p q c", c=P)))

        def out_piece():
            g_free()
            out_kept.wait()
            for q in range(QUADS):
                m = PE.transpose(G[:, q * P:(q + 1) * P], outT[:, q, :], ident[:, :])
            g_to_dve.sent_by(m)
            alpha_ok.wait()
            self_dv.sent_by(DV.tensor_tensor(acc[:, :, :], acc[:, :, :], bc(alpha[:, :], VW), ALU.mult))
            g_to_dve.wait()
            self_dv.wait()
            g_from_dve.sent_by(DV.tensor_tensor(
                acc[:, :, :], acc[:, :, :], G.rearrange("p (h c) -> p h c", c=PADV)[:, :, 0:VW], ALU.add))
            g_by[0] = "dve"

        def chunk(slot, nt, prev_nt, ahead):
            for p in range(PAIRS):
                if ahead and p in (0, 2):
                    x_piece(1 - slot, p // 2, CHUNK_TILES)
                if ahead and p in (3, 4):
                    v_piece(1 - slot, p - 3)
                if p == 1 and prev_nt:
                    out_piece()
                if p < PAIRS - 1:
                    scores(slot, p + 1, nt)
                elif ahead:
                    scores(1 - slot, 0, CHUNK_TILES)
                if prev_nt or p:
                    kept0.wait()
                    kept1.wait()
                if p == 0 and prev_nt:
                    weighted(1 - slot, QUADS - 1, prev_nt)
                if p in (2, 4, 6):
                    weighted(slot, p // 2 - 1, nt)
                turn_probs(p, nt)
                if p < PAIRS - 1:
                    exps(slot, p + 1, nt)
                elif ahead:
                    exps(1 - slot, 0, CHUNK_TILES)

        def load_full(slot, c):
            ctx_free.wait()
            sem_ctx[slot].sent_by(SP.dma_start(ctx_nat[slot][:, :, :], full_chunks[c]))

        wait(PE, qw_ok, wv_split, init, *[r for b in range(8) for r in readers[b]])
        wait(DV, init)
        wait(AC, init)
        x_piece(0, 0, TAIL_TILES)
        x_piece(0, 1, TAIL_TILES)
        v_piece(0, 0)
        scores(0, 0, TAIL_TILES)
        exps(0, 0, TAIL_TILES)
        load_full(0, 1)
        chunk(0, TAIL_TILES, 0, True)
        load_full(1, 2)
        chunk(1, CHUNK_TILES, TAIL_TILES, True)
        load_full(0, 3)
        settle(consumers)
        with nc.Fori(0, (N_FULL - 4) // 2) as i:
            chunk(0, CHUNK_TILES, CHUNK_TILES, True)
            load_full(1, 4 + i * 2)
            chunk(1, CHUNK_TILES, CHUNK_TILES, True)
            load_full(0, 5 + i * 2)
            settle(consumers)
        chunk(0, CHUNK_TILES, CHUNK_TILES, True)
        chunk(1, CHUNK_TILES, CHUNK_TILES, True)
        chunk(0, CHUNK_TILES, CHUNK_TILES, False)
        kept0.wait()
        kept1.wait()
        weighted(0, QUADS - 1, CHUNK_TILES)
        out_piece()
        g_from_dve.wait()
        DV.wait_ge(g_from_dve.sem, g_from_dve.n)
        den = sb("x0_den", [X0_HEADS], stack=st)
        y = sb("x0_y", [X0_HEADS, X0_DV], stack=st)
        t = dv.mark(DV.reciprocal(den[:, :], acc[:, :, X0_DV]))
        wait(DV, t)
        t = dv.mark(DV.tensor_tensor(y[:, :, :], acc[:, :, 0:X0_DV], bc(den[:, :], X0_DV), ALU.mult))
        add_to_x(y[:, :, :].rearrange("p h c -> p (h c)"), [t])
        for b in range(8):
            readers[b] = [last["x"]]

    def join():
        for e in (PE, AC, DV, GP, SP):
            wait(e, *[(d.sem, d.n) for d in (pe, ac, dv, gp) if d.n])

    def softmax_heads(st, s_banks, n_heads, masked, after):
        banks = list(range(s_banks, s_banks + n_heads * P // BANK))
        per = BANK // P
        name = "sm1" if masked else "sm0"
        e = sb(name + "_e", [n_heads, P], stack=st)
        mx, sm = sb(name + "_max", [n_heads], stack=st), sb(name + "_sum", [n_heads], stack=st)
        for n, b in enumerate(banks):
            hs = slice(n * per, (n + 1) * per)
            src = ps[:, b, :].rearrange("p (h c) -> p h c", c=P)
            wait(DV, after[n])
            if masked:
                t = copy_out(e[:, hs, :], src, [b], [after[n]], eng="act")
                wait(GP, t)
                t = gp.mark(GP.affine_select(out=e[:, hs, :], in_=e[:, hs, :], compare_op=ALU.is_ge,
                                             fill=-1e10, base=0, pattern=[[0, per], [-1, P]],
                                             channel_multiplier=1))
                wait(DV, t)
                src = e[:, hs, :]
            t = dv.mark(DV.tensor_reduce(mx[:, hs], src, AX.X, ALU.max))
            wait(DV, t)
            t = dv.mark(DV.tensor_tensor(e[:, hs, :], src, bc(mx[:, hs], P), ALU.subtract))
            read_by(b, t)
            wait(AC, t)
            t = ac.mark(AC.activation(e[:, hs, :], e[:, hs, :], ACT.Exp))
            wait(DV, t)
            t = dv.mark(DV.tensor_reduce(sm[:, hs], e[:, hs, :], AX.X, ALU.add))
            wait(DV, t)
            t = dv.mark(DV.reciprocal(sm[:, hs], sm[:, hs]))
            wait(DV, t)
            t = dv.mark(DV.tensor_tensor(e[:, hs, :], e[:, hs, :], bc(sm[:, hs], P), ALU.mult))
            yield e, t

    join()
    st = ExitStack()
    with st:
        G4 = A0_HEADS // A0_KV
        wq = sb("a0_wq", [DK, D], stack=st)
        wk_ = sb("a0_wk", [D], stack=st)
        wv_ = sb("a0_wv", [D], stack=st)
        wo = sb("a0_wo", [DK, A0_HEADS, 32], stack=st)
        z = sb("a0_wo_raw", [DK, D], stack=st)
        KV = A0_KV * A0_DH
        ld = [load(wq[:, :, :], a["L0_attn_Wq"].rearrange("(k p) n -> p k n", p=P)),
              load(wk_[0:KV, :], a["L0_attn_Wk"]),
              load(wv_[0:KV, :], a["L0_attn_Wv"]),
              load(z[:, :, :], a["L0_attn_Wo"].rearrange("(k p) n -> p k n", p=P))]
        wqT = sb("a0_wqT", [DK, A0_HEADS, 32], stack=st)
        wkT = sb("a0_wkT", [DK, A0_KV, G4, 32], stack=st)
        wvT = sb("a0_wvT", [DK, KV], stack=st)
        woT = sb("a0_woT", [A0_KV, D], stack=st)
        vp = sb("a0_v", [A0_KV, 32], stack=st)
        for buf in (wo, wqT, wkT, vp):
            flat = buf[(slice(None),) * (len(buf.shape))]
            zero = gp.mark(GP.memset(flat, 0.0))
        wait(PE, *ld)
        b = next_bank()
        for k in range(DK):
            for o in range(DK):
                t = PE.transpose(ps[:, b, (k * DK + o) * P:(k * DK + o + 1) * P],
                                 wq[:, o, k * P:(k + 1) * P], ident[:, :])
        t = pe.mark(t)
        wqT_ok = copy_out(wqT[:, :, :, 0:A0_DH], ps[:, b, :].rearrange("p (k h c) -> p k h c", k=DK, c=A0_DH),
                          [b], [t, zero])
        b = next_bank()
        for n, w in enumerate((wk_, wv_)):
            for k in range(DK):
                c = (n * DK + k) * KV
                t = PE.transpose(ps[:, b, c:c + KV], w[0:KV, k * P:(k + 1) * P], ident[0:KV, 0:KV])
        t = pe.mark(t)
        src = ps[:, b, 0:DK * KV].rearrange("p (k g c) -> p k g c", k=DK, c=A0_DH)
        for j in range(G4):
            wkT_ok = copy_out(wkT[:, :, :, j, 0:A0_DH], src, [b], [t, zero], eng="dve")
        wvT_ok = copy_out(wvT[:, :, :], ps[:, b, DK * KV:2 * DK * KV].rearrange("p (k c) -> p k c", k=DK),
                          [b], [t], eng="dve")
        wait(DV, ld[3], zero)
        t = dv.mark(DV.tensor_copy(wo[:, :, :, 0:A0_DH], z[:, :, :].rearrange("p k (h c) -> p k h c", c=A0_DH)))
        wo_flat = wo[:, :, :, :].rearrange("p k h c -> p k (h c)")
        woT_ok = transposed(
            lambda i, n: woT[:, i // DK:(i + n) // DK, :].rearrange("p g (k c) -> p (g k) c", c=P),
            [wo_flat[:, k, g * P:(g + 1) * P] for g in range(A0_KV) for k in range(DK)], [t])

        _, xnT_ok = layer_norm()
        wait(PE, *xnT_ok, wqT_ok, wkT_ok, wvT_ok, *woT_ok)
        qT = sb("a0_qT", [A0_KV, P], stack=st)
        kbd = sb("a0_kbd", [A0_KV, G4, P], stack=st)
        wqT_f = wqT[:, :, :, :].rearrange("p k h c -> p k (h c)")
        wkT_f = wkT[:, :, :, :, :].rearrange("p k g j c -> p k (g j c)")
        bq, bk = next_bank(), next_bank()
        for g in range(A0_KV):
            cols = slice(g * P, (g + 1) * P)
            tq = matmuls(ps[:, bq, cols], [(wqT_f[:, k, cols], xnT[:, k, :]) for k in range(DK)])
            tk = matmuls(ps[:, bk, cols], [(wkT_f[:, k, cols], xnT[:, k, :]) for k in range(DK)])
        bv = next_bank()
        tv = matmuls(ps[:, bv, 0:KV], [(xnT[:, k, :], wvT[:, k, :]) for k in range(DK)])
        q_ok = copy_out(qT[:, :, :], ps[:, bq, :].rearrange("p (g c) -> p g c", c=P), [bq], [tq],
                        mul=float(A0_DH) ** -0.5, eng="act")
        wait(DV, tk)
        for g in range(A0_KV):
            t = dv.mark(DV.tensor_tensor(
                kbd[:, g, :, :], ps[:, bk, g * P:(g + 1) * P].unsqueeze(1).to_broadcast([P, G4, P]),
                bc(mask4[:, :], P), ALU.mult))
        read_by(bk, t)
        kbd_ok = t
        v_ok = copy_out(vp[:, :, 0:A0_DH], ps[:, bv, 0:KV].rearrange("p (g c) -> p g c", c=A0_DH), [bv],
                        [tv, zero], eng="act")
        s0 = next_banks(A0_KV)
        wait(PE, q_ok, kbd_ok, v_ok)
        after = [matmuls(ps[:, s0 + g, :], [(qT[:, g, :], kbd[:, g, :, :])]) for g in range(A0_KV)]
        pT = sb("a0_pT", [A0_HEADS, P], stack=st)
        pT_ok = []
        for g, (e, t) in enumerate(softmax_heads(st, s0, A0_HEADS, False, after)):
            pT_ok += transposed(lambda i, n: pT[:, g * G4:(g + 1) * G4, :],
                                [e[:, g * G4 + j, :] for j in range(G4)], [t])
        b = next_bank()
        for g in range(A0_KV):
            wait(PE, pT_ok[g])
            for j in range(G4):
                t = PE.matmul(ps[32 * j:32 * (j + 1), b, g * P:(g + 1) * P], vp[:, g, :],
                              pT[:, g * G4 + j, :], start=True, stop=True, skip_group_check=True)
        t = pe.mark(t)
        oT = sb("a0_oT", [A0_KV, P], stack=st)
        t = copy_out(oT[:, :, :], ps[:, b, :].rearrange("p (g c) -> p g c", c=P), [b], [t])
        b = next_bank()
        wait(PE, t)
        t = matmuls(ps[:, b, 0:D], [(oT[:, g, :], woT[:, g, :]) for g in range(A0_KV)])
        add_to_x(ps[:, b, 0:D], [t], [b])

    join()
    st = ExitStack()
    with st:
        rows = sb("f_rows", [P], stack=st)
        names = ["L0_ffn_w1_s", "L0_ffn_w2_s", "L0_ffn_h1_s", "L0_ffn_h2_s"]
        ld_s = [load(rows[n * HB:(n + 1) * HB, :], a[s].rearrange("(b c) -> b c", c=P))
                for n, s in enumerate(names)]
        scale = sb("f_scale", [len(names) * HB], stack=st)
        s3 = sb("f_w3_s", [D], stack=st)
        ld_s3 = load(s3[:, :], a["L0_ffn_w3_s"].partition_broadcast(P))
        w1, w2 = sb("f_w1", [HB, D], stack=st), sb("f_w2", [HB, D], stack=st)
        h1, h2 = sb("f_h1", [HB, HID], stack=st), sb("f_h2", [HB, HID], stack=st)
        w3 = sb("f_w3", [DK, HID], stack=st)
        ld_w = [load(w[:, :, :], a[n].rearrange("(b p) i -> p b i", p=P))
                for w, n in ((w1, "L0_ffn_w1_w"), (w2, "L0_ffn_w2_w"), (h1, "L0_ffn_h1_w"),
                             (h2, "L0_ffn_h2_w"), (w3, "L0_ffn_w3_w"))]
        b = next_bank()
        wait(PE, *ld_s)
        ns = len(names) * HB
        t = pe.mark(PE.transpose(ps[:, b, 0:ns], rows[0:ns, :], ident[0:ns, 0:ns]))
        scale_ok = copy_out(scale[:, :], ps[:, b, 0:ns], [b], [t], eng="dve")

        def weight_T(w, name, n_out, n_in, ld):
            wT = sb(name, [n_in, n_out * P], stack=st)
            ok = []
            for k in range(n_in):
                ok += transposed(
                    lambda i, n: wT[:, k, i * P:(i + n) * P].rearrange("p (n c) -> p n c", c=P),
                    [w[:, o, k * P:(k + 1) * P] for o in range(n_out)], [ld])
            return wT, ok

        w1T, w1_ok = weight_T(w1, "f_w1T", HB, DK, ld_w[0])
        w2T, w2_ok = weight_T(w2, "f_w2T", HB, DK, ld_w[1])
        _, xnT_ok = layer_norm()
        hT = [sb(f"f_hT{i}", [HB, P], stack=st) for i in range(2)]
        gate = sb("f_gate", [HB, P], stack=st)
        wait(PE, *xnT_ok, *w1_ok, *w2_ok)
        wait(AC, scale_ok)
        wait(DV, scale_ok)
        h_ok = None
        for half in range(2):
            ba, bb = next_bank(), next_bank()
            for i in range(4):
                o = half * 4 + i
                ta = matmuls(ps[:, ba, i * P:(i + 1) * P],
                             [(w1T[:, k, o * P:(o + 1) * P], xnT[:, k, :]) for k in range(DK)])
                tb = matmuls(ps[:, bb, i * P:(i + 1) * P],
                             [(w2T[:, k, o * P:(o + 1) * P], xnT[:, k, :]) for k in range(DK)])
            for i in range(4):
                o = half * 4 + i
                wait(AC, ta)
                t = ac.mark(AC.activation(gate[:, o, :], ps[:, ba, i * P:(i + 1) * P], ACT.Silu,
                                          scale=scale[:, o:o + 1]))
                wait(DV, t, tb)
                h_ok = dv.mark(DV.scalar_tensor_tensor(
                    out=hT[0][:, o, :], in0=ps[:, bb, i * P:(i + 1) * P],
                    scalar=scale[:, HB + o:HB + o + 1], in1=gate[:, o, :], op0=ALU.mult, op1=ALU.mult))
            read_by(ba, t)
            read_by(bb, h_ok)
        for n, w in enumerate((h1, h2)):
            wT, w_ok = weight_T(w, f"f_h{n + 1}T", HB, HB, ld_w[2 + n])
            wait(PE, h_ok, *w_ok)
            src, dst = hT[n % 2], hT[1 - n % 2]
            for o in range(HB):
                if o % 4 == 0:
                    b = next_bank()
                c = o % 4 * P
                t = matmuls(ps[:, b, c:c + P], [(wT[:, k, o * P:(o + 1) * P], src[:, k, :]) for k in range(HB)])
                if o % 4 == 3:
                    wait(AC, t)
                    for i in range(4):
                        q = o - 3 + i
                        s = (2 + n) * HB + q
                        h_ok = ac.mark(AC.activation(dst[:, q, :], ps[:, b, i * P:(i + 1) * P], ACT.Gelu,
                                                     scale=scale[:, s:s + 1]))
                    read_by(b, h_ok)
        w3T, w3_ok = weight_T(w3, "f_w3T", DK, HB, ld_w[4])
        b = next_bank()
        wait(PE, h_ok, *w3_ok)
        t = matmuls(ps[:, b, 0:D], [(hT[0][:, k, :], w3T[:, k, :]) for k in range(HB)])
        y = sb("f_y", [D], stack=st)
        wait(DV, t, ld_s3)
        t = dv.mark(DV.tensor_tensor(y[:, :], ps[:, b, 0:D], s3[:, :], ALU.mult))
        read_by(b, t)
        add_to_x(y[:, :], [t])

    join()
    shared_w1 = sb("m_shared_w1", [DK, HID], stack=ctx)
    shared_w2 = sb("m_shared_w2", [HB, D], stack=ctx)
    exp_w1 = [sb(f"m_w1_{i}", [DK, HID], stack=ctx) for i in range(E_UNROLL)]
    exp_w2 = [sb(f"m_w2_{i}", [HB, D], stack=ctx) for i in range(E_UNROLL)]
    RING = 6
    W = D + 1
    st = ExitStack()
    with st:
        wsim = sb("x1_wsim", [3, D], stack=st)
        bsim = sb("x1_bsim", [1], stack=st)
        ld_sim = load(wsim[:, :, :], a["L1_xattn_w_sim"].rearrange("(n d) -> n d", n=3).partition_broadcast(P))
        ld_bsim = load(bsim[:, :], a["L1_xattn_b_sim"].partition_broadcast(P))
        ctx_one = [sb(f"ctx_one{i}", [CHUNK_TILES, W], stack=st) for i in range(RING)]
        sem_ctx1 = [Link(sem(f"s1_ctx{i}"), PE, 16) for i in range(RING)]
        ctx1_free = Link(sem("s1_ctx_free"), SP)
        for i in range(RING):
            ones_in = gp.mark(GP.memset(ctx_one[i][:, :, D:W], 1.0))

        def load_ctx1(n, src, nt=CHUNK_TILES):
            sem_ctx1[n % RING].sent_by(SP.dma_start(ctx_one[n % RING][:, 0:nt, 0:D], src))

        load_ctx1(0, ctx_rows[0:TAIL_TILES * P, :].rearrange("(p t) d -> p t d", t=TAIL_TILES), TAIL_TILES)
        for n in range(1, RING):
            load_ctx1(n, full_chunks[n - 1])
        wqv = sb("x1_wqv", [4 * DK, D], stack=st)
        bqv = sb("x1_bqv", [D], stack=st)
        ld_qv = [load(wqv[:, :, :], a["L1_xattn_W_qv"].rearrange("(b p) n -> p b n", p=P)),
                 load(bqv[:, :], a["L1_xattn_b_qv"].partition_broadcast(P))]
        ld_shared = [load(shared_w1[:, :, :], a["L1_ffn_shared_w1"].rearrange("s (k p) n -> p (s k) n", p=P), AC),
                     load(shared_w2[:, :, :], a["L1_ffn_shared_w2"].rearrange("s (b p) n -> p (s b) n", p=P), AC)]
        w1_rows = a["L1_ffn_routed_w1"].rearrange("e (k p) n -> e p k n", p=P)
        w2_rows = a["L1_ffn_routed_w2"].rearrange("e (b p) n -> e p b n", p=P)
        sem_w = [Link(sem(f"s_expert{i}"), PE, 32) for i in range(E_UNROLL)]

        def load_expert(slot, e, eng=SP):
            eng.dma_start(exp_w1[slot][:, :, :], w1_rows[e]).then_inc(sem_w[slot].sem, 16)
            eng.dma_start(exp_w2[slot][:, :, :], w2_rows[e]).then_inc(sem_w[slot].sem, 16)

        for i in range(E_UNROLL):
            load_expert(i, i, AC)

        enc_ok, encT_ok = layer_norm()
        g = sb("x1_g", [D], stack=st)
        scratch = sb("x1_scratch", [D], stack=st)
        const = sb("x1_const", [1], stack=st)
        wait(DV, enc_ok, ld_sim)
        t = dv.mark(DV.tensor_tensor(g[:, :], xn[:, :], wsim[:, 2, :], ALU.mult))
        wait(DV, t)
        g_ok = dv.mark(DV.tensor_tensor(g[:, :], g[:, :], wsim[:, 1, :], ALU.add))
        t = dv.mark(DV.tensor_tensor(scratch[:, :], xn[:, :], wsim[:, 0, :], ALU.mult))
        wait(DV, t)
        t = dv.mark(DV.tensor_reduce(const[:, :], scratch[:, :], AX.X, ALU.add))
        wait(DV, t, ld_bsim)
        const_ok = dv.mark(DV.tensor_tensor(const[:, :], const[:, :], bsim[:, :], ALU.add))
        gT_hi = sb("gT_hi", [DK, P], F32R, st)
        gT_lo = sb("gT_lo", [DK, P], F32R, st)
        b = next_bank()
        wait(PE, g_ok)
        for k in range(DK):
            t = PE.transpose(ps[:, b, k * P:(k + 1) * P], g[:, k * P:(k + 1) * P], ident[:, :])
        t = pe.mark(t)
        src = ps[:, b, 0:D].rearrange("p (k c) -> p k c", c=P)
        wait(AC, t)
        t = ac.mark(AC.copy(gT_hi[:, :, :], src))
        wait(DV, t)
        gT_ok = dv.mark(DV.tensor_tensor(gT_lo[:, :, :], src, gT_hi[:, :, :], ALU.subtract))

        ctxT_hi = [sb(f"c1T_hi{i}", [DK, CHUNK], F32R, st) for i in range(2)]
        ctxT_lo = [sb(f"c1T_lo{i}", [DK, CHUNK], F32R, st) for i in range(2)]
        pr = [sb(f"x1_pr{i}", [CHUNK], stack=st) for i in range(2)]
        prT = [sb(f"x1_prT{i}", [CHUNK], stack=st) for i in range(2)]
        negc = sb("x1_negc", [RING], stack=st)
        negm = sb("x1_negm", [RING], stack=st)
        alpha = sb("x1_alpha", [RING], stack=st)
        acc = sb("x1_acc", [W], stack=st)
        GP.memset(negm[:, :], 3e38)
        init = gp.mark(GP.memset(acc[:, :], 0.0))
        sc_ok = Link(sem("m_sc_ok"), DV)
        mx_ok = Link(sem("m_mx_ok"), AC)
        pr_ok = Link(sem("m_pr_ok"), PE)
        tr_full = Link(sem("m_tr_full"), AC)
        tr_kept = Link(sem("m_tr_kept"), PE)
        x_full = Link(sem("m_x_full"), AC)
        x_hi = Link(sem("m_x_hi"), DV)
        x_kept = Link(sem("m_x_kept"), PE)
        o_full = Link(sem("m_o_full"), DV)
        o_kept = Link(sem("m_o_kept"), PE)
        al_ok = Link(sem("m_al_ok"), DV)
        self_dv = Link(sem("m_self_dv"), DV)
        consumers = {PE: [pr_ok, tr_kept, x_kept, o_kept] + sem_ctx1, AC: [mx_ok, tr_full, x_full],
                     DV: [sc_ok, x_hi, o_full, al_ok, self_dv], SP: [ctx1_free]}
        tiles = lambda n: TAIL_TILES if n == 0 else CHUNK_TILES

        def turn_ctx(n):
            nt, c = tiles(n), ctx_one[n % RING]
            sem_ctx1[n % RING].wait()
            for k in range(DK):
                for i in range(nt):
                    m = PE.transpose(ps[:, 5 + k, i * P:(i + 1) * P], c[:, i, k * P:(k + 1) * P], ident[:, :])
            x_full.sent_by(m)
            x_full.wait()
            src = ps[:, 5:7, 0:nt * P]
            x_hi.sent_by(AC.copy(ctxT_hi[n % 2][:, :, 0:nt * P], src))
            x_hi.wait()
            x_kept.sent_by(DV.tensor_tensor(ctxT_lo[n % 2][:, :, 0:nt * P], src,
                                           ctxT_hi[n % 2][:, :, 0:nt * P], ALU.subtract))

        def score(n):
            nt = tiles(n)
            x_kept.wait()
            terms = [(q[:, k, :], c[n % 2][:, k, 0:nt * P]) for k in range(DK)
                     for q, c in ((gT_hi, ctxT_hi), (gT_hi, ctxT_lo), (gT_lo, ctxT_hi))]
            for i, (l, r) in enumerate(terms):
                m = PE.matmul(ps[:, n % 2, 0:nt * P], l, r, start=(i == 0), stop=(i == len(terms) - 1))
            sc_ok.sent_by(m)
            new, old = n % RING, (n - 1) % RING
            sc_ok.wait()
            self_dv.sent_by(DV.tensor_reduce(negc[:, new:new + 1], ps[:, n % 2, 0:nt * P], AX.X, ALU.max))
            self_dv.wait()
            mx_ok.sent_by(DV.scalar_tensor_tensor(out=negm[:, new:new + 1], in0=negc[:, new:new + 1], scalar=-1.0,
                                                 in1=negm[:, old:old + 1], op0=ALU.mult, op1=ALU.min))

        def probabilities(n):
            nt, new, old = tiles(n), n % RING, (n - 1) % RING
            mx_ok.wait()
            pr_ok.sent_by(AC.activation(pr[n % 2][:, 0:nt * P], ps[:, n % 2, 0:nt * P], ACT.Exp,
                                       bias=negm[:, new:new + 1], scale=1.0))
            al_ok.sent_by(AC.activation(alpha[:, new:new + 1], negm[:, old:old + 1], ACT.Exp,
                                       bias=negm[:, new:new + 1], scale=-1.0))

        def turn_pr(n, free=False):
            nt = tiles(n)
            pr_ok.wait()
            for i in range(nt):
                m = PE.transpose(ps[:, 2, i * P:(i + 1) * P], pr[n % 2][:, i * P:(i + 1) * P], ident[:, :])
                if i == 0 and free:
                    ctx1_free.sent_by(m)
            tr_full.sent_by(m)
            tr_full.wait()
            tr_kept.sent_by(AC.copy(prT[n % 2][:, 0:nt * P], ps[:, 2, 0:nt * P]))

        def sums(n, alone=False):
            nt, new = tiles(n), n % RING
            tr_kept.wait()
            if n > 1:
                o_kept.wait()
            for i in range(nt):
                m = PE.matmul(ps[:, 3 + n % 2, 0:W], prT[n % 2][:, i * P:(i + 1) * P], ctx_one[n % RING][:, i, :],
                              start=(i == 0), stop=(i == nt - 1))
            o_full.sent_by(m)
            al_ok.wait()
            if alone:
                DV.drain()
            o_full.wait()
            o_kept.sent_by(DV.scalar_tensor_tensor(out=acc[:, :], in0=acc[:, :], scalar=alpha[:, new:new + 1],
                                                  in1=ps[:, 3 + n % 2, 0:W], op0=ALU.mult, op1=ALU.add))

        def step(n, last=N_FULL, free=False):
            if n + 1 <= last:
                score(n + 1)
            if n + 2 <= last:
                turn_ctx(n + 2)
            if n + 1 <= last:
                probabilities(n + 1)
            if n >= 1:
                sums(n - 1, alone=n == last)
            turn_pr(n, free)

        wait(PE, gT_ok, ones_in, init)
        wait(DV, init)
        wait(AC, init)
        for b in range(8):
            wait(PE, *readers[b])
        turn_ctx(0)
        score(0)
        turn_ctx(1)
        probabilities(0)
        step(0)
        step(1, free=True)
        ctx1_free.wait()
        load_ctx1(RING, full_chunks[RING - 1])
        settle(consumers)
        n_loop = (N_FULL - RING) // RING
        with nc.Fori(0, n_loop) as i:
            for u in range(RING):
                step(2 + u + RING, last=10 ** 6, free=True)
                ctx1_free.wait()
                load_ctx1(1 + u, full_chunks[RING + u + i * RING])
            settle(consumers)
        for n in range(2 + n_loop * RING, N_FULL + 1):
            step(n)
        sums(N_FULL, alone=True)
        t = dv.mark(DV.drain())
        for b in range(8):
            readers[b] = [t]

        hat = sb("x1_hat", [D], stack=st)
        eh = sb("x1_eh", [D], stack=st)
        eb = sb("x1_eb", [D], stack=st)
        small = sb("x1_small", [8], stack=st)
        row = sb("x1_row", [P], stack=st)
        wait(DV, t)
        t = dv.mark(DV.reciprocal(small[:, 0:1], acc[:, D:W]))
        wait(DV, t)
        hat_ok = dv.mark(DV.tensor_scalar(hat[:, :], acc[:, 0:D], small[:, 0:1], None, ALU.mult))
        wait(DV, hat_ok)
        eh_ok = dv.mark(DV.tensor_tensor(eh[:, :], xn[:, :], hat[:, :], ALU.mult))
        fin = N_FULL % RING
        t = dv.mark(DV.tensor_tensor(small[:, 1:2], const[:, :], negm[:, fin:fin + 1], ALU.subtract))
        b = next_bank()
        wait(PE, t)
        t = pe.mark(PE.transpose(ps[0:1, b, 0:P], small[:, 1:2], ident[:, :]))
        wait(DV, t)
        t = dv.mark(DV.tensor_reduce(row[0:1, 0:1], ps[0:1, b, 0:P], AX.X, ALU.max))
        read_by(b, t)
        b = next_bank()
        wait(PE, t)
        t = matmuls(ps[:, b, 0:1], [(ones[0:1, :], row[0:1, 0:1])])
        wait(DV, t)
        t = dv.mark(DV.tensor_scalar(small[:, 2:3], ps[:, b, 0:1], -1.0, None, ALU.mult))
        read_by(b, t)
        wait(AC, t)
        t = ac.mark(AC.activation(small[:, 3:4], small[:, 1:2], ACT.Exp, bias=small[:, 2:3], scale=1.0))
        wait(DV, t)
        weights = sb("x1_weights", [P], stack=st)
        t = dv.mark(DV.tensor_scalar(weights[:, :], ones[:, :], small[:, 3:4], None, ALU.mult))
        b = next_bank()
        wait(PE, t)
        matmuls(ps[:, b, 0:D], [(weights[:, :], xn[:, :])])
        t = matmuls(ps[:, b, D:W], [(weights[:, :], ones[:, 0:1])])
        wait(DV, t)
        t = dv.mark(DV.reciprocal(small[:, 4:5], ps[:, b, D:W]))
        wait(DV, t)
        t = dv.mark(DV.scalar_tensor_tensor(out=eb[:, :], in0=ps[:, b, 0:D], scalar=small[:, 4:5],
                                            in1=xn[:, :], op0=ALU.mult, op1=ALU.mult))
        read_by(b, t)
        featT = sb("x1_featT", [3 * DK, P], stack=st)
        blocks = [f[:, k * P:(k + 1) * P] for f in (hat, eh, eb) for k in range(DK)]
        f_ok = transposed(lambda i, n: featT[:, i:i + n, :], blocks, [hat_ok, eh_ok, t])
        b = next_bank()
        wait(PE, *f_ok, *encT_ok, *ld_qv)
        t = matmuls(ps[:, b, 0:D], [(xnT[:, k, :], wqv[:, k, :]) for k in range(DK)]
                    + [(featT[:, k, :], wqv[:, DK + k, :]) for k in range(3 * DK)])
        last["xn_free"] = [t]
        y = sb("x1_y", [D], stack=st)
        wait(DV, t, ld_qv[1])
        t = dv.mark(DV.tensor_tensor(y[:, :], ps[:, b, 0:D], bqv[:, :], ALU.add))
        read_by(b, t)
        add_to_x(y[:, :], [t])

    join()
    st = ExitStack()
    with st:
        wn = [sb(f"a1_w{n}", [HB, D], stack=st) for n in "qkv"]
        ld = [load(w[:, :, :], a["L1_attn_" + n].rearrange("n h m -> (n h) m").rearrange("(b p) m -> p b m", p=P))
              for w, n in zip(wn, "QKV")]
        wo = sb("a1_wo", [DK, HID], stack=st)
        ld_o = load(wo[:, :, :], a["L1_attn_O"].rearrange("(k p) n -> p k n", p=P))
        wT, w_ok = [], []
        for n, (w, l) in enumerate(zip(wn, ld)):
            t = sb(f"a1_wT{n}", [DK, HID], stack=st)
            wT.append(t)
            for k in range(DK):
                w_ok += transposed(
                    lambda i, m: t[:, k, i * P:(i + m) * P].rearrange("p (n c) -> p n c", c=P),
                    [w[:, o, k * P:(k + 1) * P] for o in range(HB)], [l])
        woT = sb("a1_woT", [HB, D], stack=st)
        woT_ok = transposed(
            lambda i, n: woT[:, i // DK:(i + n) // DK, :].rearrange("p b (k c) -> p (b k) c", c=P),
            [wo[:, k, b * P:(b + 1) * P] for b in range(HB) for k in range(DK)], [ld_o])
        _, xnT_ok = layer_norm()
        wait(PE, *xnT_ok, *w_ok)
        qT = sb("a1_qT", [HB, P], stack=st)
        kbd = sb("a1_kbd", [HB, 2, P], stack=st)
        v = sb("a1_v", [HID], stack=st)
        q_ok, v_ok = [], []
        for half in range(2):
            bq, bk = next_bank(), next_bank()
            for i in range(4):
                o = half * 4 + i
                cols = slice(o * P, (o + 1) * P)
                tq = matmuls(ps[:, bq, i * P:(i + 1) * P], [(wT[0][:, k, cols], xnT[:, k, :]) for k in range(DK)])
                tk = matmuls(ps[:, bk, i * P:(i + 1) * P], [(wT[1][:, k, cols], xnT[:, k, :]) for k in range(DK)])
            q_ok.append(copy_out(qT[:, half * 4:half * 4 + 4, :],
                                 ps[:, bq, :].rearrange("p (g c) -> p g c", c=P), [bq], [tq], eng="act"))
            wait(DV, tk)
            for j in range(2):
                t = dv.mark(DV.tensor_scalar(kbd[:, half * 4:half * 4 + 4, j, :],
                                             ps[:, bk, :].rearrange("p (g c) -> p g c", c=P),
                                             mask2[:, j:j + 1], None, ALU.mult))
            read_by(bk, t)
            q_ok.append(t)
        s0 = next_banks(4)
        after = []
        wait(PE, *q_ok)
        for o in range(HB):
            t = matmuls(ps[:, s0 + o // 2, o % 2 * 2 * P:(o % 2 + 1) * 2 * P], [(qT[:, o, :], kbd[:, o, :, :])])
            if o % 2:
                after.append(t)
        for half in range(2):
            b = next_bank()
            t = matmuls(ps[:, b, :], [(xnT[:, k, :], wT[2][:, k, half * BANK:(half + 1) * BANK]) for k in range(DK)])
            v_ok.append(copy_out(v[:, half * BANK:(half + 1) * BANK], ps[:, b, :], [b], [t], eng="act"))
        last["xn_free"] = [t]
        pT = sb("a1_pT", [A1_HEADS, P], stack=st)
        pT_ok = []
        for n, (e, t) in enumerate(softmax_heads(st, s0, A1_HEADS, True, after)):
            pT_ok += transposed(lambda i, m: pT[:, n * 4:(n + 1) * 4, :],
                                [e[:, n * 4 + j, :] for j in range(4)], [t])
        zT = sb("a1_zT", [HB, P], stack=st)
        z_ok = []
        wait(PE, *v_ok)
        for half in range(2):
            b = next_bank()
            for o in range(4 * half, 4 * half + 4):
                wait(PE, pT_ok[o // 2])
                for j in range(2):
                    h = 2 * o + j
                    t = PE.matmul(ps[64 * j:64 * (j + 1), b, o % 4 * P:(o % 4 + 1) * P],
                                  v[:, h * A1_DH:(h + 1) * A1_DH], pT[:, h, :], start=True, stop=True,
                                  skip_group_check=True)
            t = pe.mark(t)
            z_ok.append(copy_out(zT[:, 4 * half:4 * half + 4, :],
                                 ps[:, b, :].rearrange("p (g c) -> p g c", c=P), [b], [t]))
        b = next_bank()
        wait(PE, *z_ok, *woT_ok)
        t = matmuls(ps[:, b, 0:D], [(zT[:, o, :], woT[:, o, :]) for o in range(HB)])
        add_to_x(ps[:, b, 0:D], [t], [b])

    join()
    st = ExitStack()
    with st:
        E = N_EXPERTS
        rw = sb("m_router", [DK, E], stack=st)
        eb_ = sb("m_bias", [E], stack=st)
        b1 = sb("m_b1_rows", [P], stack=st)
        sb1 = sb("m_sb1_rows", [P], stack=st)
        b2 = sb("m_b2", [D], stack=st)
        sb2 = sb("m_sb2", [D], stack=st)
        lds = [load(rw[:, :, :], a["L1_ffn_router_w"].rearrange("(k p) n -> p k n", p=P)),
               load(eb_[:, :], a["L1_ffn_expert_bias"].partition_broadcast(P)),
               load(b1[:, :], a["L1_ffn_routed_b1"].rearrange("e (b c) -> (e b) c", c=P)),
               load(sb1[0:HB, :], a["L1_ffn_shared_b1"].rearrange("e (b c) -> (e b) c", c=P)),
               load(b2[0:E, :], a["L1_ffn_routed_b2"]),
               load(sb2[:, :], a["L1_ffn_shared_b2"].rearrange("e d -> (e d)").partition_broadcast(P))]
        b1T = sb("m_b1T", [E, HB], stack=st)
        sb1T = sb("m_sb1T", [HB], stack=st)
        b = next_bank()
        wait(PE, *lds)
        PE.transpose(ps[:, b, 0:P], b1[:, :], ident[:, :])
        t = pe.mark(PE.transpose(ps[:, b, P:P + HB], sb1[0:HB, :], ident[0:HB, 0:HB]))
        b1_ok = copy_out(b1T[:, :, :], ps[:, b, 0:P].rearrange("p (e b) -> p e b", b=HB), [b], [t], eng="dve")
        sb1_ok = copy_out(sb1T[:, :], ps[:, b, P:P + HB], [b], [t], eng="dve")
        _, xnT_ok = layer_norm()
        b = next_bank()
        wait(PE, *xnT_ok)
        t = matmuls(ps[:, b, 0:E], [(xnT[:, k, :], rw[:, k, :]) for k in range(DK)])
        n_t = [0]

        def tmp(n):
            n_t[0] += 1
            return sb(f"m_t{n_t[0]}", [n], stack=st)

        def chain(inst):
            p = dv.mark(inst)
            wait(DV, p)
            return p

        lg = tmp(E)
        wait(DV, t, *lds)
        t = chain(DV.tensor_tensor(lg[:, :], ps[:, b, 0:E], eb_[:, :], ALU.add))
        read_by(b, t)
        tops, hots = [], []
        for n in range(2):
            m, eq, cand, first_, hot = tmp(1), tmp(E), tmp(E), tmp(1), tmp(E)
            chain(DV.tensor_reduce(m[:, :], lg[:, :], AX.X, ALU.max))
            chain(DV.tensor_scalar(eq[:, :], lg[:, :], m[:, 0:1], None, ALU.is_equal))
            chain(DV.scalar_tensor_tensor(out=cand[:, :], in0=eq[:, :], scalar=-99.0, in1=pos99[:, :],
                                          op0=ALU.mult, op1=ALU.add))
            chain(DV.tensor_reduce(first_[:, :], cand[:, :], AX.X, ALU.min))
            chain(DV.tensor_scalar(hot[:, :], pos[:, :], first_[:, 0:1], None, ALU.is_equal))
            tops.append(m)
            hots.append(hot)
            if n == 0:
                rest = tmp(E)
                chain(DV.scalar_tensor_tensor(out=rest[:, :], in0=hot[:, :], scalar=-3e38, in1=lg[:, :],
                                              op0=ALU.mult, op1=ALU.add))
                lg = rest
        d, e2, s, r, w2_ = tmp(1), tmp(1), tmp(1), tmp(1), tmp(1)
        comb, comb1 = tmp(E), tmp(E)
        t = chain(DV.tensor_tensor(d[:, :], tops[1][:, :], tops[0][:, :], ALU.subtract))
        wait(AC, t)
        t = ac.mark(AC.activation(e2[:, :], d[:, :], ACT.Exp))
        wait(DV, t)
        chain(DV.tensor_scalar(s[:, :], e2[:, :], 1.0, None, ALU.add))
        chain(DV.reciprocal(r[:, :], s[:, :]))
        chain(DV.tensor_tensor(w2_[:, :], e2[:, :], r[:, :], ALU.mult))
        chain(DV.tensor_scalar(comb1[:, :], hots[0][:, :], r[:, 0:1], None, ALU.mult))
        t = chain(DV.scalar_tensor_tensor(out=comb[:, :], in0=hots[1][:, :], scalar=w2_[:, 0:1], in1=comb1[:, :],
                                          op0=ALU.mult, op1=ALU.add))
        b = next_bank()
        wait(PE, t)
        t = pe.mark(PE.transpose(ps[0:E, b, 0:P], comb[:, :], ident[:, :]))
        combT = sb("m_combT", [P], stack=st)
        t = copy_out(combT[0:E, :], ps[0:E, b, 0:P], [b], [t], eng="dve")
        b = next_bank()
        wait(PE, t)
        t = matmuls(ps[:, b, 0:D], [(combT[0:E, :], b2[0:E, :])])
        acc = sb("m_acc", [D], stack=st)
        wait(DV, t)
        acc_ok = dv.mark(DV.tensor_tensor(acc[:, :], ps[:, b, 0:D], sb2[:, :], ALU.add))
        read_by(b, acc_ok)

        hid = [sb(f"m_hid{i}", [HB, P], stack=st) for i in range(2)]
        acc1 = sb("m_acc1", [D], stack=st)
        accs = [acc, acc1]
        acc1_ok = gp.mark(GP.memset(acc1[:, :], 0.0))
        h_act = Link(sem("e_h_act"), AC)
        h_dve = Link(sem("e_h_dve"), DV)
        r_act = Link(sem("e_r_act"), PE)
        r_dve = Link(sem("e_r_dve"), PE)
        y_full = Link(sem("e_y_full"), DV)
        y_kept = Link(sem("e_y_kept"), PE)
        w_free = Link(sem("e_w_free"), SP)
        consumers = {PE: [r_act, r_dve, y_kept] + sem_w, AC: [h_act], DV: [h_dve, y_full], SP: [w_free]}

        def up(n, w1, bias, free=False):
            for half, link in enumerate((h_act, h_dve)):
                bank = ps[:, 2 * (n % 2) + half, :]
                for i in range(4):
                    o = half * 4 + i
                    for k in range(DK):
                        m = PE.matmul(bank[:, i * P:(i + 1) * P], w1[:, k, o * P:(o + 1) * P], xnT[:, k, :],
                                      start=(k == 0), stop=(k == DK - 1))
                        if free and o == 0 and k == 0:
                            w_free.sent_by(m)
                link.sent_by(m)
            h_act.wait()
            for i in range(4):
                t = AC.activation(hid[n % 2][:, i, :], ps[:, 2 * (n % 2), i * P:(i + 1) * P], ACT.Relu,
                                  bias=bias(i), scale=1.0)
            r_act.sent_by(t)
            h_dve.wait()
            for i in range(4):
                t = DV.tensor_scalar(hid[n % 2][:, 4 + i, :], ps[:, 2 * (n % 2) + 1, i * P:(i + 1) * P],
                                     bias(4 + i), 0.0, ALU.add, ALU.max)
            r_dve.sent_by(t)

        def down(n, w2, weight):
            r_act.wait()
            r_dve.wait()
            if n > 1:
                y_kept.wait()
            y = ps[:, 4 + n % 2, 0:D]
            for o in range(HB):
                m = PE.matmul(y, hid[n % 2][:, o, :], w2[:, o, :], start=(o == 0), stop=(o == HB - 1))
            y_full.sent_by(m)
            y_full.wait()
            s = accs[n % 2]
            if weight is None:
                t = DV.tensor_tensor(s[:, :], s[:, :], y, ALU.add)
            else:
                t = DV.scalar_tensor_tensor(out=s[:, :], in0=y, scalar=weight, in1=s[:, :],
                                            op0=ALU.mult, op1=ALU.add)
            y_kept.sent_by(t)

        def step(n, e, free):
            slot = n % E_UNROLL
            sem_w[slot].wait()
            up(n + 1, exp_w1[slot], lambda o: bias_rows(e + 1, o), free)
            down(n, exp_w2[(n - 1) % E_UNROLL], comb[:, column(e)])

        column = lambda e: slice(e, e + 1) if isinstance(e, int) else bass.ds(e, 1)
        b1T_flat = b1T[:, :, :].rearrange("p e b -> p (e b)")
        bias_rows = lambda e, o: b1T_flat[:, column(e * HB + o)]

        wait(PE, *ld_shared, *[r for b in range(8) for r in readers[b]])
        wait(DV, acc_ok, acc1_ok, b1_ok, sb1_ok)
        wait(AC, b1_ok, sb1_ok)
        up(0, shared_w1, lambda o: sb1T[:, o:o + 1])
        sem_w[0].wait()
        up(1, exp_w1[0], lambda o: bias_rows(0, o))
        down(0, shared_w2, None)
        step(1, 0, False)
        settle(consumers)
        n_loop = (E - E_UNROLL) // E_UNROLL
        with nc.Fori(0, n_loop) as i:
            for u in range(E_UNROLL):
                step(2 + u, i * E_UNROLL + (1 + u), True)
                w_free.wait()
                load_expert(u, i * E_UNROLL + (E_UNROLL + u))
            settle(consumers)
        for e in range(1 + n_loop * E_UNROLL, E - 1):
            step(e + 1, e, False)
        down(E, exp_w2[(E - 1) % E_UNROLL], comb[:, E - 1:E])
        y = sb("m_y", [D], stack=st)
        DV.drain()
        t = dv.mark(DV.tensor_tensor(y[:, :], acc[:, :], acc1[:, :], ALU.add))
        add_to_x(y[:, :], [t])

    return finish()




INS = ["x", "ctx_1024", "L0_xattn_wq", "L0_xattn_wk", "L0_xattn_wv", "L0_attn_Wq", "L0_attn_Wk",
       "L0_attn_Wv", "L0_attn_Wo", "L0_ffn_w1_w", "L0_ffn_w1_s", "L0_ffn_w2_w", "L0_ffn_w2_s",
       "L0_ffn_h1_w", "L0_ffn_h1_s", "L0_ffn_h2_w", "L0_ffn_h2_s", "L0_ffn_w3_w", "L0_ffn_w3_s",
       "L1_xattn_w_sim", "L1_xattn_b_sim", "L1_xattn_W_qv", "L1_xattn_b_qv", "L1_attn_Q", "L1_attn_K",
       "L1_attn_V", "L1_attn_O", "L1_ffn_router_w", "L1_ffn_expert_bias", "L1_ffn_shared_w1",
       "L1_ffn_shared_b1", "L1_ffn_shared_w2", "L1_ffn_shared_b2", "L1_ffn_routed_w1",
       "L1_ffn_routed_b1", "L1_ffn_routed_w2", "L1_ffn_routed_b2"]


def kernel(**inputs):
    import concourse.bacc as bacc
    from concourse.bass_utils import run_bass_kernel_spmd

    nc = bacc.Bacc("TRN2", target_bir_lowering=False, num_devices=1)
    arrays, args = {}, {}
    for name in INS:
        v = np.ascontiguousarray(inputs[name])
        arrays[f"in_{name}"] = v
        args[name] = nc.dram_tensor(f"in_{name}", v.shape, mybir.dt.from_np(v.dtype), kind="ExternalInput").ap()
    out = nc.dram_tensor("out_0", (1, P, D), F32, kind="ExternalOutput").ap()
    build(nc, args, out)
    return run_bass_kernel_spmd(nc, [arrays], core_ids=[0]).results[0]["out_0"]
```

```python
from contextlib import ExitStack

import concourse.bass as bass
from concourse import mybir
import numpy as np

F32 = mybir.dt.float32
F32R = mybir.dt.float32r
ALU = mybir.AluOpType
ACT = mybir.ActivationFunctionType
AX = mybir.AxisListType

P = 128
D = 256
DK = D // P
EPS = 1e-5
BANK = 512

N_KEYS = 12544
TILES = N_KEYS // P
CHUNK_TILES = 4
CHUNK = CHUNK_TILES * P
TAIL_TILES = TILES % CHUNK_TILES
N_FULL = TILES // CHUNK_TILES

X0_HEADS = 16
X0_DK = 64
X0_DV = D // X0_HEADS
PAIRS = X0_HEADS // 2
QUADS = X0_HEADS // 4
PADV = 32

A0_HEADS, A0_KV, A0_DH = 16, 4, 16
HID = 1024
HB = HID // P
A1_HEADS, A1_DH = 16, 64
N_EXPERTS = 16
E_UNROLL = 4


class Done:

    def __init__(self, sem):
        self.sem, self.n = sem, 0

    def mark(self, inst):
        inst.then_inc(self.sem, 1)
        self.n += 1
        return (self.sem, self.n)


class Link:

    def __init__(self, sem, consumer, step=1):
        self.sem, self.consumer, self.step, self.n = sem, consumer, step, 0

    def sent_by(self, inst):
        inst.then_inc(self.sem, self.step)

    def wait(self):
        self.n += self.step
        self.consumer.wait_ge(self.sem, self.n)

    def settle(self):
        if self.n:
            self.consumer.sem_inc(self.sem, -self.n)
            self.n = 0


def build(nc, a, out):
    ctx = ExitStack()
    PE, AC, DV, GP, SP = nc.tensor, nc.scalar, nc.vector, nc.gpsimd, nc.sync

    def sb(name, shape, dt=F32, stack=ctx):
        return stack.enter_context(nc.sbuf_tensor(name, [P] + list(shape), dt))

    def sem(name):
        return ctx.enter_context(nc.semaphore(name))

    pe, ac, dv, gp = (Done(sem("s_" + n)) for n in ("pe", "act", "dve", "pool"))
    seen = {}

    def wait(eng, *points):
        for s, v in points:
            key = (id(eng), id(s))
            if seen.get(key, 0) < v:
                eng.wait_ge(s, v)
                seen[key] = v

    n_loads = [0]

    def load(dst, src, eng=SP):
        n_loads[0] += 1
        s = sem(f"s_load{n_loads[0]}")
        eng.dma_start(dst, src).then_inc(s, 16)
        return (s, 16)

    def settle(consumers):
        for eng, links in consumers.items():
            if any(l.n for l in links):
                if eng is not SP:
                    eng.drain()
                for l in links:
                    l.settle()

    ps = ctx.enter_context(nc.psum_tensor("ps", [P, 8, BANK], F32))

    ident = sb("ident", [P])
    mask4 = sb("mask4", [4])
    mask2 = sb("mask2", [2])
    ones = sb("ones", [P])
    minus_half = sb("minus_half", [1])
    pos = sb("pos", [N_EXPERTS])
    pos99 = sb("pos99", [N_EXPERTS])
    GP.memset(ident[:, :], 0.0)
    GP.memset(mask4[:, :], 1.0)
    GP.memset(minus_half[:, :], -0.5)
    GP.memset(mask2[:, :], 1.0)
    c0 = gp.mark(GP.memset(ones[:, :], 1.0))
    wait(GP, c0)
    GP.affine_select(out=ident[:, :], in_=ident[:, :], compare_op=ALU.not_equal, fill=1.0,
                     base=0, pattern=[[-1, P]], channel_multiplier=1)
    GP.affine_select(out=mask4[:, :], in_=mask4[:, :], compare_op=ALU.is_ge, fill=0.0,
                     base=0, pattern=[[-32, 4]], channel_multiplier=1)
    c1 = gp.mark(GP.affine_select(out=mask2[:, :], in_=mask2[:, :], compare_op=ALU.is_ge, fill=0.0,
                                  base=0, pattern=[[-64, 2]], channel_multiplier=1))
    wait(GP, c1)
    GP.affine_select(out=mask4[:, :], in_=mask4[:, :], compare_op=ALU.is_ge, fill=0.0,
                     base=31, pattern=[[32, 4]], channel_multiplier=-1)
    GP.affine_select(out=mask2[:, :], in_=mask2[:, :], compare_op=ALU.is_ge, fill=0.0,
                     base=63, pattern=[[64, 2]], channel_multiplier=-1)
    GP.iota(pos[:, :], pattern=[[1, N_EXPERTS]], base=0, channel_multiplier=0,
            allow_small_or_imprecise_dtypes=True)
    consts = gp.mark(GP.iota(pos99[:, :], pattern=[[1, N_EXPERTS]], base=99, channel_multiplier=0,
                             allow_small_or_imprecise_dtypes=True))
    for e in (PE, DV, AC):
        wait(e, consts)

    xbuf = [sb("x_even", [D]), sb("x_odd", [D])]
    xn = sb("xn", [D])
    xnT = sb("xnT", [DK, P])
    stat = sb("stat", [8])
    mv = sb("mv", [2])
    rstd = sb("rstd", [1])
    last = {"x": None, "xn_free": []}
    state = {"x": 0}

    readers = {b: [] for b in range(8)}
    turn = [0]

    def next_bank():
        b = turn[0] % 8
        turn[0] += 1
        wait(PE, *readers[b])
        readers[b] = []
        return b

    def next_banks(n):
        if turn[0] % 8 + n > 8:
            turn[0] += 8 - turn[0] % 8
        return [next_bank() for _ in range(n)][0]

    def read_by(b, point, n=1):
        for i in range(n):
            readers[b + i].append(point)

    flip = [0]

    def copy_out(dst, src, banks, after, mul=None, eng=None):
        flip[0] += 1
        use_act = flip[0] % 2 if eng is None else eng == "act"
        if use_act:
            wait(AC, *after)
            i = AC.copy(dst, src) if mul is None else AC.mul(dst, src, mul)
            p = ac.mark(i)
        else:
            wait(DV, *after)
            i = (DV.tensor_copy(dst, src) if mul is None
                 else DV.tensor_scalar(dst, src, mul, None, ALU.mult))
            p = dv.mark(i)
        for b in banks:
            read_by(b, p)
        return p

    def matmuls(dst, pairs):
        for i, (l, r) in enumerate(pairs):
            m = PE.matmul(dst, l, r, start=(i == 0), stop=(i == len(pairs) - 1))
        return pe.mark(m)

    def transposed(dst, blocks, after):
        points = []
        per = BANK // P
        rows = blocks[0].shape[0]
        for i in range(0, len(blocks), per):
            part = blocks[i:i + per]
            b = next_bank()
            wait(PE, *after)
            for j, blk in enumerate(part):
                t = PE.transpose(ps[:, b, j * P:j * P + rows], blk, ident[0:rows, 0:rows])
            t = pe.mark(t)
            points.append(copy_out(dst(i, len(part)),
                                   ps[:, b, 0:len(part) * P].rearrange("p (n c) -> p n c", c=P)[:, :, 0:rows],
                                   [b], [t]))
        return points

    def layer_norm():
        x = xbuf[state["x"]]
        wait(DV, last["x"])
        s0 = dv.mark(DV.bn_stats(stat[:, 0:6], x[:, :]))
        wait(DV, s0)
        s1 = dv.mark(DV.bn_aggr(mv[:, :], stat[:, 0:6]))
        wait(DV, s1)
        s2 = dv.mark(DV.tensor_scalar(mv[:, 1:2], mv[:, 1:2], EPS, None, ALU.add))
        wait(GP, s2)
        s2 = gp.mark(GP.tensor_tensor(rstd[:, :], mv[:, 1:2], minus_half[:, :], ALU.pow))
        wait(DV, s2, *last["xn_free"])
        s3 = dv.mark(DV.tensor_scalar(xn[:, :], x[:, :], mv[:, 0:1], rstd[:, 0:1], ALU.subtract, ALU.mult))
        tp = transposed(lambda i, n: xnT[:, :, :], [xn[:, k * P:(k + 1) * P] for k in range(DK)], [s3])
        last["xn_free"] = tp
        return s3, tp

    def add_to_x(branch, after, banks=()):
        x, y = xbuf[state["x"]], xbuf[1 - state["x"]]
        wait(DV, *after)
        last["x"] = dv.mark(DV.tensor_tensor(y[:, :], x[:, :], branch, ALU.add))
        for b in banks:
            read_by(b, last["x"])
        state["x"] = 1 - state["x"]

    def bc(ap, n):
        return ap.unsqueeze(ap.ndim).to_broadcast(list(ap.shape) + [n])

    def finish():
        wait(SP, last["x"])
        s = sem("s_out")
        SP.dma_start(out.rearrange("b s d -> (b s) d"), xbuf[state["x"]][:, :]).then_inc(s, 16)
        SP.wait_ge(s, 16)
        ctx.close()

    ld_x = load(xbuf[0][:, :], a["x"].rearrange("b s d -> (b s) d"))
    last["x"] = ld_x

    ctx_rows = a["ctx_1024"].rearrange("b s d -> (b s) d")
    st = ExitStack()
    with st:
        wk_hi, wk_lo = (sb(f"wk_{part}", [DK, X0_HEADS * X0_DK], F32R, st) for part in ("hi", "lo"))
        wv_hi, wv_lo = (sb(f"wv_{part}", [DK, D], F32R, st) for part in ("hi", "lo"))
        q_hi = sb("q_hi", [X0_HEADS, P], F32R, st)
        q_lo = sb("q_lo", [X0_HEADS, P], F32R, st)
        top, low = slice(0, X0_DK), slice(X0_DK, P)
        ctx_nat = [sb(f"ctx_nat{i}", [CHUNK_TILES, D], stack=st) for i in range(2)]
        sem_ctx = [Link(sem(f"s_ctx{i}"), PE, 16) for i in range(2)]
        ctx_free = Link(sem("s_ctx_free"), SP)

        def load_ctx(slot, rows, nt):
            sem_ctx[slot].sent_by(SP.dma_start(ctx_nat[slot][:, 0:nt, :],
                                              rows.rearrange("(p t) d -> p t d", t=nt)))

        wq = sb("x0_wq", [DK, X0_HEADS * X0_DK], stack=st)
        wk = sb("x0_wk", [DK, X0_HEADS * X0_DK], stack=st)
        wv = sb("x0_wv", [DK, D], stack=st)
        tail_rows = TAIL_TILES * P
        full_chunks = ctx_rows[tail_rows:N_KEYS, :].rearrange("(c p t) d -> c p t d", p=P, t=CHUNK_TILES)
        halves = [slice(n * BANK, (n + 1) * BANK) for n in range(2)]
        wk_in, wq_in = (a["L0_xattn_" + n].rearrange("(k p) n -> p k n", p=P) for n in ("wk", "wq"))
        ld_wk = [load(wk[:, :, c], wk_in[:, :, c], AC) for c in halves]
        load_ctx(0, ctx_rows[0:tail_rows, :], TAIL_TILES)
        ld_wq = [load(wq[:, :, c], wq_in[:, :, c]) for c in halves]
        ld_wv = load(wv[:, :, :], a["L0_xattn_wv"].rearrange("(k p) n -> p k n", p=P), AC)
        load_ctx(1, ctx_rows[tail_rows:tail_rows + CHUNK, :], CHUNK_TILES)

        def split(hi, lo, w, cols, ld):
            wait(AC, ld)
            t = ac.mark(AC.copy(hi[:, :, cols], w[:, :, cols]))
            wait(DV, t, ld)
            return dv.mark(DV.tensor_tensor(lo[:, :, cols], w[:, :, cols], hi[:, :, cols], ALU.subtract))

        def queries(half, xnT_ok):
            b = next_bank()
            wait(PE, ld_wq[half], *xnT_ok)
            for i in range(4):
                p = 4 * half + i
                t = matmuls(ps[:, b, i * P:(i + 1) * P],
                            [(wq[:, k, p * P:(p + 1) * P], xnT[:, k, :]) for k in range(DK)])
            wait(AC, t)
            scale, parts = float(X0_DK) ** -0.5, []
            for j, rows in enumerate((top, low)):
                parts.append((rows, ps[rows, b, :].rearrange("p (h c) -> p h c", c=P),
                              slice(8 * half + j, 8 * half + 8, 2)))
            for rows, src, hs in parts:
                for dst in (top, low):
                    t = ac.mark(AC.mul(q_hi[dst, hs, :], src, scale))
            wait(DV, t)
            for rows, src, hs in parts:
                for dst in (top, low):
                    t = dv.mark(DV.scalar_tensor_tensor(out=q_lo[dst, hs, :], in0=src, scalar=scale,
                                                        in1=q_hi[rows, hs, :], op0=ALU.mult, op1=ALU.subtract))
            read_by(b, t)
            return t

        keys = sb("keys", [X0_HEADS, CHUNK], F32R, st)
        ctxT_hi = [sb(f"ctxT_hi{i}", [DK, CHUNK], F32R, st) for i in range(2)]
        ctxT_lo = [sb(f"ctxT_lo{i}", [DK, CHUNK], F32R, st) for i in range(2)]
        vals = [sb(f"vals{i}", [CHUNK_TILES, X0_HEADS, PADV], stack=st) for i in range(2)]
        probs = [sb(f"probs{i}", [2, CHUNK], stack=st) for i in range(2)]
        probsT = [sb(f"probsT{i}", [4, CHUNK], stack=st) for i in range(2)]
        outT = sb("outT", [QUADS, P], stack=st)
        negm = [sb(f"negm{i}", [X0_HEADS], stack=st) for i in range(2)]
        negc = sb("negc", [X0_HEADS], stack=st)
        dm = sb("dm", [X0_HEADS], stack=st)
        alpha = sb("alpha", [X0_HEADS], stack=st)
        VW = X0_DV + 1
        acc = sb("acc", [X0_HEADS, VW], stack=st)
        GP.memset(negm[1][:, :], 3e38)
        GP.memset(acc[:, :, :], 0.0)
        GP.memset(vals[0][:, :, :, X0_DV:PADV], 1.0)
        init = gp.mark(GP.memset(vals[1][:, :, :, X0_DV:PADV], 1.0))

        to_max = Link(sem("l_to_max"), DV)
        to_exp = Link(sem("l_to_exp"), AC)
        to_turn = Link(sem("l_to_turn"), PE)
        turned0 = Link(sem("l_turned0"), AC)
        turned1 = Link(sem("l_turned1"), DV)
        kept0 = Link(sem("l_kept0"), PE)
        kept1 = Link(sem("l_kept1"), PE)
        piece_to_act = Link(sem("l_piece_to_act"), AC)
        piece_to_dve = Link(sem("l_piece_to_dve"), DV)
        hi_kept = Link(sem("l_hi_kept"), DV)
        piece_from_act = Link(sem("l_piece_from_act"), PE)
        piece_from_dve = Link(sem("l_piece_from_dve"), PE)
        k_full = Link(sem("l_k_full"), AC)
        k_kept = Link(sem("l_k_kept"), PE)
        out_full = Link(sem("l_out_full"), AC)
        out_kept = Link(sem("l_out_kept"), PE)
        alpha_ok = Link(sem("l_alpha_ok"), DV)
        self_dv = Link(sem("l_self_dv"), DV)

        S = lambda i: ps[:, 2 * i:2 * i + 2, :]
        T0, T1, K, O = (ps[:, b, :] for b in (4, 5, 6, 7))
        consumers = {
            PE: [to_turn, kept0, kept1, piece_from_act, piece_from_dve, k_kept, out_kept] + sem_ctx,
            AC: [to_exp, turned0, piece_to_act, k_full, out_full],
            DV: [to_max, turned1, piece_to_dve, hi_kept, alpha_ok, self_dv],
            SP: [ctx_free],
        }

        def k_products(slot, p, nt, K=K, free=False, wait_kept=True):
            cols = slice(0, nt * P)
            terms = [(w[:, k, p * P:(p + 1) * P], c[slot][:, k, cols]) for k in range(DK)
                     for w, c in ((wk_hi, ctxT_hi), (wk_hi, ctxT_lo), (wk_lo, ctxT_hi))]
            if wait_kept:
                k_kept.wait()
            for n, (l, r) in enumerate(terms):
                m = PE.matmul(K[:, cols], l, r, start=(n == 0), stop=(n == len(terms) - 1))
                if free and n == 0:
                    ctx_free.sent_by(m)
            k_full.sent_by(m)

        def k_high(p, nt, K=K):
            cols = slice(0, nt * P)
            k_full.wait()
            for j, half in enumerate((top, low)):
                hi_kept.sent_by(AC.copy(keys[half, 2 * p + j, cols], K[half, cols]))

        def k_low(p, nt, K=K):
            cols = slice(0, nt * P)
            for j, (half, other) in enumerate(((top, low), (low, top))):
                hi_kept.wait()
                m = DV.tensor_tensor(keys[other, 2 * p + j, cols], K[half, cols],
                                     keys[half, 2 * p + j, cols], ALU.subtract)
            k_kept.sent_by(m)

        def x_piece(slot, k, nt):
            if k == 0:
                sem_ctx[slot].wait()
            for t in range(nt):
                m = PE.transpose(T0[:, t * P:(t + 1) * P], ctx_nat[slot][:, t, k * P:(k + 1) * P], ident[:, :])
            piece_to_act.sent_by(m)

        def x_high(slot, k, nt):
            piece_to_act.wait()
            hi_kept.sent_by(AC.copy(ctxT_hi[slot][:, k, 0:nt * P], T0[:, 0:nt * P]))

        def x_low(slot, k, nt):
            hi_kept.wait()
            piece_from_dve.sent_by(DV.tensor_tensor(ctxT_lo[slot][:, k, 0:nt * P], T0[:, 0:nt * P],
                                                   ctxT_hi[slot][:, k, 0:nt * P], ALU.subtract))

        def v_piece(slot, t):
            cols = slice(t * P, (t + 1) * P)
            terms = [(l[slot][:, k, cols], r[:, k, :]) for k in range(DK)
                     for l, r in ((ctxT_hi, wv_hi), (ctxT_hi, wv_lo), (ctxT_lo, wv_hi))]
            for n, (l, r) in enumerate(terms):
                m = PE.matmul(T0[:, 0:D], l, r, start=(n == 0), stop=(n == len(terms) - 1))
            piece_to_act.sent_by(m)

        def keep_v(slot, t):
            piece_to_act.wait()
            piece_from_act.sent_by(AC.copy(vals[slot][:, t, :, 0:X0_DV],
                                      T0[:, 0:D].rearrange("p (h c) -> p h c", h=X0_HEADS)))

        def scores(slot, p, nt):
            for j in range(2):
                h = 2 * p + j
                for n, q in enumerate((q_hi, q_lo)):
                    m = PE.matmul(S(p % 2)[:, j, 0:nt * P], q[:, h, :], keys[:, h, 0:nt * P],
                                  start=(n == 0), stop=(n == 1))
            to_max.sent_by(m)

        def maxima(slot, p, nt):
            to_max.wait()
            self_dv.sent_by(DV.tensor_reduce(negc[:, 2 * p:2 * p + 2], S(p % 2)[:, :, 0:nt * P], AX.X, ALU.max))
            self_dv.wait()
            new = DV.scalar_tensor_tensor(
                out=negm[slot][:, 2 * p:2 * p + 2], in0=negc[:, 2 * p:2 * p + 2], scalar=-1.0,
                in1=negm[1 - slot][:, 2 * p:2 * p + 2], op0=ALU.mult, op1=ALU.min)
            if p == PAIRS - 1:
                self_dv.sent_by(new)
                self_dv.wait()
                new = DV.tensor_tensor(dm[:, :], negm[slot][:, :], negm[1 - slot][:, :], ALU.subtract)
            to_exp.sent_by(new)

        def exps(slot, p, nt):
            to_exp.wait()
            for j in range(2):
                i = AC.activation(probs[p % 2][:, j, 0:nt * P], S(p % 2)[:, j, 0:nt * P], ACT.Exp,
                                  bias=negm[slot][:, 2 * p + j:2 * p + j + 1], scale=1.0)
            to_turn.sent_by(i)
            if p == PAIRS - 1:
                alpha_ok.sent_by(AC.activation(alpha[:, :], dm[:, :], ACT.Exp))

        def turn_probs(p, nt, piece_kept):
            to_turn.wait()
            for j, bank, link in ((1, T1, turned1), (0, T0, turned0)):
                if j == 0 and piece_kept:
                    piece_kept.wait()
                for t in range(nt):
                    m = PE.transpose(bank[:, t * P:(t + 1) * P], probs[p % 2][:, j, t * P:(t + 1) * P],
                                     ident[:, :])
                link.sent_by(m)

        def keep_turned0(p, nt):
            dst = probsT[p // 2 % 2]
            turned0.wait()
            kept0.sent_by(AC.copy(dst[:, 2 * (p % 2), 0:nt * P], T0[:, 0:nt * P]))

        def keep_turned1(p, nt):
            dst = probsT[p // 2 % 2]
            turned1.wait()
            kept1.sent_by(DV.tensor_copy(dst[:, 2 * (p % 2) + 1, 0:nt * P], T1[:, 0:nt * P]))

        def weighted(slot, q, nt, half):
            for t in range(half * nt // 2, (half + 1) * nt // 2):
                for j in range(4):
                    m = PE.matmul(O[PADV * j:PADV * (j + 1), q * P:(q + 1) * P], vals[slot][:, t, 4 * q + j, :],
                                  probsT[q % 2][:, j, t * P:(t + 1) * P], start=(t == 0), stop=(t == nt - 1),
                                  skip_group_check=True)
            if q == QUADS - 1 and half:
                out_full.sent_by(m)

        def keep_out():
            out_full.wait()
            out_kept.sent_by(AC.copy(outT[:, :, :], O.rearrange("p (q c) -> p q c", c=P)))

        def out_piece():
            for q in range(QUADS):
                m = PE.transpose(T0[:, q * P:(q + 1) * P], outT[:, q, :], ident[:, :])
            piece_to_dve.sent_by(m)

        def add_out():
            alpha_ok.wait()
            self_dv.sent_by(DV.tensor_tensor(acc[:, :, :], acc[:, :, :], bc(alpha[:, :], VW), ALU.mult))
            piece_to_dve.wait()
            self_dv.wait()
            piece_from_dve.sent_by(DV.tensor_tensor(
                acc[:, :, :], acc[:, :, :], T0.rearrange("p (h c) -> p h c", c=PADV)[:, :, 0:VW], ALU.add))

        X_STEPS, OUT_STEP, V_STEPS = (0, 3), 4, (1, 2, 5, 6)

        def chunk(slot, nt, prev_nt, ahead):
            for p in range(PAIRS):
                if p < PAIRS - 1:
                    pair = (slot, p + 1, nt)
                else:
                    pair = (1 - slot, 0, CHUNK_TILES) if ahead else None
                x = X_STEPS.index(p) if ahead > 1 and p in X_STEPS else None
                v = V_STEPS.index(p) if ahead and p in V_STEPS else None
                out_here = prev_nt and p == OUT_STEP
                turned_before = prev_nt or p
                if pair:
                    scores(*pair)
                if turned_before:
                    kept0.wait()
                piece_kept = None
                if x is not None:
                    x_piece(slot, x, CHUNK_TILES)
                    piece_kept = piece_from_dve
                if out_here:
                    out_piece()
                    piece_kept = piece_from_dve
                if ahead:
                    k_products(1 - slot, p, CHUNK_TILES, free=ahead > 1 and p == X_STEPS[-1] + 1)
                elif p == 0:
                    k_kept.wait()
                if v is not None:
                    v_piece(1 - slot, v)
                    piece_kept = piece_from_act
                if turned_before:
                    kept1.wait()
                if p >= 2:
                    if prev_nt and p == 2:
                        out_kept.wait()
                    weighted(slot, p // 2 - 1, nt, p % 2)
                elif prev_nt:
                    weighted(1 - slot, QUADS - 1, prev_nt, p)
                turn_probs(p, nt, piece_kept)
                if x is not None:
                    x_high(slot, x, CHUNK_TILES)
                if ahead:
                    k_high(p, CHUNK_TILES)
                if v is not None:
                    keep_v(1 - slot, v)
                keep_turned0(p, nt)
                if pair:
                    exps(*pair)
                if prev_nt and p == 1:
                    keep_out()
                if pair:
                    maxima(*pair)
                if x is not None:
                    x_low(slot, x, CHUNK_TILES)
                if out_here:
                    add_out()
                if ahead:
                    k_low(p, CHUNK_TILES)
                keep_turned1(p, nt)

        def load_chunk(slot, n):
            ctx_free.wait()
            sem_ctx[slot].sent_by(SP.dma_start(ctx_nat[slot][:, :, :], full_chunks[n - 1]))

        key_banks = (K, O, T1)

        def first_keys(pairs):
            for p in pairs:
                bank = key_banks[p % len(key_banks)]
                k_products(0, p, TAIL_TILES, bank, wait_kept=p >= len(key_banks), free=p in (0, 6))
                k_high(p, TAIL_TILES, bank)
                k_low(p, TAIL_TILES, bank)

        def turn_block(slot, k, nt):
            x_piece(slot, k, nt)
            x_high(slot, k, nt)
            x_low(slot, k, nt)

        for k in range(DK):
            turn_block(0, k, TAIL_TILES)
            piece_from_dve.wait()
        wk_ok = split(wk_hi, wk_lo, wk, halves[0], ld_wk[0])
        _, xnT_ok = layer_norm()
        wait(PE, wk_ok)
        first_keys((0, 1))
        wk_ok = split(wk_hi, wk_lo, wk, halves[1], ld_wk[1])
        queries(0, xnT_ok)
        first_keys((2, 3))
        wait(PE, wk_ok)
        wv_ok = split(wv_hi, wv_lo, wv, slice(0, D), ld_wv)
        turn_block(1, 0, CHUNK_TILES)
        first_keys((4, 5))
        wait(PE, wv_ok)
        wait(AC, init)
        wait(DV, init)
        piece_from_dve.wait()
        v_piece(0, 0)
        keep_v(0, 0)
        q_ok = queries(1, xnT_ok)
        last["xn_free"] = last["xn_free"] + [q_ok]
        piece_from_act.wait()
        turn_block(1, 1, CHUNK_TILES)
        first_keys((6, 7))
        piece_from_dve.wait()
        v_piece(0, 1)
        keep_v(0, 1)
        for _ in key_banks[1:]:
            k_kept.wait()
        wait(PE, q_ok, init, *[r for b in range(8) for r in readers[b]])
        scores(0, 0, TAIL_TILES)
        maxima(0, 0, TAIL_TILES)
        piece_from_act.wait()
        exps(0, 0, TAIL_TILES)
        load_chunk(0, 2)
        load_chunk(1, 3)
        chunk(0, TAIL_TILES, 0, 2)
        load_chunk(0, 4)
        chunk(1, CHUNK_TILES, TAIL_TILES, 2)
        settle(consumers)
        n_loop = (N_FULL - 4) // 2
        with nc.Fori(0, n_loop) as i:
            for u in range(2):
                load_chunk(1 - u, i * 2 + (5 + u))
                chunk(u, CHUNK_TILES, CHUNK_TILES, 2)
            settle(consumers)
        for n in range(2 + 2 * n_loop, N_FULL + 1):
            chunk(n % 2, CHUNK_TILES, CHUNK_TILES, min(N_FULL - n, 2))
        kept0.wait()
        kept1.wait()
        for half in range(2):
            weighted(N_FULL % 2, QUADS - 1, CHUNK_TILES, half)
        keep_out()
        out_kept.wait()
        out_piece()
        add_out()
        piece_from_dve.wait()
        DV.wait_ge(piece_from_dve.sem, piece_from_dve.n)
        DV.wait_ge(piece_from_dve.sem, piece_from_dve.n)
        den = sb("x0_den", [X0_HEADS], stack=st)
        y = sb("x0_y", [X0_HEADS, X0_DV], stack=st)
        t = dv.mark(DV.reciprocal(den[:, :], acc[:, :, X0_DV]))
        wait(DV, t)
        t = dv.mark(DV.tensor_tensor(y[:, :, :], acc[:, :, 0:X0_DV], bc(den[:, :], X0_DV), ALU.mult))
        add_to_x(y[:, :, :].rearrange("p h c -> p (h c)"), [t])
        for b in range(8):
            readers[b] = [last["x"]]

    def join():
        for e in (PE, AC, DV, GP, SP):
            wait(e, *[(d.sem, d.n) for d in (pe, ac, dv, gp) if d.n])

    def softmax_heads(st, s_banks, n_heads, masked, after):
        banks = list(range(s_banks, s_banks + n_heads * P // BANK))
        per = BANK // P
        name = "sm1" if masked else "sm0"
        e = sb(name + "_e", [n_heads, P], stack=st)
        mx, sm = sb(name + "_max", [n_heads], stack=st), sb(name + "_sum", [n_heads], stack=st)
        for n, b in enumerate(banks):
            hs = slice(n * per, (n + 1) * per)
            src = ps[:, b, :].rearrange("p (h c) -> p h c", c=P)
            wait(DV, after[n])
            if masked:
                t = copy_out(e[:, hs, :], src, [b], [after[n]], eng="act")
                wait(GP, t)
                t = gp.mark(GP.affine_select(out=e[:, hs, :], in_=e[:, hs, :], compare_op=ALU.is_ge,
                                             fill=-1e10, base=0, pattern=[[0, per], [-1, P]],
                                             channel_multiplier=1))
                wait(DV, t)
                src = e[:, hs, :]
            t = dv.mark(DV.tensor_reduce(mx[:, hs], src, AX.X, ALU.max))
            wait(DV, t)
            t = dv.mark(DV.tensor_tensor(e[:, hs, :], src, bc(mx[:, hs], P), ALU.subtract))
            read_by(b, t)
            wait(AC, t)
            t = ac.mark(AC.activation(e[:, hs, :], e[:, hs, :], ACT.Exp))
            wait(DV, t)
            t = dv.mark(DV.tensor_reduce(sm[:, hs], e[:, hs, :], AX.X, ALU.add))
            wait(DV, t)
            t = dv.mark(DV.reciprocal(sm[:, hs], sm[:, hs]))
            wait(DV, t)
            t = dv.mark(DV.tensor_tensor(e[:, hs, :], e[:, hs, :], bc(sm[:, hs], P), ALU.mult))
            yield e, t

    join()
    st = ExitStack()
    with st:
        G4 = A0_HEADS // A0_KV
        wq = sb("a0_wq", [DK, D], stack=st)
        wk_ = sb("a0_wk", [D], stack=st)
        wv_ = sb("a0_wv", [D], stack=st)
        wo = sb("a0_wo", [DK, A0_HEADS, 32], stack=st)
        z = sb("a0_wo_raw", [DK, D], stack=st)
        KV = A0_KV * A0_DH
        ld = [load(wq[:, :, :], a["L0_attn_Wq"].rearrange("(k p) n -> p k n", p=P)),
              load(wk_[0:KV, :], a["L0_attn_Wk"]),
              load(wv_[0:KV, :], a["L0_attn_Wv"]),
              load(z[:, :, :], a["L0_attn_Wo"].rearrange("(k p) n -> p k n", p=P))]
        wqT = sb("a0_wqT", [DK, A0_HEADS, 32], stack=st)
        wkT = sb("a0_wkT", [DK, A0_KV, G4, 32], stack=st)
        wvT = sb("a0_wvT", [DK, KV], stack=st)
        woT = sb("a0_woT", [A0_KV, D], stack=st)
        vp = sb("a0_v", [A0_KV, 32], stack=st)
        for buf in (wo, wqT, wkT, vp):
            flat = buf[(slice(None),) * (len(buf.shape))]
            zero = gp.mark(GP.memset(flat, 0.0))
        wait(PE, *ld)
        b = next_bank()
        for k in range(DK):
            for o in range(DK):
                t = PE.transpose(ps[:, b, (k * DK + o) * P:(k * DK + o + 1) * P],
                                 wq[:, o, k * P:(k + 1) * P], ident[:, :])
        t = pe.mark(t)
        wqT_ok = copy_out(wqT[:, :, :, 0:A0_DH], ps[:, b, :].rearrange("p (k h c) -> p k h c", k=DK, c=A0_DH),
                          [b], [t, zero])
        b = next_bank()
        for n, w in enumerate((wk_, wv_)):
            for k in range(DK):
                c = (n * DK + k) * KV
                t = PE.transpose(ps[:, b, c:c + KV], w[0:KV, k * P:(k + 1) * P], ident[0:KV, 0:KV])
        t = pe.mark(t)
        src = ps[:, b, 0:DK * KV].rearrange("p (k g c) -> p k g c", k=DK, c=A0_DH)
        for j in range(G4):
            wkT_ok = copy_out(wkT[:, :, :, j, 0:A0_DH], src, [b], [t, zero], eng="dve")
        wvT_ok = copy_out(wvT[:, :, :], ps[:, b, DK * KV:2 * DK * KV].rearrange("p (k c) -> p k c", k=DK),
                          [b], [t], eng="dve")
        wait(DV, ld[3], zero)
        t = dv.mark(DV.tensor_copy(wo[:, :, :, 0:A0_DH], z[:, :, :].rearrange("p k (h c) -> p k h c", c=A0_DH)))
        wo_flat = wo[:, :, :, :].rearrange("p k h c -> p k (h c)")
        woT_ok = transposed(
            lambda i, n: woT[:, i // DK:(i + n) // DK, :].rearrange("p g (k c) -> p (g k) c", c=P),
            [wo_flat[:, k, g * P:(g + 1) * P] for g in range(A0_KV) for k in range(DK)], [t])

        _, xnT_ok = layer_norm()
        wait(PE, *xnT_ok, wqT_ok, wkT_ok, wvT_ok, *woT_ok)
        qT = sb("a0_qT", [A0_KV, P], stack=st)
        kbd = sb("a0_kbd", [A0_KV, G4, P], stack=st)
        wqT_f = wqT[:, :, :, :].rearrange("p k h c -> p k (h c)")
        wkT_f = wkT[:, :, :, :, :].rearrange("p k g j c -> p k (g j c)")
        bq, bk = next_bank(), next_bank()
        for g in range(A0_KV):
            cols = slice(g * P, (g + 1) * P)
            tq = matmuls(ps[:, bq, cols], [(wqT_f[:, k, cols], xnT[:, k, :]) for k in range(DK)])
            tk = matmuls(ps[:, bk, cols], [(wkT_f[:, k, cols], xnT[:, k, :]) for k in range(DK)])
        bv = next_bank()
        tv = matmuls(ps[:, bv, 0:KV], [(xnT[:, k, :], wvT[:, k, :]) for k in range(DK)])
        q_ok = copy_out(qT[:, :, :], ps[:, bq, :].rearrange("p (g c) -> p g c", c=P), [bq], [tq],
                        mul=float(A0_DH) ** -0.5, eng="act")
        wait(DV, tk)
        for g in range(A0_KV):
            t = dv.mark(DV.tensor_tensor(
                kbd[:, g, :, :], ps[:, bk, g * P:(g + 1) * P].unsqueeze(1).to_broadcast([P, G4, P]),
                bc(mask4[:, :], P), ALU.mult))
        read_by(bk, t)
        kbd_ok = t
        v_ok = copy_out(vp[:, :, 0:A0_DH], ps[:, bv, 0:KV].rearrange("p (g c) -> p g c", c=A0_DH), [bv],
                        [tv, zero], eng="act")
        s0 = next_banks(A0_KV)
        wait(PE, q_ok, kbd_ok, v_ok)
        after = [matmuls(ps[:, s0 + g, :], [(qT[:, g, :], kbd[:, g, :, :])]) for g in range(A0_KV)]
        pT = sb("a0_pT", [A0_HEADS, P], stack=st)
        pT_ok = []
        for g, (e, t) in enumerate(softmax_heads(st, s0, A0_HEADS, False, after)):
            pT_ok += transposed(lambda i, n: pT[:, g * G4:(g + 1) * G4, :],
                                [e[:, g * G4 + j, :] for j in range(G4)], [t])
        b = next_bank()
        for g in range(A0_KV):
            wait(PE, pT_ok[g])
            for j in range(G4):
                t = PE.matmul(ps[32 * j:32 * (j + 1), b, g * P:(g + 1) * P], vp[:, g, :],
                              pT[:, g * G4 + j, :], start=True, stop=True, skip_group_check=True)
        t = pe.mark(t)
        oT = sb("a0_oT", [A0_KV, P], stack=st)
        t = copy_out(oT[:, :, :], ps[:, b, :].rearrange("p (g c) -> p g c", c=P), [b], [t])
        b = next_bank()
        wait(PE, t)
        t = matmuls(ps[:, b, 0:D], [(oT[:, g, :], woT[:, g, :]) for g in range(A0_KV)])
        add_to_x(ps[:, b, 0:D], [t], [b])

    join()
    st = ExitStack()
    with st:
        rows = sb("f_rows", [P], stack=st)
        names = ["L0_ffn_w1_s", "L0_ffn_w2_s", "L0_ffn_h1_s", "L0_ffn_h2_s"]
        ld_s = [load(rows[n * HB:(n + 1) * HB, :], a[s].rearrange("(b c) -> b c", c=P))
                for n, s in enumerate(names)]
        scale = sb("f_scale", [len(names) * HB], stack=st)
        s3 = sb("f_w3_s", [D], stack=st)
        ld_s3 = load(s3[:, :], a["L0_ffn_w3_s"].partition_broadcast(P))
        w1, w2 = sb("f_w1", [HB, D], stack=st), sb("f_w2", [HB, D], stack=st)
        h1, h2 = sb("f_h1", [HB, HID], stack=st), sb("f_h2", [HB, HID], stack=st)
        w3 = sb("f_w3", [DK, HID], stack=st)
        ld_w = [load(w[:, :, :], a[n].rearrange("(b p) i -> p b i", p=P))
                for w, n in ((w1, "L0_ffn_w1_w"), (w2, "L0_ffn_w2_w"), (h1, "L0_ffn_h1_w"),
                             (h2, "L0_ffn_h2_w"), (w3, "L0_ffn_w3_w"))]
        b = next_bank()
        wait(PE, *ld_s)
        ns = len(names) * HB
        t = pe.mark(PE.transpose(ps[:, b, 0:ns], rows[0:ns, :], ident[0:ns, 0:ns]))
        scale_ok = copy_out(scale[:, :], ps[:, b, 0:ns], [b], [t], eng="dve")

        def weight_T(w, name, n_out, n_in, ld):
            wT = sb(name, [n_in, n_out * P], stack=st)
            ok = []
            for k in range(n_in):
                ok += transposed(
                    lambda i, n: wT[:, k, i * P:(i + n) * P].rearrange("p (n c) -> p n c", c=P),
                    [w[:, o, k * P:(k + 1) * P] for o in range(n_out)], [ld])
            return wT, ok

        w1T, w1_ok = weight_T(w1, "f_w1T", HB, DK, ld_w[0])
        w2T, w2_ok = weight_T(w2, "f_w2T", HB, DK, ld_w[1])
        _, xnT_ok = layer_norm()
        hT = [sb(f"f_hT{i}", [HB, P], stack=st) for i in range(2)]
        gate = sb("f_gate", [HB, P], stack=st)
        wait(PE, *xnT_ok, *w1_ok, *w2_ok)
        wait(AC, scale_ok)
        wait(DV, scale_ok)
        h_ok = None
        for half in range(2):
            ba, bb = next_bank(), next_bank()
            for i in range(4):
                o = half * 4 + i
                ta = matmuls(ps[:, ba, i * P:(i + 1) * P],
                             [(w1T[:, k, o * P:(o + 1) * P], xnT[:, k, :]) for k in range(DK)])
                tb = matmuls(ps[:, bb, i * P:(i + 1) * P],
                             [(w2T[:, k, o * P:(o + 1) * P], xnT[:, k, :]) for k in range(DK)])
            for i in range(4):
                o = half * 4 + i
                wait(AC, ta)
                t = ac.mark(AC.activation(gate[:, o, :], ps[:, ba, i * P:(i + 1) * P], ACT.Silu,
                                          scale=scale[:, o:o + 1]))
                wait(DV, t, tb)
                h_ok = dv.mark(DV.scalar_tensor_tensor(
                    out=hT[0][:, o, :], in0=ps[:, bb, i * P:(i + 1) * P],
                    scalar=scale[:, HB + o:HB + o + 1], in1=gate[:, o, :], op0=ALU.mult, op1=ALU.mult))
            read_by(ba, t)
            read_by(bb, h_ok)
        for n, w in enumerate((h1, h2)):
            wT, w_ok = weight_T(w, f"f_h{n + 1}T", HB, HB, ld_w[2 + n])
            wait(PE, h_ok, *w_ok)
            src, dst = hT[n % 2], hT[1 - n % 2]
            for o in range(HB):
                if o % 4 == 0:
                    b = next_bank()
                c = o % 4 * P
                t = matmuls(ps[:, b, c:c + P], [(wT[:, k, o * P:(o + 1) * P], src[:, k, :]) for k in range(HB)])
                if o % 4 == 3:
                    wait(AC, t)
                    for i in range(4):
                        q = o - 3 + i
                        s = (2 + n) * HB + q
                        h_ok = ac.mark(AC.activation(dst[:, q, :], ps[:, b, i * P:(i + 1) * P], ACT.Gelu,
                                                     scale=scale[:, s:s + 1]))
                    read_by(b, h_ok)
        w3T, w3_ok = weight_T(w3, "f_w3T", DK, HB, ld_w[4])
        b = next_bank()
        wait(PE, h_ok, *w3_ok)
        t = matmuls(ps[:, b, 0:D], [(hT[0][:, k, :], w3T[:, k, :]) for k in range(HB)])
        y = sb("f_y", [D], stack=st)
        wait(DV, t, ld_s3)
        t = dv.mark(DV.tensor_tensor(y[:, :], ps[:, b, 0:D], s3[:, :], ALU.mult))
        read_by(b, t)
        add_to_x(y[:, :], [t])

    join()
    shared_w1 = sb("m_shared_w1", [DK, HID], stack=ctx)
    shared_w2 = sb("m_shared_w2", [HB, D], stack=ctx)
    exp_w1 = [sb(f"m_w1_{i}", [DK, HID], stack=ctx) for i in range(E_UNROLL)]
    exp_w2 = [sb(f"m_w2_{i}", [HB, D], stack=ctx) for i in range(E_UNROLL)]
    RING = 6
    W = D + 1
    st = ExitStack()
    with st:
        wsim = sb("x1_wsim", [3, D], stack=st)
        bsim = sb("x1_bsim", [1], stack=st)
        ld_sim = load(wsim[:, :, :], a["L1_xattn_w_sim"].rearrange("(n d) -> n d", n=3).partition_broadcast(P))
        ld_bsim = load(bsim[:, :], a["L1_xattn_b_sim"].partition_broadcast(P))
        ctx_one = [sb(f"ctx_one{i}", [CHUNK_TILES, W], stack=st) for i in range(RING)]
        sem_ctx1 = [Link(sem(f"s1_ctx{i}"), PE, 16) for i in range(RING)]
        ctx1_free = Link(sem("s1_ctx_free"), SP)
        for i in range(RING):
            ones_in = gp.mark(GP.memset(ctx_one[i][:, :, D:W], 1.0))

        def load_ctx1(n, src, nt=CHUNK_TILES):
            sem_ctx1[n % RING].sent_by(SP.dma_start(ctx_one[n % RING][:, 0:nt, 0:D], src))

        load_ctx1(0, ctx_rows[0:TAIL_TILES * P, :].rearrange("(p t) d -> p t d", t=TAIL_TILES), TAIL_TILES)
        for n in range(1, RING):
            load_ctx1(n, full_chunks[n - 1])
        wqv = sb("x1_wqv", [4 * DK, D], stack=st)
        bqv = sb("x1_bqv", [D], stack=st)
        ld_qv = [load(wqv[:, :, :], a["L1_xattn_W_qv"].rearrange("(b p) n -> p b n", p=P)),
                 load(bqv[:, :], a["L1_xattn_b_qv"].partition_broadcast(P))]
        ld_shared = [load(shared_w1[:, :, :], a["L1_ffn_shared_w1"].rearrange("s (k p) n -> p (s k) n", p=P), AC),
                     load(shared_w2[:, :, :], a["L1_ffn_shared_w2"].rearrange("s (b p) n -> p (s b) n", p=P), AC)]
        w1_rows = a["L1_ffn_routed_w1"].rearrange("e (k p) n -> e p k n", p=P)
        w2_rows = a["L1_ffn_routed_w2"].rearrange("e (b p) n -> e p b n", p=P)
        sem_w = [Link(sem(f"s_expert{i}"), PE, 32) for i in range(E_UNROLL)]

        def load_expert(slot, e, eng=SP):
            eng.dma_start(exp_w1[slot][:, :, :], w1_rows[e]).then_inc(sem_w[slot].sem, 16)
            eng.dma_start(exp_w2[slot][:, :, :], w2_rows[e]).then_inc(sem_w[slot].sem, 16)

        for i in range(E_UNROLL):
            load_expert(i, i, AC)

        enc_ok, encT_ok = layer_norm()
        g = sb("x1_g", [D], stack=st)
        scratch = sb("x1_scratch", [D], stack=st)
        const = sb("x1_const", [1], stack=st)
        wait(DV, enc_ok, ld_sim)
        t = dv.mark(DV.tensor_tensor(g[:, :], xn[:, :], wsim[:, 2, :], ALU.mult))
        wait(DV, t)
        g_ok = dv.mark(DV.tensor_tensor(g[:, :], g[:, :], wsim[:, 1, :], ALU.add))
        t = dv.mark(DV.tensor_tensor(scratch[:, :], xn[:, :], wsim[:, 0, :], ALU.mult))
        wait(DV, t)
        t = dv.mark(DV.tensor_reduce(const[:, :], scratch[:, :], AX.X, ALU.add))
        wait(DV, t, ld_bsim)
        const_ok = dv.mark(DV.tensor_tensor(const[:, :], const[:, :], bsim[:, :], ALU.add))
        gT_hi = sb("gT_hi", [DK, P], F32R, st)
        gT_lo = sb("gT_lo", [DK, P], F32R, st)
        b = next_bank()
        wait(PE, g_ok)
        for k in range(DK):
            t = PE.transpose(ps[:, b, k * P:(k + 1) * P], g[:, k * P:(k + 1) * P], ident[:, :])
        t = pe.mark(t)
        src = ps[:, b, 0:D].rearrange("p (k c) -> p k c", c=P)
        wait(AC, t)
        t = ac.mark(AC.copy(gT_hi[:, :, :], src))
        wait(DV, t)
        gT_ok = dv.mark(DV.tensor_tensor(gT_lo[:, :, :], src, gT_hi[:, :, :], ALU.subtract))

        ctxT_hi = [sb(f"c1T_hi{i}", [DK, CHUNK], F32R, st) for i in range(2)]
        ctxT_lo = [sb(f"c1T_lo{i}", [DK, CHUNK], F32R, st) for i in range(2)]
        pr = [sb(f"x1_pr{i}", [CHUNK], stack=st) for i in range(2)]
        prT = [sb(f"x1_prT{i}", [CHUNK], stack=st) for i in range(2)]
        negc = sb("x1_negc", [RING], stack=st)
        negm = sb("x1_negm", [RING], stack=st)
        alpha = sb("x1_alpha", [RING], stack=st)
        acc = sb("x1_acc", [W], stack=st)
        GP.memset(negm[:, :], 3e38)
        init = gp.mark(GP.memset(acc[:, :], 0.0))
        sc_ok = Link(sem("m_sc_ok"), DV)
        mx_ok = Link(sem("m_mx_ok"), AC)
        pr_ok = Link(sem("m_pr_ok"), PE)
        tr_full = Link(sem("m_tr_full"), AC)
        tr_kept = Link(sem("m_tr_kept"), PE)
        x_full = Link(sem("m_x_full"), AC)
        x_hi = Link(sem("m_x_hi"), DV)
        x_kept = Link(sem("m_x_kept"), PE)
        o_full = Link(sem("m_o_full"), DV)
        o_kept = Link(sem("m_o_kept"), PE)
        al_ok = Link(sem("m_al_ok"), DV)
        self_dv = Link(sem("m_self_dv"), DV)
        consumers = {PE: [pr_ok, tr_kept, x_kept, o_kept] + sem_ctx1, AC: [mx_ok, tr_full, x_full],
                     DV: [sc_ok, x_hi, o_full, al_ok, self_dv], SP: [ctx1_free]}
        tiles = lambda n: TAIL_TILES if n == 0 else CHUNK_TILES

        def turn_ctx(n):
            nt, c = tiles(n), ctx_one[n % RING]
            sem_ctx1[n % RING].wait()
            for k in range(DK):
                for i in range(nt):
                    m = PE.transpose(ps[:, 5 + k, i * P:(i + 1) * P], c[:, i, k * P:(k + 1) * P], ident[:, :])
            x_full.sent_by(m)
            x_full.wait()
            src = ps[:, 5:7, 0:nt * P]
            x_hi.sent_by(AC.copy(ctxT_hi[n % 2][:, :, 0:nt * P], src))
            x_hi.wait()
            x_kept.sent_by(DV.tensor_tensor(ctxT_lo[n % 2][:, :, 0:nt * P], src,
                                           ctxT_hi[n % 2][:, :, 0:nt * P], ALU.subtract))

        def score(n):
            nt = tiles(n)
            x_kept.wait()
            terms = [(q[:, k, :], c[n % 2][:, k, 0:nt * P]) for k in range(DK)
                     for q, c in ((gT_hi, ctxT_hi), (gT_hi, ctxT_lo), (gT_lo, ctxT_hi))]
            for i, (l, r) in enumerate(terms):
                m = PE.matmul(ps[:, n % 2, 0:nt * P], l, r, start=(i == 0), stop=(i == len(terms) - 1))
            sc_ok.sent_by(m)
            new, old = n % RING, (n - 1) % RING
            sc_ok.wait()
            self_dv.sent_by(DV.tensor_reduce(negc[:, new:new + 1], ps[:, n % 2, 0:nt * P], AX.X, ALU.max))
            self_dv.wait()
            mx_ok.sent_by(DV.scalar_tensor_tensor(out=negm[:, new:new + 1], in0=negc[:, new:new + 1], scalar=-1.0,
                                                 in1=negm[:, old:old + 1], op0=ALU.mult, op1=ALU.min))

        def probabilities(n):
            nt, new, old = tiles(n), n % RING, (n - 1) % RING
            mx_ok.wait()
            pr_ok.sent_by(AC.activation(pr[n % 2][:, 0:nt * P], ps[:, n % 2, 0:nt * P], ACT.Exp,
                                       bias=negm[:, new:new + 1], scale=1.0))
            al_ok.sent_by(AC.activation(alpha[:, new:new + 1], negm[:, old:old + 1], ACT.Exp,
                                       bias=negm[:, new:new + 1], scale=-1.0))

        def turn_pr(n, free=False):
            nt = tiles(n)
            pr_ok.wait()
            for i in range(nt):
                m = PE.transpose(ps[:, 2, i * P:(i + 1) * P], pr[n % 2][:, i * P:(i + 1) * P], ident[:, :])
                if i == 0 and free:
                    ctx1_free.sent_by(m)
            tr_full.sent_by(m)
            tr_full.wait()
            tr_kept.sent_by(AC.copy(prT[n % 2][:, 0:nt * P], ps[:, 2, 0:nt * P]))

        def sums(n, alone=False):
            nt, new = tiles(n), n % RING
            tr_kept.wait()
            if n > 1:
                o_kept.wait()
            for i in range(nt):
                m = PE.matmul(ps[:, 3 + n % 2, 0:W], prT[n % 2][:, i * P:(i + 1) * P], ctx_one[n % RING][:, i, :],
                              start=(i == 0), stop=(i == nt - 1))
            o_full.sent_by(m)
            al_ok.wait()
            if alone:
                DV.drain()
            o_full.wait()
            o_kept.sent_by(DV.scalar_tensor_tensor(out=acc[:, :], in0=acc[:, :], scalar=alpha[:, new:new + 1],
                                                  in1=ps[:, 3 + n % 2, 0:W], op0=ALU.mult, op1=ALU.add))

        def step(n, last=N_FULL, free=False):
            if n + 1 <= last:
                score(n + 1)
            if n + 2 <= last:
                turn_ctx(n + 2)
            if n + 1 <= last:
                probabilities(n + 1)
            if n >= 1:
                sums(n - 1, alone=n == last)
            turn_pr(n, free)

        wait(PE, gT_ok, ones_in, init)
        wait(DV, init)
        wait(AC, init)
        for b in range(8):
            wait(PE, *readers[b])
        turn_ctx(0)
        score(0)
        turn_ctx(1)
        probabilities(0)
        step(0)
        step(1, free=True)
        ctx1_free.wait()
        load_ctx1(RING, full_chunks[RING - 1])
        settle(consumers)
        n_loop = (N_FULL - RING) // RING
        with nc.Fori(0, n_loop) as i:
            for u in range(RING):
                step(2 + u + RING, last=10 ** 6, free=True)
                ctx1_free.wait()
                load_ctx1(1 + u, full_chunks[RING + u + i * RING])
            settle(consumers)
        for n in range(2 + n_loop * RING, N_FULL + 1):
            step(n)
        sums(N_FULL, alone=True)
        t = dv.mark(DV.drain())
        for b in range(8):
            readers[b] = [t]

        hat = sb("x1_hat", [D], stack=st)
        eh = sb("x1_eh", [D], stack=st)
        eb = sb("x1_eb", [D], stack=st)
        small = sb("x1_small", [8], stack=st)
        row = sb("x1_row", [P], stack=st)
        wait(DV, t)
        t = dv.mark(DV.reciprocal(small[:, 0:1], acc[:, D:W]))
        wait(DV, t)
        hat_ok = dv.mark(DV.tensor_scalar(hat[:, :], acc[:, 0:D], small[:, 0:1], None, ALU.mult))
        wait(DV, hat_ok)
        eh_ok = dv.mark(DV.tensor_tensor(eh[:, :], xn[:, :], hat[:, :], ALU.mult))
        fin = N_FULL % RING
        t = dv.mark(DV.tensor_tensor(small[:, 1:2], const[:, :], negm[:, fin:fin + 1], ALU.subtract))
        b = next_bank()
        wait(PE, t)
        t = pe.mark(PE.transpose(ps[0:1, b, 0:P], small[:, 1:2], ident[:, :]))
        wait(DV, t)
        t = dv.mark(DV.tensor_reduce(row[0:1, 0:1], ps[0:1, b, 0:P], AX.X, ALU.max))
        read_by(b, t)
        b = next_bank()
        wait(PE, t)
        t = matmuls(ps[:, b, 0:1], [(ones[0:1, :], row[0:1, 0:1])])
        wait(DV, t)
        t = dv.mark(DV.tensor_scalar(small[:, 2:3], ps[:, b, 0:1], -1.0, None, ALU.mult))
        read_by(b, t)
        wait(AC, t)
        t = ac.mark(AC.activation(small[:, 3:4], small[:, 1:2], ACT.Exp, bias=small[:, 2:3], scale=1.0))
        wait(DV, t)
        weights = sb("x1_weights", [P], stack=st)
        t = dv.mark(DV.tensor_scalar(weights[:, :], ones[:, :], small[:, 3:4], None, ALU.mult))
        b = next_bank()
        wait(PE, t)
        matmuls(ps[:, b, 0:D], [(weights[:, :], xn[:, :])])
        t = matmuls(ps[:, b, D:W], [(weights[:, :], ones[:, 0:1])])
        wait(DV, t)
        t = dv.mark(DV.reciprocal(small[:, 4:5], ps[:, b, D:W]))
        wait(DV, t)
        t = dv.mark(DV.scalar_tensor_tensor(out=eb[:, :], in0=ps[:, b, 0:D], scalar=small[:, 4:5],
                                            in1=xn[:, :], op0=ALU.mult, op1=ALU.mult))
        read_by(b, t)
        featT = sb("x1_featT", [3 * DK, P], stack=st)
        blocks = [f[:, k * P:(k + 1) * P] for f in (hat, eh, eb) for k in range(DK)]
        f_ok = transposed(lambda i, n: featT[:, i:i + n, :], blocks, [hat_ok, eh_ok, t])
        b = next_bank()
        wait(PE, *f_ok, *encT_ok, *ld_qv)
        t = matmuls(ps[:, b, 0:D], [(xnT[:, k, :], wqv[:, k, :]) for k in range(DK)]
                    + [(featT[:, k, :], wqv[:, DK + k, :]) for k in range(3 * DK)])
        last["xn_free"] = [t]
        y = sb("x1_y", [D], stack=st)
        wait(DV, t, ld_qv[1])
        t = dv.mark(DV.tensor_tensor(y[:, :], ps[:, b, 0:D], bqv[:, :], ALU.add))
        read_by(b, t)
        add_to_x(y[:, :], [t])

    join()
    st = ExitStack()
    with st:
        wn = [sb(f"a1_w{n}", [HB, D], stack=st) for n in "qkv"]
        ld = [load(w[:, :, :], a["L1_attn_" + n].rearrange("n h m -> (n h) m").rearrange("(b p) m -> p b m", p=P))
              for w, n in zip(wn, "QKV")]
        wo = sb("a1_wo", [DK, HID], stack=st)
        ld_o = load(wo[:, :, :], a["L1_attn_O"].rearrange("(k p) n -> p k n", p=P))
        wT, w_ok = [], []
        for n, (w, l) in enumerate(zip(wn, ld)):
            t = sb(f"a1_wT{n}", [DK, HID], stack=st)
            wT.append(t)
            for k in range(DK):
                w_ok += transposed(
                    lambda i, m: t[:, k, i * P:(i + m) * P].rearrange("p (n c) -> p n c", c=P),
                    [w[:, o, k * P:(k + 1) * P] for o in range(HB)], [l])
        woT = sb("a1_woT", [HB, D], stack=st)
        woT_ok = transposed(
            lambda i, n: woT[:, i // DK:(i + n) // DK, :].rearrange("p b (k c) -> p (b k) c", c=P),
            [wo[:, k, b * P:(b + 1) * P] for b in range(HB) for k in range(DK)], [ld_o])
        _, xnT_ok = layer_norm()
        wait(PE, *xnT_ok, *w_ok)
        qT = sb("a1_qT", [HB, P], stack=st)
        kbd = sb("a1_kbd", [HB, 2, P], stack=st)
        v = sb("a1_v", [HID], stack=st)
        q_ok, v_ok = [], []
        for half in range(2):
            bq, bk = next_bank(), next_bank()
            for i in range(4):
                o = half * 4 + i
                cols = slice(o * P, (o + 1) * P)
                tq = matmuls(ps[:, bq, i * P:(i + 1) * P], [(wT[0][:, k, cols], xnT[:, k, :]) for k in range(DK)])
                tk = matmuls(ps[:, bk, i * P:(i + 1) * P], [(wT[1][:, k, cols], xnT[:, k, :]) for k in range(DK)])
            q_ok.append(copy_out(qT[:, half * 4:half * 4 + 4, :],
                                 ps[:, bq, :].rearrange("p (g c) -> p g c", c=P), [bq], [tq], eng="act"))
            wait(DV, tk)
            for j in range(2):
                t = dv.mark(DV.tensor_scalar(kbd[:, half * 4:half * 4 + 4, j, :],
                                             ps[:, bk, :].rearrange("p (g c) -> p g c", c=P),
                                             mask2[:, j:j + 1], None, ALU.mult))
            read_by(bk, t)
            q_ok.append(t)
        s0 = next_banks(4)
        after = []
        wait(PE, *q_ok)
        for o in range(HB):
            t = matmuls(ps[:, s0 + o // 2, o % 2 * 2 * P:(o % 2 + 1) * 2 * P], [(qT[:, o, :], kbd[:, o, :, :])])
            if o % 2:
                after.append(t)
        for half in range(2):
            b = next_bank()
            t = matmuls(ps[:, b, :], [(xnT[:, k, :], wT[2][:, k, half * BANK:(half + 1) * BANK]) for k in range(DK)])
            v_ok.append(copy_out(v[:, half * BANK:(half + 1) * BANK], ps[:, b, :], [b], [t], eng="act"))
        last["xn_free"] = [t]
        pT = sb("a1_pT", [A1_HEADS, P], stack=st)
        pT_ok = []
        for n, (e, t) in enumerate(softmax_heads(st, s0, A1_HEADS, True, after)):
            pT_ok += transposed(lambda i, m: pT[:, n * 4:(n + 1) * 4, :],
                                [e[:, n * 4 + j, :] for j in range(4)], [t])
        zT = sb("a1_zT", [HB, P], stack=st)
        z_ok = []
        wait(PE, *v_ok)
        for half in range(2):
            b = next_bank()
            for o in range(4 * half, 4 * half + 4):
                wait(PE, pT_ok[o // 2])
                for j in range(2):
                    h = 2 * o + j
                    t = PE.matmul(ps[64 * j:64 * (j + 1), b, o % 4 * P:(o % 4 + 1) * P],
                                  v[:, h * A1_DH:(h + 1) * A1_DH], pT[:, h, :], start=True, stop=True,
                                  skip_group_check=True)
            t = pe.mark(t)
            z_ok.append(copy_out(zT[:, 4 * half:4 * half + 4, :],
                                 ps[:, b, :].rearrange("p (g c) -> p g c", c=P), [b], [t]))
        b = next_bank()
        wait(PE, *z_ok, *woT_ok)
        t = matmuls(ps[:, b, 0:D], [(zT[:, o, :], woT[:, o, :]) for o in range(HB)])
        add_to_x(ps[:, b, 0:D], [t], [b])

    join()
    st = ExitStack()
    with st:
        E = N_EXPERTS
        rw = sb("m_router", [DK, E], stack=st)
        eb_ = sb("m_bias", [E], stack=st)
        b1 = sb("m_b1_rows", [P], stack=st)
        sb1 = sb("m_sb1_rows", [P], stack=st)
        b2 = sb("m_b2", [D], stack=st)
        sb2 = sb("m_sb2", [D], stack=st)
        lds = [load(rw[:, :, :], a["L1_ffn_router_w"].rearrange("(k p) n -> p k n", p=P)),
               load(eb_[:, :], a["L1_ffn_expert_bias"].partition_broadcast(P)),
               load(b1[:, :], a["L1_ffn_routed_b1"].rearrange("e (b c) -> (e b) c", c=P)),
               load(sb1[0:HB, :], a["L1_ffn_shared_b1"].rearrange("e (b c) -> (e b) c", c=P)),
               load(b2[0:E, :], a["L1_ffn_routed_b2"]),
               load(sb2[:, :], a["L1_ffn_shared_b2"].rearrange("e d -> (e d)").partition_broadcast(P))]
        b1T = sb("m_b1T", [E, HB], stack=st)
        sb1T = sb("m_sb1T", [HB], stack=st)
        b = next_bank()
        wait(PE, *lds)
        PE.transpose(ps[:, b, 0:P], b1[:, :], ident[:, :])
        t = pe.mark(PE.transpose(ps[:, b, P:P + HB], sb1[0:HB, :], ident[0:HB, 0:HB]))
        b1_ok = copy_out(b1T[:, :, :], ps[:, b, 0:P].rearrange("p (e b) -> p e b", b=HB), [b], [t], eng="dve")
        sb1_ok = copy_out(sb1T[:, :], ps[:, b, P:P + HB], [b], [t], eng="dve")
        _, xnT_ok = layer_norm()
        b = next_bank()
        wait(PE, *xnT_ok)
        t = matmuls(ps[:, b, 0:E], [(xnT[:, k, :], rw[:, k, :]) for k in range(DK)])
        n_t = [0]

        def tmp(n):
            n_t[0] += 1
            return sb(f"m_t{n_t[0]}", [n], stack=st)

        def chain(inst):
            p = dv.mark(inst)
            wait(DV, p)
            return p

        lg = tmp(E)
        wait(DV, t, *lds)
        t = chain(DV.tensor_tensor(lg[:, :], ps[:, b, 0:E], eb_[:, :], ALU.add))
        read_by(b, t)
        tops, hots = [], []
        for n in range(2):
            m, eq, cand, first_, hot = tmp(1), tmp(E), tmp(E), tmp(1), tmp(E)
            chain(DV.tensor_reduce(m[:, :], lg[:, :], AX.X, ALU.max))
            chain(DV.tensor_scalar(eq[:, :], lg[:, :], m[:, 0:1], None, ALU.is_equal))
            chain(DV.scalar_tensor_tensor(out=cand[:, :], in0=eq[:, :], scalar=-99.0, in1=pos99[:, :],
                                          op0=ALU.mult, op1=ALU.add))
            chain(DV.tensor_reduce(first_[:, :], cand[:, :], AX.X, ALU.min))
            chain(DV.tensor_scalar(hot[:, :], pos[:, :], first_[:, 0:1], None, ALU.is_equal))
            tops.append(m)
            hots.append(hot)
            if n == 0:
                rest = tmp(E)
                chain(DV.scalar_tensor_tensor(out=rest[:, :], in0=hot[:, :], scalar=-3e38, in1=lg[:, :],
                                              op0=ALU.mult, op1=ALU.add))
                lg = rest
        d, e2, s, r, w2_ = tmp(1), tmp(1), tmp(1), tmp(1), tmp(1)
        comb, comb1 = tmp(E), tmp(E)
        t = chain(DV.tensor_tensor(d[:, :], tops[1][:, :], tops[0][:, :], ALU.subtract))
        wait(AC, t)
        t = ac.mark(AC.activation(e2[:, :], d[:, :], ACT.Exp))
        wait(DV, t)
        chain(DV.tensor_scalar(s[:, :], e2[:, :], 1.0, None, ALU.add))
        chain(DV.reciprocal(r[:, :], s[:, :]))
        chain(DV.tensor_tensor(w2_[:, :], e2[:, :], r[:, :], ALU.mult))
        chain(DV.tensor_scalar(comb1[:, :], hots[0][:, :], r[:, 0:1], None, ALU.mult))
        t = chain(DV.scalar_tensor_tensor(out=comb[:, :], in0=hots[1][:, :], scalar=w2_[:, 0:1], in1=comb1[:, :],
                                          op0=ALU.mult, op1=ALU.add))
        b = next_bank()
        wait(PE, t)
        t = pe.mark(PE.transpose(ps[0:E, b, 0:P], comb[:, :], ident[:, :]))
        combT = sb("m_combT", [P], stack=st)
        t = copy_out(combT[0:E, :], ps[0:E, b, 0:P], [b], [t], eng="dve")
        b = next_bank()
        wait(PE, t)
        t = matmuls(ps[:, b, 0:D], [(combT[0:E, :], b2[0:E, :])])
        acc = sb("m_acc", [D], stack=st)
        wait(DV, t)
        acc_ok = dv.mark(DV.tensor_tensor(acc[:, :], ps[:, b, 0:D], sb2[:, :], ALU.add))
        read_by(b, acc_ok)

        hid = [sb(f"m_hid{i}", [HB, P], stack=st) for i in range(2)]
        acc1 = sb("m_acc1", [D], stack=st)
        accs = [acc, acc1]
        acc1_ok = gp.mark(GP.memset(acc1[:, :], 0.0))
        h_act = Link(sem("e_h_act"), AC)
        h_dve = Link(sem("e_h_dve"), DV)
        r_act = Link(sem("e_r_act"), PE)
        r_dve = Link(sem("e_r_dve"), PE)
        y_full = Link(sem("e_y_full"), DV)
        y_kept = Link(sem("e_y_kept"), PE)
        w_free = Link(sem("e_w_free"), SP)
        consumers = {PE: [r_act, r_dve, y_kept] + sem_w, AC: [h_act], DV: [h_dve, y_full], SP: [w_free]}

        def up(n, w1, bias, free=False):
            for half, link in enumerate((h_act, h_dve)):
                bank = ps[:, 2 * (n % 2) + half, :]
                for i in range(4):
                    o = half * 4 + i
                    for k in range(DK):
                        m = PE.matmul(bank[:, i * P:(i + 1) * P], w1[:, k, o * P:(o + 1) * P], xnT[:, k, :],
                                      start=(k == 0), stop=(k == DK - 1))
                        if free and o == 0 and k == 0:
                            w_free.sent_by(m)
                link.sent_by(m)
            h_act.wait()
            for i in range(4):
                t = AC.activation(hid[n % 2][:, i, :], ps[:, 2 * (n % 2), i * P:(i + 1) * P], ACT.Relu,
                                  bias=bias(i), scale=1.0)
            r_act.sent_by(t)
            h_dve.wait()
            for i in range(4):
                t = DV.tensor_scalar(hid[n % 2][:, 4 + i, :], ps[:, 2 * (n % 2) + 1, i * P:(i + 1) * P],
                                     bias(4 + i), 0.0, ALU.add, ALU.max)
            r_dve.sent_by(t)

        def down(n, w2, weight):
            r_act.wait()
            r_dve.wait()
            if n > 1:
                y_kept.wait()
            y = ps[:, 4 + n % 2, 0:D]
            for o in range(HB):
                m = PE.matmul(y, hid[n % 2][:, o, :], w2[:, o, :], start=(o == 0), stop=(o == HB - 1))
            y_full.sent_by(m)
            y_full.wait()
            s = accs[n % 2]
            if weight is None:
                t = DV.tensor_tensor(s[:, :], s[:, :], y, ALU.add)
            else:
                t = DV.scalar_tensor_tensor(out=s[:, :], in0=y, scalar=weight, in1=s[:, :],
                                            op0=ALU.mult, op1=ALU.add)
            y_kept.sent_by(t)

        def step(n, e, free):
            slot = n % E_UNROLL
            sem_w[slot].wait()
            up(n + 1, exp_w1[slot], lambda o: bias_rows(e + 1, o), free)
            down(n, exp_w2[(n - 1) % E_UNROLL], comb[:, column(e)])

        column = lambda e: slice(e, e + 1) if isinstance(e, int) else bass.ds(e, 1)
        b1T_flat = b1T[:, :, :].rearrange("p e b -> p (e b)")
        bias_rows = lambda e, o: b1T_flat[:, column(e * HB + o)]

        wait(PE, *ld_shared, *[r for b in range(8) for r in readers[b]])
        wait(DV, acc_ok, acc1_ok, b1_ok, sb1_ok)
        wait(AC, b1_ok, sb1_ok)
        up(0, shared_w1, lambda o: sb1T[:, o:o + 1])
        sem_w[0].wait()
        up(1, exp_w1[0], lambda o: bias_rows(0, o))
        down(0, shared_w2, None)
        step(1, 0, False)
        settle(consumers)
        n_loop = (E - E_UNROLL) // E_UNROLL
        with nc.Fori(0, n_loop) as i:
            for u in range(E_UNROLL):
                step(2 + u, i * E_UNROLL + (1 + u), True)
                w_free.wait()
                load_expert(u, i * E_UNROLL + (E_UNROLL + u))
            settle(consumers)
        for e in range(1 + n_loop * E_UNROLL, E - 1):
            step(e + 1, e, False)
        down(E, exp_w2[(E - 1) % E_UNROLL], comb[:, E - 1:E])
        y = sb("m_y", [D], stack=st)
        DV.drain()
        t = dv.mark(DV.tensor_tensor(y[:, :], acc[:, :], acc1[:, :], ALU.add))
        add_to_x(y[:, :], [t])

    return finish()




INS = ["x", "ctx_1024", "L0_xattn_wq", "L0_xattn_wk", "L0_xattn_wv", "L0_attn_Wq", "L0_attn_Wk",
       "L0_attn_Wv", "L0_attn_Wo", "L0_ffn_w1_w", "L0_ffn_w1_s", "L0_ffn_w2_w", "L0_ffn_w2_s",
       "L0_ffn_h1_w", "L0_ffn_h1_s", "L0_ffn_h2_w", "L0_ffn_h2_s", "L0_ffn_w3_w", "L0_ffn_w3_s",
       "L1_xattn_w_sim", "L1_xattn_b_sim", "L1_xattn_W_qv", "L1_xattn_b_qv", "L1_attn_Q", "L1_attn_K",
       "L1_attn_V", "L1_attn_O", "L1_ffn_router_w", "L1_ffn_expert_bias", "L1_ffn_shared_w1",
       "L1_ffn_shared_b1", "L1_ffn_shared_w2", "L1_ffn_shared_b2", "L1_ffn_routed_w1",
       "L1_ffn_routed_b1", "L1_ffn_routed_w2", "L1_ffn_routed_b2"]


def kernel(**inputs):
    import concourse.bacc as bacc
    from concourse.bass_utils import run_bass_kernel_spmd

    nc = bacc.Bacc("TRN2", target_bir_lowering=False, num_devices=1)
    arrays, args = {}, {}
    for name in INS:
        v = np.ascontiguousarray(inputs[name])
        arrays[f"in_{name}"] = v
        args[name] = nc.dram_tensor(f"in_{name}", v.shape, mybir.dt.from_np(v.dtype), kind="ExternalInput").ap()
    out = nc.dram_tensor("out_0", (1, P, D), F32, kind="ExternalOutput").ap()
    build(nc, args, out)
    return run_bass_kernel_spmd(nc, [arrays], core_ids=[0]).results[0]["out_0"]
```

```python
from contextlib import ExitStack
from itertools import chain

import concourse.bass as bass
from concourse import mybir
import numpy as np

F32 = mybir.dt.float32
F32R = mybir.dt.float32r
ALU = mybir.AluOpType
ACT = mybir.ActivationFunctionType
AX = mybir.AxisListType

P = 128
D = 256
DK = D // P
EPS = 1e-5
BANK = 512

N_KEYS = 12544
TILES = N_KEYS // P
CHUNK_TILES = 4
CHUNK = CHUNK_TILES * P
TAIL_TILES = TILES % CHUNK_TILES
N_FULL = TILES // CHUNK_TILES

X0_HEADS = 16
X0_DK = 64
X0_DV = D // X0_HEADS
PAIRS = X0_HEADS // 2
QUADS = X0_HEADS // 4
PADV = 32

A0_HEADS, A0_KV, A0_DH = 16, 4, 16
HID = 1024
HB = HID // P
A1_HEADS, A1_DH = 16, 64
N_EXPERTS = 16
E_UNROLL = 4
C_UNROLL = 4

GAP_NORM, GAP_SCORES, GAP_GROUPS, GAP_OUTPUT = 2, 3, (4, 5, 5, 5), 6
GAPS_1 = (4, 3, 3, 3, 3)


class Done:

    def __init__(self, sem):
        self.sem, self.n = sem, 0

    def mark(self, inst):
        inst.then_inc(self.sem, 1)
        self.n += 1
        return (self.sem, self.n)


class Link:

    def __init__(self, sem, consumer, step=1):
        self.sem, self.consumer, self.step, self.n = sem, consumer, step, 0

    def sent_by(self, inst):
        inst.then_inc(self.sem, self.step)

    def wait(self):
        self.n += self.step
        self.consumer.wait_ge(self.sem, self.n)

    def settle(self):
        if self.n:
            self.consumer.sem_inc(self.sem, -self.n)
            self.n = 0


def build(nc, a, out):
    ctx = ExitStack()
    PE, AC, DV, GP, SP = nc.tensor, nc.scalar, nc.vector, nc.gpsimd, nc.sync

    def sb(name, shape, dt=F32, stack=ctx):
        return stack.enter_context(nc.sbuf_tensor(name, [P] + list(shape), dt))

    def sem(name):
        return ctx.enter_context(nc.semaphore(name))

    pe, ac, dv, gp = (Done(sem("s_" + n)) for n in ("pe", "act", "dve", "pool"))
    seen = {}

    def wait(eng, *points):
        for s, v in points:
            key = (id(eng), id(s))
            if seen.get(key, 0) < v:
                eng.wait_ge(s, v)
                seen[key] = v

    n_loads = [0]

    def load(dst, src, eng=SP):
        n_loads[0] += 1
        s = sem(f"s_load{n_loads[0]}")
        eng.dma_start(dst, src).then_inc(s, 16)
        return (s, 16)

    def settle(consumers):
        for eng, links in consumers.items():
            if any(l.n for l in links):
                if eng is not SP:
                    eng.drain()
                for l in links:
                    l.settle()

    ps = ctx.enter_context(nc.psum_tensor("ps", [P, 8, BANK], F32))

    ident = sb("ident", [P])
    mask4 = sb("mask4", [4])
    mask2 = sb("mask2", [2])
    ones = sb("ones", [P])
    minus_half = sb("minus_half", [1])
    pos = sb("pos", [N_EXPERTS])
    pos99 = sb("pos99", [N_EXPERTS])
    GP.memset(ident[:, :], 0.0)
    GP.memset(mask4[:, :], 1.0)
    GP.memset(minus_half[:, :], -0.5)
    GP.memset(mask2[:, :], 1.0)
    c0 = gp.mark(GP.memset(ones[:, :], 1.0))
    wait(GP, c0)
    GP.affine_select(out=ident[:, :], in_=ident[:, :], compare_op=ALU.not_equal, fill=1.0,
                     base=0, pattern=[[-1, P]], channel_multiplier=1)
    GP.affine_select(out=mask4[:, :], in_=mask4[:, :], compare_op=ALU.is_ge, fill=0.0,
                     base=0, pattern=[[-32, 4]], channel_multiplier=1)
    c1 = gp.mark(GP.affine_select(out=mask2[:, :], in_=mask2[:, :], compare_op=ALU.is_ge, fill=0.0,
                                  base=0, pattern=[[-64, 2]], channel_multiplier=1))
    wait(GP, c1)
    GP.affine_select(out=mask4[:, :], in_=mask4[:, :], compare_op=ALU.is_ge, fill=0.0,
                     base=31, pattern=[[32, 4]], channel_multiplier=-1)
    GP.affine_select(out=mask2[:, :], in_=mask2[:, :], compare_op=ALU.is_ge, fill=0.0,
                     base=63, pattern=[[64, 2]], channel_multiplier=-1)
    GP.iota(pos[:, :], pattern=[[1, N_EXPERTS]], base=0, channel_multiplier=0,
            allow_small_or_imprecise_dtypes=True)
    consts = gp.mark(GP.iota(pos99[:, :], pattern=[[1, N_EXPERTS]], base=99, channel_multiplier=0,
                             allow_small_or_imprecise_dtypes=True))
    for e in (PE, DV, AC):
        wait(e, consts)

    xbuf = [sb("x_even", [D]), sb("x_odd", [D])]
    xn = sb("xn", [D])
    xnT = sb("xnT", [DK, P])
    stat = sb("stat", [8])
    mv = sb("mv", [2])
    rstd = sb("rstd", [1])
    last = {"x": None, "xn_free": []}
    state = {"x": 0}

    readers = {b: [] for b in range(8)}
    turn = [0]
    busy = set()

    def next_bank():
        while turn[0] % 8 in busy:
            turn[0] += 1
        b = turn[0] % 8
        turn[0] += 1
        wait(PE, *readers[b])
        readers[b] = []
        return b

    def next_banks(n):
        if turn[0] % 8 + n > 8:
            turn[0] += 8 - turn[0] % 8
        return [next_bank() for _ in range(n)][0]

    def read_by(b, point, n=1):
        for i in range(n):
            readers[b + i].append(point)

    flip = [0]

    def copy_out(dst, src, banks, after, mul=None, eng=None):
        flip[0] += 1
        use_act = flip[0] % 2 if eng is None else eng == "act"
        if use_act:
            wait(AC, *after)
            i = AC.copy(dst, src) if mul is None else AC.mul(dst, src, mul)
            p = ac.mark(i)
        else:
            wait(DV, *after)
            i = (DV.tensor_copy(dst, src) if mul is None
                 else DV.tensor_scalar(dst, src, mul, None, ALU.mult))
            p = dv.mark(i)
        for b in banks:
            read_by(b, p)
        return p

    def matmuls(dst, pairs):
        for i, (l, r) in enumerate(pairs):
            m = PE.matmul(dst, l, r, start=(i == 0), stop=(i == len(pairs) - 1))
        return pe.mark(m)

    def transposed(dst, blocks, after, eng=None):
        points = []
        per = BANK // P
        rows = blocks[0].shape[0]
        for i in range(0, len(blocks), per):
            part = blocks[i:i + per]
            b = next_bank()
            wait(PE, *after)
            for j, blk in enumerate(part):
                t = PE.transpose(ps[:, b, j * P:j * P + rows], blk, ident[0:rows, 0:rows])
            t = pe.mark(t)
            points.append(copy_out(dst(i, len(part)),
                                   ps[:, b, 0:len(part) * P].rearrange("p (n c) -> p n c", c=P)[:, :, 0:rows],
                                   [b], [t], eng=eng))
        return points

    def weight_T(ok, wT, w, n_out, n_in, ld, eng=None):
        per = BANK // P
        for k in range(n_in):
            for i in range(0, n_out, per):
                m = min(per, n_out - i)
                ok += transposed(
                    lambda _, n: wT[:, k, i * P:(i + n) * P].rearrange("p (n c) -> p n c", c=P),
                    [w[:, o, k * P:(k + 1) * P] for o in range(i, i + m)], [ld], eng)
                yield

    def beside(work, n=10 ** 6):
        for _ in zip(range(n), work):
            pass

    def layer_norm():
        x = xbuf[state["x"]]
        wait(DV, last["x"])
        s0 = dv.mark(DV.bn_stats(stat[:, 0:6], x[:, :]))
        wait(DV, s0)
        s1 = dv.mark(DV.bn_aggr(mv[:, :], stat[:, 0:6]))
        wait(DV, s1)
        s2 = dv.mark(DV.tensor_scalar(mv[:, 1:2], mv[:, 1:2], EPS, None, ALU.add))
        wait(GP, s2)
        s2 = gp.mark(GP.tensor_tensor(rstd[:, :], mv[:, 1:2], minus_half[:, :], ALU.pow))
        wait(DV, s2, *last["xn_free"])
        s3 = dv.mark(DV.tensor_scalar(xn[:, :], x[:, :], mv[:, 0:1], rstd[:, 0:1], ALU.subtract, ALU.mult))
        tp = transposed(lambda i, n: xnT[:, :, :], [xn[:, k * P:(k + 1) * P] for k in range(DK)], [s3])
        last["xn_free"] = tp
        return s3, tp

    def add_to_x(branch, after, banks=()):
        x, y = xbuf[state["x"]], xbuf[1 - state["x"]]
        wait(DV, *after)
        last["x"] = dv.mark(DV.tensor_tensor(y[:, :], x[:, :], branch, ALU.add))
        for b in banks:
            read_by(b, last["x"])
        state["x"] = 1 - state["x"]

    def bc(ap, n):
        return ap.unsqueeze(ap.ndim).to_broadcast(list(ap.shape) + [n])

    def finish():
        layer0.close()
        wait(SP, last["x"])
        s = sem("s_out")
        SP.dma_start(out.rearrange("b s d -> (b s) d"), xbuf[state["x"]][:, :]).then_inc(s, 16)
        SP.wait_ge(s, 16)
        ctx.close()

    ld_x = load(xbuf[0][:, :], a["x"].rearrange("b s d -> (b s) d"))
    last["x"] = ld_x

    KV = A0_KV * A0_DH
    layer0 = ExitStack()
    a0_wq = sb("a0_wq", [DK, D], stack=layer0)
    a0_wk = sb("a0_wk", [D], stack=layer0)
    a0_wv = sb("a0_wv", [D], stack=layer0)
    a0_wo = sb("a0_wo", [DK, D], stack=layer0)
    f_w1, f_w2 = sb("f_w1", [HB, D], stack=layer0), sb("f_w2", [HB, D], stack=layer0)
    f_w3 = sb("f_w3", [DK, HID], stack=layer0)
    f_h1 = sb("f_h1", [HB, HID], stack=layer0)

    ctx_rows = a["ctx_1024"].rearrange("b s d -> (b s) d")
    st = ExitStack()
    with st:
        wk_hi, wk_lo = (sb(f"wk_{part}", [DK, X0_HEADS * X0_DK], F32R, st) for part in ("hi", "lo"))
        wv_hi, wv_lo = (sb(f"wv_{part}", [DK, D], F32R, st) for part in ("hi", "lo"))
        q_hi = sb("q_hi", [X0_HEADS, P], F32R, st)
        q_lo = sb("q_lo", [X0_HEADS, P], F32R, st)
        top, low = slice(0, X0_DK), slice(X0_DK, P)
        ctx_nat = [sb(f"ctx_nat{i}", [CHUNK_TILES, D], stack=st) for i in range(2)]
        sem_ctx = [Link(sem(f"s_ctx{i}"), PE, 16) for i in range(2)]
        ctx_free = Link(sem("s_ctx_free"), SP)

        def load_ctx(slot, rows, nt):
            sem_ctx[slot].sent_by(SP.dma_start(ctx_nat[slot][:, 0:nt, :],
                                              rows.rearrange("(p t) d -> p t d", t=nt)))

        keys = sb("keys", [X0_HEADS, CHUNK], F32R, st)
        raw = ExitStack()
        wq = sb("x0_wq", [DK, X0_HEADS * X0_DK], stack=raw)
        wk = sb("x0_wk", [DK, X0_HEADS * X0_DK], stack=raw)
        wv = sb("x0_wv", [DK, D], stack=raw)
        raw.close()
        probs = [sb(f"probs{i}", [2, CHUNK], stack=st) for i in range(2)]
        probsT = [sb(f"probsT{i}", [4, CHUNK], stack=st) for i in range(2)]
        tail_rows = TAIL_TILES * P
        full_chunks = ctx_rows[tail_rows:N_KEYS, :].rearrange("(c p t) d -> c p t d", p=P, t=CHUNK_TILES)
        halves = [slice(n * BANK, (n + 1) * BANK) for n in range(2)]
        wk_in, wq_in = (a["L0_xattn_" + n].rearrange("(k p) n -> p k n", p=P) for n in ("wk", "wq"))
        ld_wk = [load(wk[:, :, c], wk_in[:, :, c], AC) for c in halves]
        load_ctx(0, ctx_rows[0:tail_rows, :], TAIL_TILES)
        ld_wq = [load(wq[:, :, c], wq_in[:, :, c]) for c in halves]
        ld_wv = load(wv[:, :, :], a["L0_xattn_wv"].rearrange("(k p) n -> p k n", p=P), AC)
        load_ctx(1, ctx_rows[tail_rows:tail_rows + CHUNK, :], CHUNK_TILES)

        def split(hi, lo, w, cols, ld):
            wait(AC, ld)
            t = ac.mark(AC.copy(hi[:, :, cols], w[:, :, cols]))
            wait(DV, t, ld)
            return dv.mark(DV.tensor_tensor(lo[:, :, cols], w[:, :, cols], hi[:, :, cols], ALU.subtract))

        def queries(half, xnT_ok):
            b = next_bank()
            wait(PE, ld_wq[half], *xnT_ok)
            for i in range(4):
                p = 4 * half + i
                t = matmuls(ps[:, b, i * P:(i + 1) * P],
                            [(wq[:, k, p * P:(p + 1) * P], xnT[:, k, :]) for k in range(DK)])
            wait(AC, t)
            scale, parts = float(X0_DK) ** -0.5, []
            for j, rows in enumerate((top, low)):
                parts.append((rows, ps[rows, b, :].rearrange("p (h c) -> p h c", c=P),
                              slice(8 * half + j, 8 * half + 8, 2)))
            for rows, src, hs in parts:
                for dst in (top, low):
                    t = ac.mark(AC.mul(q_hi[dst, hs, :], src, scale))
            wait(DV, t)
            for rows, src, hs in parts:
                for dst in (top, low):
                    t = dv.mark(DV.scalar_tensor_tensor(out=q_lo[dst, hs, :], in0=src, scalar=scale,
                                                        in1=q_hi[rows, hs, :], op0=ALU.mult, op1=ALU.subtract))
            read_by(b, t)
            return t

        ctxT_hi = [sb(f"ctxT_hi{i}", [DK, CHUNK], F32R, st) for i in range(2)]
        ctxT_lo = [sb(f"ctxT_lo{i}", [DK, CHUNK], F32R, st) for i in range(2)]
        vals = [sb(f"vals{i}", [CHUNK_TILES, X0_HEADS, PADV], stack=st) for i in range(2)]
        outT = sb("outT", [QUADS, P], stack=st)
        negm = [sb(f"negm{i}", [X0_HEADS], stack=st) for i in range(2)]
        negc = sb("negc", [X0_HEADS], stack=st)
        dm = sb("dm", [X0_HEADS], stack=st)
        alpha = sb("alpha", [X0_HEADS], stack=st)
        VW = X0_DV + 1
        acc = sb("acc", [X0_HEADS, VW], stack=st)
        den = sb("x0_den", [X0_HEADS], stack=st)
        y = sb("x0_y", [X0_HEADS, X0_DV], stack=st)
        GP.memset(negm[1][:, :], 3e38)
        GP.memset(acc[:, :, :], 0.0)
        GP.memset(vals[0][:, :, :, X0_DV:PADV], 1.0)
        init = gp.mark(GP.memset(vals[1][:, :, :, X0_DV:PADV], 1.0))

        to_max = Link(sem("l_to_max"), DV)
        to_exp = Link(sem("l_to_exp"), AC)
        to_turn = Link(sem("l_to_turn"), PE)
        turned0 = Link(sem("l_turned0"), AC)
        turned1 = Link(sem("l_turned1"), DV)
        kept0 = Link(sem("l_kept0"), PE)
        kept1 = Link(sem("l_kept1"), PE)
        piece_to_act = Link(sem("l_piece_to_act"), AC)
        piece_to_dve = Link(sem("l_piece_to_dve"), DV)
        hi_kept = Link(sem("l_hi_kept"), DV)
        piece_from_act = Link(sem("l_piece_from_act"), PE)
        piece_from_dve = Link(sem("l_piece_from_dve"), PE)
        k_full = Link(sem("l_k_full"), AC)
        k_kept = Link(sem("l_k_kept"), PE)
        out_full = Link(sem("l_out_full"), AC)
        out_kept = Link(sem("l_out_kept"), PE)
        alpha_ok = Link(sem("l_alpha_ok"), DV)
        self_dv = Link(sem("l_self_dv"), DV)

        S = lambda i: ps[:, 2 * i:2 * i + 2, :]
        T0, T1, K, O = (ps[:, b, :] for b in (4, 5, 6, 7))
        consumers = {
            PE: [to_turn, kept0, kept1, piece_from_act, piece_from_dve, k_kept, out_kept] + sem_ctx,
            AC: [to_exp, turned0, piece_to_act, k_full, out_full],
            DV: [to_max, turned1, piece_to_dve, hi_kept, alpha_ok, self_dv],
            SP: [ctx_free],
        }

        def k_products(slot, p, nt, K=K, free=False, wait_kept=True):
            cols = slice(0, nt * P)
            terms = [(w[:, k, p * P:(p + 1) * P], c[slot][:, k, cols]) for k in range(DK)
                     for w, c in ((wk_hi, ctxT_hi), (wk_hi, ctxT_lo), (wk_lo, ctxT_hi))]
            if wait_kept:
                k_kept.wait()
            for n, (l, r) in enumerate(terms):
                m = PE.matmul(K[:, cols], l, r, start=(n == 0), stop=(n == len(terms) - 1))
                if free and n == 0:
                    ctx_free.sent_by(m)
            k_full.sent_by(m)

        def k_high(p, nt, K=K):
            cols = slice(0, nt * P)
            k_full.wait()
            for j, half in enumerate((top, low)):
                hi_kept.sent_by(AC.copy(keys[half, 2 * p + j, cols], K[half, cols]))

        def k_low(p, nt, K=K):
            cols = slice(0, nt * P)
            for j, (half, other) in enumerate(((top, low), (low, top))):
                hi_kept.wait()
                m = DV.tensor_tensor(keys[other, 2 * p + j, cols], K[half, cols],
                                     keys[half, 2 * p + j, cols], ALU.subtract)
            k_kept.sent_by(m)

        def x_piece(slot, k, nt):
            if k == 0:
                sem_ctx[slot].wait()
            for t in range(nt):
                m = PE.transpose(T0[:, t * P:(t + 1) * P], ctx_nat[slot][:, t, k * P:(k + 1) * P], ident[:, :])
            piece_to_act.sent_by(m)

        def x_high(slot, k, nt):
            piece_to_act.wait()
            hi_kept.sent_by(AC.copy(ctxT_hi[slot][:, k, 0:nt * P], T0[:, 0:nt * P]))

        def x_low(slot, k, nt):
            hi_kept.wait()
            piece_from_dve.sent_by(DV.tensor_tensor(ctxT_lo[slot][:, k, 0:nt * P], T0[:, 0:nt * P],
                                                   ctxT_hi[slot][:, k, 0:nt * P], ALU.subtract))

        def v_piece(slot, t):
            cols = slice(t * P, (t + 1) * P)
            terms = [(l[slot][:, k, cols], r[:, k, :]) for k in range(DK)
                     for l, r in ((ctxT_hi, wv_hi), (ctxT_hi, wv_lo), (ctxT_lo, wv_hi))]
            for n, (l, r) in enumerate(terms):
                m = PE.matmul(T0[:, 0:D], l, r, start=(n == 0), stop=(n == len(terms) - 1))
            piece_to_act.sent_by(m)

        def keep_v(slot, t):
            piece_to_act.wait()
            piece_from_act.sent_by(AC.copy(vals[slot][:, t, :, 0:X0_DV],
                                      T0[:, 0:D].rearrange("p (h c) -> p h c", h=X0_HEADS)))

        def scores(slot, p, nt):
            for j in range(2):
                h = 2 * p + j
                for n, q in enumerate((q_hi, q_lo)):
                    m = PE.matmul(S(p % 2)[:, j, 0:nt * P], q[:, h, :], keys[:, h, 0:nt * P],
                                  start=(n == 0), stop=(n == 1))
            to_max.sent_by(m)

        def maxima(slot, p, nt):
            to_max.wait()
            self_dv.sent_by(DV.tensor_reduce(negc[:, 2 * p:2 * p + 2], S(p % 2)[:, :, 0:nt * P], AX.X, ALU.max))
            self_dv.wait()
            new = DV.scalar_tensor_tensor(
                out=negm[slot][:, 2 * p:2 * p + 2], in0=negc[:, 2 * p:2 * p + 2], scalar=-1.0,
                in1=negm[1 - slot][:, 2 * p:2 * p + 2], op0=ALU.mult, op1=ALU.min)
            if p == PAIRS - 1:
                self_dv.sent_by(new)
                self_dv.wait()
                new = DV.tensor_tensor(dm[:, :], negm[slot][:, :], negm[1 - slot][:, :], ALU.subtract)
            to_exp.sent_by(new)

        def exps(slot, p, nt):
            to_exp.wait()
            for j in range(2):
                i = AC.activation(probs[p % 2][:, j, 0:nt * P], S(p % 2)[:, j, 0:nt * P], ACT.Exp,
                                  bias=negm[slot][:, 2 * p + j:2 * p + j + 1], scale=1.0)
            to_turn.sent_by(i)
            if p == PAIRS - 1:
                alpha_ok.sent_by(AC.activation(alpha[:, :], dm[:, :], ACT.Exp))

        def turn_probs(p, nt, piece_kept):
            to_turn.wait()
            for j, bank, link in ((1, T1, turned1), (0, T0, turned0)):
                if j == 0 and piece_kept:
                    piece_kept.wait()
                for t in range(nt):
                    m = PE.transpose(bank[:, t * P:(t + 1) * P], probs[p % 2][:, j, t * P:(t + 1) * P],
                                     ident[:, :])
                link.sent_by(m)

        def keep_turned0(p, nt):
            dst = probsT[p // 2 % 2]
            turned0.wait()
            kept0.sent_by(AC.copy(dst[:, 2 * (p % 2), 0:nt * P], T0[:, 0:nt * P]))

        def keep_turned1(p, nt):
            dst = probsT[p // 2 % 2]
            turned1.wait()
            kept1.sent_by(DV.tensor_copy(dst[:, 2 * (p % 2) + 1, 0:nt * P], T1[:, 0:nt * P]))

        def weighted(slot, q, nt, half):
            for t in range(half * nt // 2, (half + 1) * nt // 2):
                for j in range(4):
                    m = PE.matmul(O[PADV * j:PADV * (j + 1), q * P:(q + 1) * P], vals[slot][:, t, 4 * q + j, :],
                                  probsT[q % 2][:, j, t * P:(t + 1) * P], start=(t == 0), stop=(t == nt - 1),
                                  skip_group_check=True)
            if q == QUADS - 1 and half:
                out_full.sent_by(m)

        def keep_out():
            out_full.wait()
            out_kept.sent_by(AC.copy(outT[:, :, :], O.rearrange("p (q c) -> p q c", c=P)))

        def out_piece():
            for q in range(QUADS):
                m = PE.transpose(T0[:, q * P:(q + 1) * P], outT[:, q, :], ident[:, :])
            piece_to_dve.sent_by(m)

        def add_out():
            alpha_ok.wait()
            self_dv.sent_by(DV.tensor_tensor(acc[:, :, :], acc[:, :, :], bc(alpha[:, :], VW), ALU.mult))
            piece_to_dve.wait()
            self_dv.wait()
            piece_from_dve.sent_by(DV.tensor_tensor(
                acc[:, :, :], acc[:, :, :], T0.rearrange("p (h c) -> p h c", c=PADV)[:, :, 0:VW], ALU.add))

        X_STEPS, OUT_STEP, V_STEPS = (0, 3), 4, (1, 2, 5, 6)

        def chunk(slot, nt, prev_nt, ahead):
            for p in range(PAIRS):
                if p < PAIRS - 1:
                    pair = (slot, p + 1, nt)
                else:
                    pair = (1 - slot, 0, CHUNK_TILES) if ahead else None
                x = X_STEPS.index(p) if ahead > 1 and p in X_STEPS else None
                v = V_STEPS.index(p) if ahead and p in V_STEPS else None
                out_here = prev_nt and p == OUT_STEP
                turned_before = prev_nt or p
                if pair:
                    scores(*pair)
                if turned_before:
                    kept0.wait()
                piece_kept = None
                if x is not None:
                    x_piece(slot, x, CHUNK_TILES)
                    piece_kept = piece_from_dve
                if out_here:
                    out_piece()
                    piece_kept = piece_from_dve
                if ahead:
                    k_products(1 - slot, p, CHUNK_TILES, free=ahead > 1 and p == X_STEPS[-1] + 1)
                elif p == 0:
                    k_kept.wait()
                if v is not None:
                    v_piece(1 - slot, v)
                    piece_kept = piece_from_act
                if turned_before:
                    kept1.wait()
                if p >= 2:
                    if prev_nt and p == 2:
                        out_kept.wait()
                    weighted(slot, p // 2 - 1, nt, p % 2)
                elif prev_nt:
                    weighted(1 - slot, QUADS - 1, prev_nt, p)
                turn_probs(p, nt, piece_kept)
                if x is not None:
                    x_high(slot, x, CHUNK_TILES)
                if ahead:
                    k_high(p, CHUNK_TILES)
                if v is not None:
                    keep_v(1 - slot, v)
                keep_turned0(p, nt)
                if pair:
                    exps(*pair)
                if prev_nt and p == 1:
                    keep_out()
                if pair:
                    maxima(*pair)
                if x is not None:
                    x_low(slot, x, CHUNK_TILES)
                if out_here:
                    add_out()
                if ahead:
                    k_low(p, CHUNK_TILES)
                keep_turned1(p, nt)

        def load_chunk(slot, n):
            ctx_free.wait()
            sem_ctx[slot].sent_by(SP.dma_start(ctx_nat[slot][:, :, :], full_chunks[n - 1]))

        key_banks = (K, O, T1)

        def first_keys(pairs):
            for p in pairs:
                bank = key_banks[p % len(key_banks)]
                k_products(0, p, TAIL_TILES, bank, wait_kept=p >= len(key_banks), free=p in (0, 6))
                k_high(p, TAIL_TILES, bank)
                k_low(p, TAIL_TILES, bank)

        def turn_block(slot, k, nt):
            x_piece(slot, k, nt)
            x_high(slot, k, nt)
            x_low(slot, k, nt)

        for k in range(DK):
            turn_block(0, k, TAIL_TILES)
            piece_from_dve.wait()
        wk_ok = split(wk_hi, wk_lo, wk, halves[0], ld_wk[0])
        _, xnT_ok = layer_norm()
        wait(PE, wk_ok)
        first_keys((0, 1))
        wk_ok = split(wk_hi, wk_lo, wk, halves[1], ld_wk[1])
        queries(0, xnT_ok)
        first_keys((2, 3))
        wait(PE, wk_ok)
        wv_ok = split(wv_hi, wv_lo, wv, slice(0, D), ld_wv)
        turn_block(1, 0, CHUNK_TILES)
        first_keys((4, 5))
        wait(PE, wv_ok)
        wait(AC, init)
        wait(DV, init)
        piece_from_dve.wait()
        v_piece(0, 0)
        keep_v(0, 0)
        q_ok = queries(1, xnT_ok)
        last["xn_free"] = last["xn_free"] + [q_ok]
        piece_from_act.wait()
        turn_block(1, 1, CHUNK_TILES)
        first_keys((6, 7))
        piece_from_dve.wait()
        v_piece(0, 1)
        keep_v(0, 1)
        for _ in key_banks[1:]:
            k_kept.wait()
        wait(PE, q_ok, init, *[r for b in range(8) for r in readers[b]])
        scores(0, 0, TAIL_TILES)
        maxima(0, 0, TAIL_TILES)
        piece_from_act.wait()
        exps(0, 0, TAIL_TILES)
        load_chunk(0, 2)
        load_chunk(1, 3)
        chunk(0, TAIL_TILES, 0, 2)
        load_chunk(0, 4)
        ld_a0 = [load(a0_wq[:, :, :], a["L0_attn_Wq"].rearrange("(k p) n -> p k n", p=P)),
                 load(a0_wk[0:KV, :], a["L0_attn_Wk"]),
                 load(a0_wv[0:KV, :], a["L0_attn_Wv"]),
                 load(a0_wo[:, :, :], a["L0_attn_Wo"].rearrange("(k p) n -> p k n", p=P))]
        ld_w1, ld_w2, ld_w3, ld_h1 = [
            load(w[:, :, :], a[n].rearrange("(b p) i -> p b i", p=P))
            for w, n in ((f_w1, "L0_ffn_w1_w"), (f_w2, "L0_ffn_w2_w"), (f_w3, "L0_ffn_w3_w"), (f_h1, "L0_ffn_h1_w"))]
        chunk(1, CHUNK_TILES, TAIL_TILES, 2)
        settle(consumers)
        n_loop = (N_FULL - 4) // C_UNROLL
        with nc.Fori(0, n_loop) as i:
            for u in range(C_UNROLL):
                load_chunk((1 + u) % 2, i * C_UNROLL + (5 + u))
                chunk(u % 2, CHUNK_TILES, CHUNK_TILES, 2)
            settle(consumers)
        for n in range(2 + C_UNROLL * n_loop, N_FULL + 1):
            chunk(n % 2, CHUNK_TILES, CHUNK_TILES, min(N_FULL - n, 2))
        kept0.wait()
        kept1.wait()
        for half in range(2):
            weighted(N_FULL % 2, QUADS - 1, CHUNK_TILES, half)
        keep_out()
        phase1_read = pe.mark(PE.transpose(K[:, 0:P], ident[:, :], ident[:, :]))

    def join():
        for e in (PE, AC, DV, GP, SP):
            wait(e, *[(d.sem, d.n) for d in (pe, ac, dv, gp) if d.n])

    def softmax_heads(st, s_banks, n_heads, masked, after):
        banks = list(range(s_banks, s_banks + n_heads * P // BANK))
        per = BANK // P
        name = "sm1" if masked else "sm0"
        e = sb(name + "_e", [n_heads, P], stack=st)
        mx, sm = sb(name + "_max", [n_heads], stack=st), sb(name + "_sum", [n_heads], stack=st)

        def exps(n):
            b = banks[n]
            hs = slice(n * per, (n + 1) * per)
            src = ps[:, b, :].rearrange("p (h c) -> p h c", c=P)
            wait(DV, after[n])
            if masked:
                wait(DV, in_mask[n])
                src = e[:, hs, :]
            t = dv.mark(DV.tensor_reduce(mx[:, hs], src, AX.X, ALU.max))
            wait(DV, t)
            t = dv.mark(DV.tensor_tensor(e[:, hs, :], src, bc(mx[:, hs], P), ALU.subtract))
            read_by(b, t)
            wait(AC, t)
            return ac.mark(AC.activation(e[:, hs, :], e[:, hs, :], ACT.Exp))

        in_mask = []
        for n, b in enumerate(banks if masked else []):
            hs = slice(n * per, (n + 1) * per)
            t = copy_out(e[:, hs, :], ps[:, b, :].rearrange("p (h c) -> p h c", c=P), [b], [after[n]], eng="act")
            wait(GP, t)
            in_mask.append(gp.mark(GP.affine_select(
                out=e[:, hs, :], in_=e[:, hs, :], compare_op=ALU.is_ge, fill=-1e10, base=0,
                pattern=[[0, per], [-1, P]], channel_multiplier=1)))
        points = [exps(0)]
        for n in range(len(banks)):
            if n + 1 < len(banks):
                points.append(exps(n + 1))
            hs = slice(n * per, (n + 1) * per)
            wait(DV, points[n])
            t = dv.mark(DV.tensor_reduce(sm[:, hs], e[:, hs, :], AX.X, ALU.add))
            wait(DV, t)
            t = dv.mark(DV.reciprocal(sm[:, hs], sm[:, hs]))
            wait(DV, t)
            t = dv.mark(DV.tensor_tensor(e[:, hs, :], e[:, hs, :], bc(sm[:, hs], P), ALU.mult))
            yield e, t

    G4 = A0_HEADS // A0_KV
    wo = sb("a0_wo_padded", [DK, A0_HEADS, 32], stack=layer0)
    wqT = sb("a0_wqT", [DK, A0_HEADS, 32], stack=layer0)
    wkT = sb("a0_wkT", [DK, A0_KV, G4, 32], stack=layer0)
    wvT = sb("a0_wvT", [DK, KV], stack=layer0)
    woT = sb("a0_woT", [A0_KV, D], stack=layer0)
    vp = sb("a0_v", [A0_KV, 32], stack=layer0)
    w1T, w2T = sb("f_w1T", [DK, HID], stack=layer0), sb("f_w2T", [DK, HID], stack=layer0)
    w3T = sb("f_w3T", [HB, D], stack=layer0)
    h1T = sb("f_h1T", [HB, HID], stack=layer0)
    f_h2 = sb("f_h2", [HB, HID], stack=layer0)
    hT = [sb(f"f_hT{i}", [HB, P], stack=layer0) for i in range(2)]
    scale_rows = sb("f_scale_rows", [P], stack=layer0)
    scale_names = ["L0_ffn_w1_s", "L0_ffn_w2_s", "L0_ffn_h1_s", "L0_ffn_h2_s"]
    scale = sb("f_scale", [len(scale_names) * HB], stack=layer0)
    s3 = sb("f_w3_s", [D], stack=layer0)

    busy.update((4, 7))
    for b in range(8):
        readers[b] = []
    wait(GP, phase1_read)
    wait(AC, phase1_read)
    for buf in (wo, wqT, wkT, vp):
        flat = buf[(slice(None),) * (len(buf.shape))]
        zero = gp.mark(GP.memset(flat, 0.0))
    wait(AC, ld_a0[3], zero)
    wo_ok = ac.mark(AC.copy(wo[:, :, :, 0:A0_DH], a0_wo[:, :, :].rearrange("p k (h c) -> p k h c", c=A0_DH)))
    out_kept.wait()
    out_piece()
    add_out()
    piece_from_dve.wait()
    DV.wait_ge(piece_from_dve.sem, piece_from_dve.n)
    t = dv.mark(DV.reciprocal(den[:, :], acc[:, :, X0_DV]))
    wait(DV, t)
    t = dv.mark(DV.tensor_tensor(y[:, :, :], acc[:, :, 0:X0_DV], bc(den[:, :], X0_DV), ALU.mult))
    add_to_x(y[:, :, :].rearrange("p h c -> p (h c)"), [t])
    wait(PE, *ld_a0)
    b = next_bank()
    for k in range(DK):
        for o in range(DK):
            t = PE.transpose(ps[:, b, (k * DK + o) * P:(k * DK + o + 1) * P],
                             a0_wq[:, o, k * P:(k + 1) * P], ident[:, :])
    t = pe.mark(t)
    wqT_ok = copy_out(wqT[:, :, :, 0:A0_DH], ps[:, b, :].rearrange("p (k h c) -> p k h c", k=DK, c=A0_DH),
                      [b], [t, zero], eng="act")
    b = next_bank()
    for n, w in enumerate((a0_wk, a0_wv)):
        for k in range(DK):
            c = (n * DK + k) * KV
            t = PE.transpose(ps[:, b, c:c + KV], w[0:KV, k * P:(k + 1) * P], ident[0:KV, 0:KV])
    t = pe.mark(t)
    src = ps[:, b, 0:DK * KV].rearrange("p (k g c) -> p k g c", k=DK, c=A0_DH)
    for j in range(G4):
        wkT_ok = copy_out(wkT[:, :, :, j, 0:A0_DH], src, [b], [t, zero], eng="act")
    wvT_ok = copy_out(wvT[:, :, :], ps[:, b, DK * KV:2 * DK * KV].rearrange("p (k c) -> p k c", k=DK),
                      [b], [t], eng="act")
    w1_ok, w2_ok, h1_ok, w3_ok, h2_ok = [], [], [], [], []
    sem_h2 = sem("s_load_h2")
    h2T = f_h1
    ffn_weights = chain(
        weight_T(w1_ok, w1T, f_w1, HB, DK, ld_w1, "act"), weight_T(w2_ok, w2T, f_w2, HB, DK, ld_w2, "act"),
        weight_T(h1_ok, h1T, f_h1, HB, HB, ld_h1, "act"), weight_T(w3_ok, w3T, f_w3, DK, HB, ld_w3, "act"),
        weight_T(h2_ok, h2T, f_h2, HB, HB, (sem_h2, 16)))
    wo_flat = wo[:, :, :, :].rearrange("p k h c -> p k (h c)")
    beside(ffn_weights, GAP_NORM)
    _, xnT_ok = layer_norm()
    busy.clear()
    woT_ok = transposed(
        lambda i, n: woT[:, i // DK:(i + n) // DK, :].rearrange("p g (k c) -> p (g k) c", c=P),
        [wo_flat[:, k, g * P:(g + 1) * P] for g in range(A0_KV) for k in range(DK)], [wo_ok], "act")
    wait(SP, last["x"])
    SP.dma_start(f_h2[:, :, :], a["L0_ffn_h2_w"].rearrange("(b p) i -> p b i", p=P)).then_inc(sem_h2, 16)
    ld_scales = [load(scale_rows[n * HB:(n + 1) * HB, :], a[name].rearrange("(b c) -> b c", c=P))
                 for n, name in enumerate(scale_names)]
    ld_s3 = load(s3[:, :], a["L0_ffn_w3_s"].partition_broadcast(P))
    st = ExitStack()
    with st:
        wait(PE, *xnT_ok, wqT_ok, wkT_ok, wvT_ok, *woT_ok)
        qT = sb("a0_qT", [A0_KV, P], stack=st)
        kbd = sb("a0_kbd", [A0_KV, G4, P], stack=st)
        wqT_f = wqT[:, :, :, :].rearrange("p k h c -> p k (h c)")
        wkT_f = wkT[:, :, :, :, :].rearrange("p k g j c -> p k (g j c)")
        bq, bk = next_bank(), next_bank()
        for g in range(A0_KV):
            cols = slice(g * P, (g + 1) * P)
            tq = matmuls(ps[:, bq, cols], [(wqT_f[:, k, cols], xnT[:, k, :]) for k in range(DK)])
            tk = matmuls(ps[:, bk, cols], [(wkT_f[:, k, cols], xnT[:, k, :]) for k in range(DK)])
        bv = next_bank()
        tv = matmuls(ps[:, bv, 0:KV], [(xnT[:, k, :], wvT[:, k, :]) for k in range(DK)])
        q_ok = copy_out(qT[:, :, :], ps[:, bq, :].rearrange("p (g c) -> p g c", c=P), [bq], [tq],
                        mul=float(A0_DH) ** -0.5, eng="act")
        wait(DV, tk)
        kbd_ok = []
        for g in range(A0_KV):
            t = dv.mark(DV.tensor_tensor(
                kbd[:, g, :, :], ps[:, bk, g * P:(g + 1) * P].unsqueeze(1).to_broadcast([P, G4, P]),
                bc(mask4[:, :], P), ALU.mult))
            kbd_ok.append(t)
        read_by(bk, t)
        v_ok = copy_out(vp[:, :, 0:A0_DH], ps[:, bv, 0:KV].rearrange("p (g c) -> p g c", c=A0_DH), [bv],
                        [tv, zero], eng="act")
        beside(ffn_weights, GAP_SCORES)
        s0 = next_banks(A0_KV)
        after = []
        for g in range(A0_KV):
            wait(PE, q_ok, kbd_ok[g])
            after.append(matmuls(ps[:, s0 + g, :], [(qT[:, g, :], kbd[:, g, :, :])]))
        wait(PE, v_ok)
        pT = kbd[:, :, :, :].rearrange("p g j c -> p (g j) c")
        pT_ok = []
        busy.update(range(s0, s0 + A0_KV))
        for g, (e, t) in enumerate(softmax_heads(st, s0, A0_HEADS, False, after)):
            beside(ffn_weights, GAP_GROUPS[g])
            pT_ok += transposed(lambda i, n: pT[:, g * G4:(g + 1) * G4, :],
                                [e[:, g * G4 + j, :] for j in range(G4)], [t])
        busy.clear()
        b = next_bank()
        for g in range(A0_KV):
            wait(PE, pT_ok[g])
            for j in range(G4):
                t = PE.matmul(ps[32 * j:32 * (j + 1), b, g * P:(g + 1) * P], vp[:, g, :],
                              pT[:, g * G4 + j, :], start=True, stop=True, skip_group_check=True)
        t = pe.mark(t)
        oT = sb("a0_oT", [A0_KV, P], stack=st)
        t = copy_out(oT[:, :, :], ps[:, b, :].rearrange("p (g c) -> p g c", c=P), [b], [t])
        b = next_bank()
        wait(PE, t)
        t = matmuls(ps[:, b, 0:D], [(oT[:, g, :], woT[:, g, :]) for g in range(A0_KV)])
        add_to_x(ps[:, b, 0:D], [t], [b])

    st = layer0
    with st:
        b = next_bank()
        wait(PE, *ld_scales)
        ns = len(scale_names) * HB
        t = pe.mark(PE.transpose(ps[:, b, 0:ns], scale_rows[0:ns, :], ident[0:ns, 0:ns]))
        scale_ok = copy_out(scale[:, :], ps[:, b, 0:ns], [b], [t], eng="act")
        beside(ffn_weights, GAP_OUTPUT)
        _, xnT_ok = layer_norm()
        gate = hT[1]
        wait(PE, *xnT_ok, *w1_ok, *w2_ok)
        wait(AC, scale_ok)
        wait(DV, scale_ok)
        h_ok = None
        for half in range(2):
            ba, bb = next_bank(), next_bank()
            for i in range(4):
                o = half * 4 + i
                ta = matmuls(ps[:, ba, i * P:(i + 1) * P],
                             [(w1T[:, k, o * P:(o + 1) * P], xnT[:, k, :]) for k in range(DK)])
                tb = matmuls(ps[:, bb, i * P:(i + 1) * P],
                             [(w2T[:, k, o * P:(o + 1) * P], xnT[:, k, :]) for k in range(DK)])
            for i in range(4):
                o = half * 4 + i
                wait(AC, ta)
                t = ac.mark(AC.activation(gate[:, o, :], ps[:, ba, i * P:(i + 1) * P], ACT.Silu,
                                          scale=scale[:, o:o + 1]))
                wait(DV, t, tb)
                h_ok = dv.mark(DV.scalar_tensor_tensor(
                    out=hT[0][:, o, :], in0=ps[:, bb, i * P:(i + 1) * P],
                    scalar=scale[:, HB + o:HB + o + 1], in1=gate[:, o, :], op0=ALU.mult, op1=ALU.mult))
            read_by(ba, t)
            read_by(bb, h_ok)
        beside(ffn_weights, 5)
        for n, (wT, w_ok) in enumerate(((h1T, h1_ok), (h2T, h2_ok))):
            if n == 1:
                beside(ffn_weights)
            wait(PE, h_ok, *w_ok)
            src, dst = hT[n % 2], hT[1 - n % 2]
            for o in range(HB):
                if o % 4 == 0:
                    b = next_bank()
                c = o % 4 * P
                t = matmuls(ps[:, b, c:c + P], [(wT[:, k, o * P:(o + 1) * P], src[:, k, :]) for k in range(HB)])
                if n == 0:
                    beside(ffn_weights, 1)
                if o % 4 == 3:
                    wait(AC, t)
                    for i in range(4):
                        q = o - 3 + i
                        s = (2 + n) * HB + q
                        h_ok = ac.mark(AC.activation(dst[:, q, :], ps[:, b, i * P:(i + 1) * P], ACT.Gelu,
                                                     scale=scale[:, s:s + 1]))
                    read_by(b, h_ok)
        b = next_bank()
        wait(PE, h_ok, *w3_ok)
        t = matmuls(ps[:, b, 0:D], [(hT[0][:, k, :], w3T[:, k, :]) for k in range(HB)])
        y = sb("f_y", [D], stack=st)
        wait(DV, t, ld_s3)
        t = dv.mark(DV.tensor_tensor(y[:, :], ps[:, b, 0:D], s3[:, :], ALU.mult))
        read_by(b, t)
        add_to_x(y[:, :], [t])

    RING = 6
    W = D + 1
    ctx_one = [sb(f"ctx_one{i}", [CHUNK_TILES, W]) for i in range(RING)]
    wsim = sb("x1_wsim", [3, D])
    bsim = sb("x1_bsim", [1])
    shared_w1 = sb("m_shared_w1", [DK, HID])
    shared_w2 = sb("m_shared_w2", [HB, D])
    exp_w1 = [sb(f"m_w1_{i}", [DK, HID]) for i in range(E_UNROLL)]
    exp_w2 = [sb(f"m_w2_{i}", [HB, D]) for i in range(E_UNROLL)]
    E = N_EXPERTS
    rw = sb("m_router", [DK, E])
    eb_ = sb("m_bias", [E])
    b1 = sb("m_b1_rows", [P])
    sb1 = sb("m_sb1_rows", [P])
    b1T = sb("m_b1T", [E, HB])
    sb1T = sb("m_sb1T", [HB])
    b2 = sb("m_b2", [D])
    sb2 = sb("m_sb2", [D])
    a1_wT = [sb(f"a1_wT{n}", [DK, HID]) for n in range(3)]
    a1_woT = sb("a1_woT", [HB, D])
    a1_w = [exp_w2[2][:, :, :], exp_w2[3][:, :, :], exp_w1[3][:, :, :].rearrange("p k (b d) -> p (k b) d", d=D)]
    a1_wo = exp_w1[2]
    st = ExitStack()
    with st:
        wait(SP, *w3_ok)
        sem_ctx1 = [Link(sem(f"s1_ctx{i}"), PE, 16) for i in range(RING)]
        ctx1_free = Link(sem("s1_ctx_free"), SP)

        def load_ctx1(n, src, nt=CHUNK_TILES):
            sem_ctx1[n % RING].sent_by(SP.dma_start(ctx_one[n % RING][:, 0:nt, 0:D], src))

        load_ctx1(0, ctx_rows[0:TAIL_TILES * P, :].rearrange("(p t) d -> p t d", t=TAIL_TILES), TAIL_TILES)
        load_ctx1(1, full_chunks[0])
        ld_sim = load(wsim[:, :, :], a["L1_xattn_w_sim"].rearrange("(n d) -> n d", n=3).partition_broadcast(P))
        ld_bsim = load(bsim[:, :], a["L1_xattn_b_sim"].partition_broadcast(P))
        for n in range(2, RING):
            load_ctx1(n, full_chunks[n - 1])
        wait(GP, *w3_ok)
        for i in range(RING):
            ones_in = gp.mark(GP.memset(ctx_one[i][:, :, D:W], 1.0))
        join()
        wqv = sb("x1_wqv", [4 * DK, D], stack=st)
        bqv = sb("x1_bqv", [D], stack=st)
        ld_qv = [load(wqv[:, :, :], a["L1_xattn_W_qv"].rearrange("(b p) n -> p b n", p=P)),
                 load(bqv[:, :], a["L1_xattn_b_qv"].partition_broadcast(P))]
        w1_rows = a["L1_ffn_routed_w1"].rearrange("e (k p) n -> e p k n", p=P)
        w2_rows = a["L1_ffn_routed_w2"].rearrange("e (b p) n -> e p b n", p=P)
        sem_w = [Link(sem(f"s_expert{i}"), PE, 32) for i in range(E_UNROLL)]

        def load_expert(slot, e, eng=SP):
            eng.dma_start(exp_w1[slot][:, :, :], w1_rows[e]).then_inc(sem_w[slot].sem, 16)
            eng.dma_start(exp_w2[slot][:, :, :], w2_rows[e]).then_inc(sem_w[slot].sem, 16)


        enc_ok, encT_ok = layer_norm()
        g = sb("x1_g", [D], stack=st)
        scratch = sb("x1_scratch", [D], stack=st)
        const = sb("x1_const", [1], stack=st)
        wait(DV, enc_ok, ld_sim)
        t = dv.mark(DV.tensor_tensor(g[:, :], xn[:, :], wsim[:, 2, :], ALU.mult))
        wait(DV, t)
        g_ok = dv.mark(DV.tensor_tensor(g[:, :], g[:, :], wsim[:, 1, :], ALU.add))
        t = dv.mark(DV.tensor_tensor(scratch[:, :], xn[:, :], wsim[:, 0, :], ALU.mult))
        wait(DV, t)
        t = dv.mark(DV.tensor_reduce(const[:, :], scratch[:, :], AX.X, ALU.add))
        wait(DV, t, ld_bsim)
        const_ok = dv.mark(DV.tensor_tensor(const[:, :], const[:, :], bsim[:, :], ALU.add))
        gT_hi = sb("gT_hi", [DK, P], F32R, st)
        gT_lo = sb("gT_lo", [DK, P], F32R, st)
        b = next_bank()
        wait(PE, g_ok)
        for k in range(DK):
            t = PE.transpose(ps[:, b, k * P:(k + 1) * P], g[:, k * P:(k + 1) * P], ident[:, :])
        t = pe.mark(t)
        src = ps[:, b, 0:D].rearrange("p (k c) -> p k c", c=P)
        wait(AC, t)
        t = ac.mark(AC.copy(gT_hi[:, :, :], src))
        wait(DV, t)
        gT_ok = dv.mark(DV.tensor_tensor(gT_lo[:, :, :], src, gT_hi[:, :, :], ALU.subtract))

        ctxT_hi = [sb(f"c1T_hi{i}", [DK, CHUNK], F32R, st) for i in range(2)]
        ctxT_lo = [sb(f"c1T_lo{i}", [DK, CHUNK], F32R, st) for i in range(2)]
        pr = [sb(f"x1_pr{i}", [CHUNK], stack=st) for i in range(2)]
        prT = [sb(f"x1_prT{i}", [CHUNK], stack=st) for i in range(2)]
        negc = sb("x1_negc", [RING], stack=st)
        negm = sb("x1_negm", [RING], stack=st)
        alpha = sb("x1_alpha", [RING], stack=st)
        acc = sb("x1_acc", [W], stack=st)
        GP.memset(negm[:, :], 3e38)
        init = gp.mark(GP.memset(acc[:, :], 0.0))
        sc_ok = Link(sem("m_sc_ok"), DV)
        mx_ok = Link(sem("m_mx_ok"), AC)
        pr_ok = Link(sem("m_pr_ok"), PE)
        tr_full = Link(sem("m_tr_full"), AC)
        tr_kept = Link(sem("m_tr_kept"), PE)
        x_full = Link(sem("m_x_full"), AC)
        x_hi = Link(sem("m_x_hi"), DV)
        x_kept = Link(sem("m_x_kept"), PE)
        o_full = Link(sem("m_o_full"), DV)
        o_kept = Link(sem("m_o_kept"), PE)
        al_ok = Link(sem("m_al_ok"), DV)
        self_dv = Link(sem("m_self_dv"), DV)
        consumers = {PE: [pr_ok, tr_kept, x_kept, o_kept] + sem_ctx1, AC: [mx_ok, tr_full, x_full],
                     DV: [sc_ok, x_hi, o_full, al_ok, self_dv], SP: [ctx1_free]}
        tiles = lambda n: TAIL_TILES if n == 0 else CHUNK_TILES

        def turn_ctx(n, k):
            nt, c = tiles(n), ctx_one[n % RING]
            if k == 0:
                sem_ctx1[n % RING].wait()
            for i in range(nt):
                m = PE.transpose(ps[:, 5 + k, i * P:(i + 1) * P], c[:, i, k * P:(k + 1) * P], ident[:, :])
            x_full.sent_by(m)
            src = ps[:, 5 + k, 0:nt * P]
            x_full.wait()
            x_hi.sent_by(AC.copy(ctxT_hi[n % 2][:, k, 0:nt * P], src))
            x_hi.wait()
            x_kept.sent_by(DV.tensor_tensor(ctxT_lo[n % 2][:, k, 0:nt * P], src,
                                           ctxT_hi[n % 2][:, k, 0:nt * P], ALU.subtract))

        def score(n):
            nt = tiles(n)
            x_kept.wait()
            terms = [(q[:, k, :], c[n % 2][:, k, 0:nt * P]) for k in range(DK)
                     for q, c in ((gT_hi, ctxT_hi), (gT_hi, ctxT_lo), (gT_lo, ctxT_hi))]
            for i, (l, r) in enumerate(terms):
                m = PE.matmul(ps[:, n % 2, 0:nt * P], l, r, start=(i == 0), stop=(i == len(terms) - 1))
            sc_ok.sent_by(m)

        def maximum(n):
            nt, new, old = tiles(n), n % RING, (n - 1) % RING
            sc_ok.wait()
            self_dv.sent_by(DV.tensor_reduce(negc[:, new:new + 1], ps[:, n % 2, 0:nt * P], AX.X, ALU.max))
            self_dv.wait()
            mx_ok.sent_by(DV.scalar_tensor_tensor(out=negm[:, new:new + 1], in0=negc[:, new:new + 1], scalar=-1.0,
                                                 in1=negm[:, old:old + 1], op0=ALU.mult, op1=ALU.min))

        def probabilities(n):
            nt, new, old = tiles(n), n % RING, (n - 1) % RING
            mx_ok.wait()
            pr_ok.sent_by(AC.activation(pr[n % 2][:, 0:nt * P], ps[:, n % 2, 0:nt * P], ACT.Exp,
                                       bias=negm[:, new:new + 1], scale=1.0))
            al_ok.sent_by(AC.activation(alpha[:, new:new + 1], negm[:, old:old + 1], ACT.Exp,
                                       bias=negm[:, new:new + 1], scale=-1.0))

        def turn_pr(n, free=False):
            nt = tiles(n)
            pr_ok.wait()
            for i in range(nt):
                m = PE.transpose(ps[:, 2, i * P:(i + 1) * P], pr[n % 2][:, i * P:(i + 1) * P], ident[:, :])
                if i == 0 and free:
                    ctx1_free.sent_by(m)
            tr_full.sent_by(m)
            tr_full.wait()
            tr_kept.sent_by(AC.copy(prT[n % 2][:, 0:nt * P], ps[:, 2, 0:nt * P]))

        def sums(n, alone=False):
            nt, new = tiles(n), n % RING
            tr_kept.wait()
            if n > 1:
                o_kept.wait()
            for i in range(nt):
                m = PE.matmul(ps[:, 3 + n % 2, 0:W], prT[n % 2][:, i * P:(i + 1) * P], ctx_one[n % RING][:, i, :],
                              start=(i == 0), stop=(i == nt - 1))
            o_full.sent_by(m)
            al_ok.wait()
            if alone:
                DV.drain()
            o_full.wait()
            o_kept.sent_by(DV.scalar_tensor_tensor(out=acc[:, :], in0=acc[:, :], scalar=alpha[:, new:new + 1],
                                                  in1=ps[:, 3 + n % 2, 0:W], op0=ALU.mult, op1=ALU.add))

        def step(n, last=N_FULL, free=False):
            if n + 1 <= last:
                x_kept.wait()
            if n + 2 <= last:
                turn_ctx(n + 2, 0)
            if n + 1 <= last:
                score(n + 1)
            if n + 2 <= last:
                turn_ctx(n + 2, 1)
            if n + 1 <= last:
                maximum(n + 1)
                probabilities(n + 1)
            if n >= 1:
                sums(n - 1, alone=n == last)
            turn_pr(n, free)

        wait(PE, gT_ok, ones_in, init)
        wait(DV, init)
        wait(AC, init)
        for b in range(8):
            wait(PE, *readers[b])
        turn_ctx(0, 0)
        turn_ctx(0, 1)
        x_kept.wait()
        score(0)
        maximum(0)
        turn_ctx(1, 0)
        turn_ctx(1, 1)
        probabilities(0)
        step(0)
        step(1, free=True)
        ctx1_free.wait()
        load_ctx1(RING, full_chunks[RING - 1])
        settle(consumers)
        n_loop = (N_FULL - RING) // RING
        with nc.Fori(0, n_loop) as i:
            for u in range(RING):
                step(2 + u + RING, last=10 ** 6, free=True)
                ctx1_free.wait()
                load_ctx1(1 + u, full_chunks[RING + u + i * RING])
            settle(consumers)
        ld_a1 = [load(w, a["L1_attn_" + n].rearrange("n h m -> (n h) m").rearrange("(b p) m -> p b m", p=P))
                 for w, n in zip(a1_w, "QKV")]
        ld_a1.append(load(a1_wo[:, :, :], a["L1_attn_O"].rearrange("(k p) n -> p k n", p=P)))
        ld_small = [load(rw[:, :, :], a["L1_ffn_router_w"].rearrange("(k p) n -> p k n", p=P)),
                    load(eb_[:, :], a["L1_ffn_expert_bias"].partition_broadcast(P)),
                    load(b1[:, :], a["L1_ffn_routed_b1"].rearrange("e (b c) -> (e b) c", c=P)),
                    load(sb1[0:HB, :], a["L1_ffn_shared_b1"].rearrange("e (b c) -> (e b) c", c=P)),
                    load(b2[0:E, :], a["L1_ffn_routed_b2"]),
                    load(sb2[:, :], a["L1_ffn_shared_b2"].rearrange("e d -> (e d)").partition_broadcast(P))]
        ld_shared = [load(shared_w1[:, :, :], a["L1_ffn_shared_w1"].rearrange("s (k p) n -> p (s k) n", p=P)),
                     load(shared_w2[:, :, :], a["L1_ffn_shared_w2"].rearrange("s (b p) n -> p (s b) n", p=P))]
        for i in range(2):
            load_expert(i, i)
        for n in range(2 + n_loop * RING, N_FULL + 1):
            step(n)
        sums(N_FULL, alone=True)
        t = dv.mark(DV.drain())
        for b in range(8):
            readers[b] = [t]

        w_ok, woT_ok = [], []

        def turn_o():
            for i in range(0, HB, 2):
                woT_ok.extend(transposed(
                    lambda _, n: a1_woT[:, i:i + 2, :].rearrange("p b (k c) -> p (b k) c", c=P),
                    [a1_wo[:, k, b * P:(b + 1) * P] for b in (i, i + 1) for k in range(DK)], [ld_a1[3]], "act"))
                yield

        attn_weights = chain(*[weight_T(w_ok, t, w, HB, DK, l, "act") for t, w, l in zip(a1_wT, a1_w, ld_a1)],
                             turn_o())

        hat = sb("x1_hat", [D], stack=st)
        eh = sb("x1_eh", [D], stack=st)
        eb = sb("x1_eb", [D], stack=st)
        small = sb("x1_small", [8], stack=st)
        row = sb("x1_row", [P], stack=st)
        wait(DV, t)
        t = dv.mark(DV.reciprocal(small[:, 0:1], acc[:, D:W]))
        wait(DV, t)
        hat_ok = dv.mark(DV.tensor_scalar(hat[:, :], acc[:, 0:D], small[:, 0:1], None, ALU.mult))
        wait(DV, hat_ok)
        eh_ok = dv.mark(DV.tensor_tensor(eh[:, :], xn[:, :], hat[:, :], ALU.mult))
        fin = N_FULL % RING
        t = dv.mark(DV.tensor_tensor(small[:, 1:2], const[:, :], negm[:, fin:fin + 1], ALU.subtract))
        beside(attn_weights, GAPS_1[0])
        b = next_bank()
        wait(PE, t)
        t = pe.mark(PE.transpose(ps[0:1, b, 0:P], small[:, 1:2], ident[:, :]))
        wait(DV, t)
        t = dv.mark(DV.tensor_reduce(row[0:1, 0:1], ps[0:1, b, 0:P], AX.X, ALU.max))
        read_by(b, t)
        beside(attn_weights, GAPS_1[1])
        b = next_bank()
        wait(PE, t)
        t = matmuls(ps[:, b, 0:1], [(ones[0:1, :], row[0:1, 0:1])])
        wait(DV, t)
        t = dv.mark(DV.tensor_scalar(small[:, 2:3], ps[:, b, 0:1], -1.0, None, ALU.mult))
        read_by(b, t)
        wait(AC, t)
        t = ac.mark(AC.activation(small[:, 3:4], small[:, 1:2], ACT.Exp, bias=small[:, 2:3], scale=1.0))
        wait(DV, t)
        weights = sb("x1_weights", [P], stack=st)
        t = dv.mark(DV.tensor_scalar(weights[:, :], ones[:, :], small[:, 3:4], None, ALU.mult))
        beside(attn_weights, GAPS_1[2])
        b = next_bank()
        wait(PE, t)
        matmuls(ps[:, b, 0:D], [(weights[:, :], xn[:, :])])
        t = matmuls(ps[:, b, D:W], [(weights[:, :], ones[:, 0:1])])
        wait(DV, t)
        t = dv.mark(DV.reciprocal(small[:, 4:5], ps[:, b, D:W]))
        wait(DV, t)
        t = dv.mark(DV.scalar_tensor_tensor(out=eb[:, :], in0=ps[:, b, 0:D], scalar=small[:, 4:5],
                                            in1=xn[:, :], op0=ALU.mult, op1=ALU.mult))
        read_by(b, t)
        beside(attn_weights, GAPS_1[3])
        featT = sb("x1_featT", [3 * DK, P], stack=st)
        blocks = [f[:, k * P:(k + 1) * P] for f in (hat, eh, eb) for k in range(DK)]
        f_ok = transposed(lambda i, n: featT[:, i:i + n, :], blocks, [hat_ok, eh_ok, t])
        b = next_bank()
        wait(PE, *f_ok, *encT_ok, *ld_qv)
        t = matmuls(ps[:, b, 0:D], [(xnT[:, k, :], wqv[:, k, :]) for k in range(DK)]
                    + [(featT[:, k, :], wqv[:, DK + k, :]) for k in range(3 * DK)])
        last["xn_free"] = [t]
        y = sb("x1_y", [D], stack=st)
        wait(DV, t, ld_qv[1])
        t = dv.mark(DV.tensor_tensor(y[:, :], ps[:, b, 0:D], bqv[:, :], ALU.add))
        read_by(b, t)
        add_to_x(y[:, :], [t])

    beside(attn_weights, GAPS_1[4])
    join()
    st = ExitStack()
    with st:
        _, xnT_ok = layer_norm()
        beside(attn_weights)
        wait(SP, *w_ok, *woT_ok)
        for i in range(2, E_UNROLL):
            load_expert(i, i)
        wT, woT = a1_wT, a1_woT
        wait(PE, *xnT_ok, *w_ok)
        qT = sb("a1_qT", [HB, P], stack=st)
        kbd = sb("a1_kbd", [HB, 2, P], stack=st)
        v = sb("a1_v", [HID], stack=st)
        q_ok, v_ok = [], []
        for half in range(2):
            bq, bk = next_bank(), next_bank()
            for i in range(4):
                o = half * 4 + i
                cols = slice(o * P, (o + 1) * P)
                tq = matmuls(ps[:, bq, i * P:(i + 1) * P], [(wT[0][:, k, cols], xnT[:, k, :]) for k in range(DK)])
                tk = matmuls(ps[:, bk, i * P:(i + 1) * P], [(wT[1][:, k, cols], xnT[:, k, :]) for k in range(DK)])
            q_ok.append(copy_out(qT[:, half * 4:half * 4 + 4, :],
                                 ps[:, bq, :].rearrange("p (g c) -> p g c", c=P), [bq], [tq], eng="act"))
            wait(DV, tk)
            for j in range(2):
                t = dv.mark(DV.tensor_scalar(kbd[:, half * 4:half * 4 + 4, j, :],
                                             ps[:, bk, :].rearrange("p (g c) -> p g c", c=P),
                                             mask2[:, j:j + 1], None, ALU.mult))
            read_by(bk, t)
            q_ok.append(t)
        s0 = next_banks(4)
        after = []
        for o in range(HB):
            if o % 4 == 0:
                wait(PE, *q_ok[o // 2:o // 2 + 2])
            t = matmuls(ps[:, s0 + o // 2, o % 2 * 2 * P:(o % 2 + 1) * 2 * P], [(qT[:, o, :], kbd[:, o, :, :])])
            if o % 2:
                after.append(t)
        pT = sb("a1_pT", [A1_HEADS, P], stack=st)
        pT_ok = []
        zT = sb("a1_zT", [HB, P], stack=st)
        z_ok = []

        def outputs(half):
            b = next_bank()
            wait(PE, *v_ok)
            for o in range(4 * half, 4 * half + 4):
                wait(PE, pT_ok[o // 2])
                for j in range(2):
                    h = 2 * o + j
                    t = PE.matmul(ps[64 * j:64 * (j + 1), b, o % 4 * P:(o % 4 + 1) * P],
                                  v[:, h * A1_DH:(h + 1) * A1_DH], pT[:, h, :], start=True, stop=True,
                                  skip_group_check=True)
            z_ok.append(copy_out(zT[:, 4 * half:4 * half + 4, :],
                                 ps[:, b, :].rearrange("p (g c) -> p g c", c=P), [b], [pe.mark(t)]))

        for n, (e, e_ok) in enumerate(softmax_heads(st, s0, A1_HEADS, True, after)):
            if n == 0:
                for half in range(2):
                    b = next_bank()
                    cols = slice(half * BANK, (half + 1) * BANK)
                    t = matmuls(ps[:, b, :], [(xnT[:, k, :], wT[2][:, k, cols]) for k in range(DK)])
                    v_ok.append(copy_out(v[:, cols], ps[:, b, :], [b], [t], eng="act"))
                last["xn_free"] = [t]
            pT_ok += transposed(lambda i, m: pT[:, n * 4:(n + 1) * 4, :],
                                [e[:, n * 4 + j, :] for j in range(4)], [e_ok], "act")
            if n == 2:
                outputs(0)
        outputs(1)
        b = next_bank()
        wait(PE, *z_ok, *woT_ok)
        t = matmuls(ps[:, b, 0:D], [(zT[:, o, :], woT[:, o, :]) for o in range(HB)])
        add_to_x(ps[:, b, 0:D], [t], [b])

    b = next_bank()
    wait(PE, *ld_small)
    PE.transpose(ps[:, b, 0:P], b1[:, :], ident[:, :])
    t = pe.mark(PE.transpose(ps[:, b, P:P + HB], sb1[0:HB, :], ident[0:HB, 0:HB]))
    b1_ok = copy_out(b1T[:, :, :], ps[:, b, 0:P].rearrange("p (e b) -> p e b", b=HB), [b], [t], eng="act")
    sb1_ok = copy_out(sb1T[:, :], ps[:, b, P:P + HB], [b], [t], eng="act")
    join()
    st = ExitStack()
    with st:
        _, xnT_ok = layer_norm()
        acc = sb("m_acc", [D], stack=st)
        acc1 = sb("m_acc1", [D], stack=st)
        accs = [acc, acc1]
        wait(GP, last["x"], *ld_small)
        acc_ok = gp.mark(GP.tensor_tensor(acc[:, :], xbuf[state["x"]][:, :], sb2[:, :], ALU.add))
        busy.update(range(6))
        b = next_bank()
        wait(PE, *xnT_ok)
        t = matmuls(ps[:, b, 0:E], [(xnT[:, k, :], rw[:, k, :]) for k in range(DK)])
        n_t = [0]

        def tmp(n):
            n_t[0] += 1
            return sb(f"m_t{n_t[0]}", [n], stack=st)

        def then(inst):
            p = dv.mark(inst)
            wait(DV, p)
            return p

        lg = tmp(E)
        wait(DV, t, *ld_small)
        t = then(DV.tensor_tensor(lg[:, :], ps[:, b, 0:E], eb_[:, :], ALU.add))
        read_by(b, t)
        tops, hots = [], []
        for n in range(2):
            m, eq, cand, first_, hot = tmp(1), tmp(E), tmp(E), tmp(1), tmp(E)
            then(DV.tensor_reduce(m[:, :], lg[:, :], AX.X, ALU.max))
            then(DV.tensor_scalar(eq[:, :], lg[:, :], m[:, 0:1], None, ALU.is_equal))
            then(DV.scalar_tensor_tensor(out=cand[:, :], in0=eq[:, :], scalar=-99.0, in1=pos99[:, :],
                                          op0=ALU.mult, op1=ALU.add))
            then(DV.tensor_reduce(first_[:, :], cand[:, :], AX.X, ALU.min))
            then(DV.tensor_scalar(hot[:, :], pos[:, :], first_[:, 0:1], None, ALU.is_equal))
            tops.append(m)
            hots.append(hot)
            if n == 0:
                rest = tmp(E)
                then(DV.scalar_tensor_tensor(out=rest[:, :], in0=hot[:, :], scalar=-3e38, in1=lg[:, :],
                                              op0=ALU.mult, op1=ALU.add))
                lg = rest
        d, e2, s, r, w2_ = tmp(1), tmp(1), tmp(1), tmp(1), tmp(1)
        comb, comb1 = tmp(E), tmp(E)
        t = then(DV.tensor_tensor(d[:, :], tops[1][:, :], tops[0][:, :], ALU.subtract))
        wait(AC, t)
        t = ac.mark(AC.activation(e2[:, :], d[:, :], ACT.Exp))
        wait(DV, t)
        then(DV.tensor_scalar(s[:, :], e2[:, :], 1.0, None, ALU.add))
        then(DV.reciprocal(r[:, :], s[:, :]))
        then(DV.tensor_tensor(w2_[:, :], e2[:, :], r[:, :], ALU.mult))
        then(DV.tensor_scalar(comb1[:, :], hots[0][:, :], r[:, 0:1], None, ALU.mult))
        t = then(DV.scalar_tensor_tensor(out=comb[:, :], in0=hots[1][:, :], scalar=w2_[:, 0:1], in1=comb1[:, :],
                                          op0=ALU.mult, op1=ALU.add))
        comb_ok = t

        hid = [sb(f"m_hid{i}", [HB, P], stack=st) for i in range(2)]
        h_act = Link(sem("e_h_act"), AC)
        h_dve = Link(sem("e_h_dve"), DV)
        r_act = Link(sem("e_r_act"), PE)
        r_dve = Link(sem("e_r_dve"), PE)
        y_full = Link(sem("e_y_full"), DV)
        y_kept = Link(sem("e_y_kept"), PE)
        w_free = Link(sem("e_w_free"), SP)
        consumers = {PE: [r_act, r_dve, y_kept] + sem_w, AC: [h_act], DV: [h_dve, y_full], SP: [w_free]}

        def up(n, w1, bias, free=False):
            for half, link in enumerate((h_act, h_dve)):
                bank = ps[:, 2 * (n % 2) + half, :]
                for i in range(4):
                    o = half * 4 + i
                    for k in range(DK):
                        m = PE.matmul(bank[:, i * P:(i + 1) * P], w1[:, k, o * P:(o + 1) * P], xnT[:, k, :],
                                      start=(k == 0), stop=(k == DK - 1))
                        if free and o == 0 and k == 0:
                            w_free.sent_by(m)
                link.sent_by(m)
            h_act.wait()
            for i in range(4):
                t = AC.activation(hid[n % 2][:, i, :], ps[:, 2 * (n % 2), i * P:(i + 1) * P], ACT.Relu,
                                  bias=bias(i), scale=1.0)
            r_act.sent_by(t)
            h_dve.wait()
            for i in range(4):
                t = DV.tensor_scalar(hid[n % 2][:, 4 + i, :], ps[:, 2 * (n % 2) + 1, i * P:(i + 1) * P],
                                     bias(4 + i), 0.0, ALU.add, ALU.max)
            r_dve.sent_by(t)

        def down(n, w2, weight):
            r_act.wait()
            r_dve.wait()
            if n > 1:
                y_kept.wait()
            y = ps[:, 4 + n % 2, 0:D]
            for o in range(HB):
                m = PE.matmul(y, hid[n % 2][:, o, :], w2[:, o, :], start=(o == 0), stop=(o == HB - 1))
            y_full.sent_by(m)
            y_full.wait()
            s = accs[n % 2]
            if weight is None:
                t = DV.tensor_tensor(s[:, :], s[:, :], y, ALU.add)
            else:
                t = DV.scalar_tensor_tensor(out=s[:, :], in0=y, scalar=weight, in1=s[:, :],
                                            op0=ALU.mult, op1=ALU.add)
            y_kept.sent_by(t)

        def step(n, e, free):
            slot = n % E_UNROLL
            sem_w[slot].wait()
            up(n + 1, exp_w1[slot], lambda o: bias_rows(e + 1, o), free)
            down(n, exp_w2[(n - 1) % E_UNROLL], comb[:, column(e)])

        column = lambda e: slice(e, e + 1) if isinstance(e, int) else bass.ds(e, 1)
        b1T_flat = b1T[:, :, :].rearrange("p e b -> p (e b)")
        bias_rows = lambda e, o: b1T_flat[:, column(e * HB + o)]

        wait(PE, *ld_shared, *[r for b in range(6) for r in readers[b]])
        wait(DV, b1_ok, sb1_ok)
        wait(AC, b1_ok, sb1_ok)
        up(0, shared_w1, lambda o: sb1T[:, o:o + 1])
        sem_w[0].wait()
        up(1, exp_w1[0], lambda o: bias_rows(0, o))
        b = next_bank()
        wait(PE, comb_ok)
        t = pe.mark(PE.transpose(ps[0:E, b, 0:P], comb[:, :], ident[:, :]))
        combT = sb("m_combT", [P], stack=st)
        t = copy_out(combT[0:E, :], ps[0:E, b, 0:P], [b], [t], eng="dve")
        wait(DV, acc_ok)
        down(0, shared_w2, None)
        b = next_bank()
        wait(PE, t)
        t = matmuls(ps[:, b, 0:D], [(combT[0:E, :], b2[0:E, :])])
        wait(DV, copy_out(acc1[:, :], ps[:, b, 0:D], [b], [t], eng="dve"))
        step(1, 0, False)
        settle(consumers)
        n_loop = (E - E_UNROLL) // E_UNROLL
        with nc.Fori(0, n_loop) as i:
            for u in range(E_UNROLL):
                step(2 + u, i * E_UNROLL + (1 + u), True)
                w_free.wait()
                load_expert(u, i * E_UNROLL + (E_UNROLL + u))
            settle(consumers)
        for e in range(1 + n_loop * E_UNROLL, E - 1):
            step(e + 1, e, False)
        down(E, exp_w2[(E - 1) % E_UNROLL], comb[:, E - 1:E])
        DV.drain()
        last["x"] = dv.mark(DV.tensor_tensor(xbuf[1 - state["x"]][:, :], acc[:, :], acc1[:, :], ALU.add))
        state["x"] = 1 - state["x"]

    return finish()




INS = ["x", "ctx_1024", "L0_xattn_wq", "L0_xattn_wk", "L0_xattn_wv", "L0_attn_Wq", "L0_attn_Wk",
       "L0_attn_Wv", "L0_attn_Wo", "L0_ffn_w1_w", "L0_ffn_w1_s", "L0_ffn_w2_w", "L0_ffn_w2_s",
       "L0_ffn_h1_w", "L0_ffn_h1_s", "L0_ffn_h2_w", "L0_ffn_h2_s", "L0_ffn_w3_w", "L0_ffn_w3_s",
       "L1_xattn_w_sim", "L1_xattn_b_sim", "L1_xattn_W_qv", "L1_xattn_b_qv", "L1_attn_Q", "L1_attn_K",
       "L1_attn_V", "L1_attn_O", "L1_ffn_router_w", "L1_ffn_expert_bias", "L1_ffn_shared_w1",
       "L1_ffn_shared_b1", "L1_ffn_shared_w2", "L1_ffn_shared_b2", "L1_ffn_routed_w1",
       "L1_ffn_routed_b1", "L1_ffn_routed_w2", "L1_ffn_routed_b2"]


def kernel(**inputs):
    import concourse.bacc as bacc
    from concourse.bass_utils import run_bass_kernel_spmd

    nc = bacc.Bacc("TRN2", target_bir_lowering=False, num_devices=1)
    arrays, args = {}, {}
    for name in INS:
        v = np.ascontiguousarray(inputs[name])
        arrays[f"in_{name}"] = v
        args[name] = nc.dram_tensor(f"in_{name}", v.shape, mybir.dt.from_np(v.dtype), kind="ExternalInput").ap()
    out = nc.dram_tensor("out_0", (1, P, D), F32, kind="ExternalOutput").ap()
    build(nc, args, out)
    return run_bass_kernel_spmd(nc, [arrays], core_ids=[0]).results[0]["out_0"]
```
